# Optimizing a Trainium2 kernel written in Bass

```python
import numpy as np
import jax
import jax.numpy as jnp

def _softmax(x, axis=-1):
    return jax.nn.softmax(x, axis=axis)

def _gelu(x):
    return jax.nn.gelu(x, approximate=True)

def _silu(x):
    return jax.nn.silu(x)

def _sigmoid(x):
    return jax.nn.sigmoid(x)

def _layernorm(x, axis=-1, eps=1e-05):
    m = jnp.mean(x, axis=axis, keepdims=True)
    v = jnp.var(x, axis=axis, keepdims=True)
    return (x - m) / jnp.sqrt(v + eps)

def _scatter_add(tgt, idx, src, axis=0):
    return tgt.at[idx].add(src)

def _segment_sum(src, seg, n):
    return jax.ops.segment_sum(src, seg, n)
kernel_name = 'mk_perceiver_d1_seqx_r2_3056ba'

def setup_inputs(seed: int=0):
    np.random.seed(seed)
    _w = jnp.asarray

    def _rec_inputs():
        import jax
        import jax.numpy as jnp
        _rk = jax.random.key(seed)
        x = -0.0003929 + 0.9999 * jax.random.normal(jax.random.fold_in(_rk, 1), (8, 64, 512), jnp.float32)
        _lenS = 64 - jax.random.randint(jax.random.fold_in(_rk, 7), (8,), 0, max(1, 64 // 4) + 1, jnp.int32)
        _lenS2 = 1601 - jax.random.randint(jax.random.fold_in(_rk, 8), (8,), 0, max(1, 1601 // 4) + 1, jnp.int32)
        _ctx_768P = jax.random.normal(jax.random.fold_in(_rk, 11), (8, 16, 384), jnp.float32)
        _ctx_768c = jax.random.dirichlet(jax.random.fold_in(_rk, 511), 0.3 * jnp.ones((16,), jnp.float32), (8, 1601))
        _ctx_768t = jnp.einsum('bsk,bkd->bsd', _ctx_768c, _ctx_768P)
        _ctx_768t = _ctx_768t * jax.lax.rsqrt(jnp.mean(jnp.square(_ctx_768t)) + 1e-12) * 0.953939
        ctx_768 = 2.09791e-05 + 1.00001 * (_ctx_768t + 0.3 * jax.random.normal(jax.random.fold_in(_rk, 611), (8, 1601, 384), jnp.float32))
        return (x, ctx_768)
    x, ctx_768 = _rec_inputs()

    def _L0_xattn_setup():
        import jax, jax.numpy as jnp
        import numpy as np
        QUERY_DIM = 512
        KEY_DIM = 384
        NUM_HEADS = 16
        HEAD_DIM = QUERY_DIM // NUM_HEADS
        SCALE = HEAD_DIM ** (-0.5)
        key = jax.random.key(seed)
        ks = jax.random.split(key, 11)
        B, Nq, Nk = (4, 2048, 512)
        s_q = QUERY_DIM ** (-0.5)
        s_k = KEY_DIM ** (-0.5)
        return {'query': jax.random.normal(ks[0], (B, Nq, QUERY_DIM), jnp.float32), 'key': jax.random.normal(ks[1], (B, Nk, KEY_DIM), jnp.float32), 'value': jax.random.normal(ks[2], (B, Nk, KEY_DIM), jnp.float32), 'Wq': jax.random.normal(ks[3], (QUERY_DIM, QUERY_DIM), jnp.float32) * s_q, 'bq': jnp.zeros((QUERY_DIM,), jnp.float32), 'Wk': jax.random.normal(ks[4], (KEY_DIM, QUERY_DIM), jnp.float32) * s_k, 'bk': jnp.zeros((QUERY_DIM,), jnp.float32), 'Wv': jax.random.normal(ks[5], (KEY_DIM, QUERY_DIM), jnp.float32) * s_k, 'bv': jnp.zeros((QUERY_DIM,), jnp.float32), 'Wo': jax.random.normal(ks[6], (QUERY_DIM, QUERY_DIM), jnp.float32) * s_q, 'bo': jnp.zeros((QUERY_DIM,), jnp.float32)}
    _L0_xattn_all = _L0_xattn_setup()
    _L0_xattn_in = {k: v for k, v in _L0_xattn_all.items() if k in ('Wq', 'bq', 'Wk', 'bk', 'Wv', 'bv', 'Wo', 'bo')}
    del _L0_xattn_all

    def _L0_attn_setup():
        import jax, jax.numpy as jnp
        import numpy as np
        import math
        B, T, D = (4, 1024, 512)
        H = 16
        HD = D // H
        LAT = 128
        ROPE = 32
        EPS = 1e-06

        def rms_norm(x, g):
            rms = jnp.sqrt(jnp.mean(x * x, axis=-1, keepdims=True) + EPS)
            return g * (x / rms)
        key = jax.random.key(seed)
        ks = jax.random.split(key, 7)
        s = lambda fan_in: 1.0 / math.sqrt(fan_in)
        x = jax.random.normal(ks[0], (B, T, D), dtype=jnp.float32)
        Wq = jax.random.normal(ks[1], (D, D), dtype=jnp.float32) * s(D)
        Wkv = jax.random.normal(ks[2], (D, LAT), dtype=jnp.float32) * s(D)
        Wk = jax.random.normal(ks[3], (LAT, H * ROPE), dtype=jnp.float32) * s(LAT)
        Wv = jax.random.normal(ks[4], (LAT, H * (HD - ROPE)), dtype=jnp.float32) * s(LAT)
        Wo = jax.random.normal(ks[5], (D, D), dtype=jnp.float32) * s(D)
        q_g = jnp.ones((HD,), dtype=jnp.float32)
        k_g = jnp.ones((ROPE,), dtype=jnp.float32)
        return {'x': x, 'Wq': Wq, 'Wkv': Wkv, 'Wk': Wk, 'Wv': Wv, 'Wo': Wo, 'q_g': q_g, 'k_g': k_g}
    _L0_attn_all = _L0_attn_setup()
    _L0_attn_in = {k: v for k, v in _L0_attn_all.items() if k in ('Wq', 'Wkv', 'Wk', 'Wv', 'Wo', 'q_g', 'k_g')}
    del _L0_attn_all

    def _L0_ffn_setup():
        import jax, jax.numpy as jnp
        import numpy as np
        NEG_INF = -1e+30

        def _moe_forward(x, router_w, router_b, w1, b1, w2, b2, top_k=2):
            B, S, D = x.shape
            E = router_w.shape[1]
            logits = jnp.einsum('bsd,de->bse', x, router_w) + router_b
            top_vals, top_idx = jax.lax.top_k(logits, top_k)
            keep = jax.nn.one_hot(top_idx, E, dtype=logits.dtype).sum(-2) > 0
            sparse_logits = jnp.where(keep, logits, NEG_INF)
            gating = jax.nn.softmax(sparse_logits, axis=-1)
            xf = x.reshape(-1, D)
            gf = gating.reshape(-1, E)
            h = jax.nn.relu(jnp.einsum('td,edh->eth', xf, w1) + b1[:, None, :])
            y = jnp.einsum('eth,ehd->etd', h, w2) + b2[:, None, :]
            out = jnp.einsum('etd,te->td', y, gf)
            return out.reshape(B, S, D)
        key = jax.random.key(seed)
        ks = jax.random.split(key, 5)
        B, S, D, E, H = (2, 1024, 512, 8, 2048)
        scale = 0.02
        return {'x': jax.random.normal(ks[0], (B, S, D), dtype=jnp.float32), 'router_w': jax.random.normal(ks[1], (D, E), dtype=jnp.float32) * scale, 'router_b': jnp.zeros((E,), dtype=jnp.float32), 'w1': jax.random.normal(ks[2], (E, D, H), dtype=jnp.float32) * scale, 'b1': jnp.zeros((E, H), dtype=jnp.float32), 'w2': jax.random.normal(ks[3], (E, H, D), dtype=jnp.float32) * scale, 'b2': jnp.zeros((E, D), dtype=jnp.float32)}
    _L0_ffn_all = _L0_ffn_setup()
    _L0_ffn_in = {k: v for k, v in _L0_ffn_all.items() if k in ('router_w', 'router_b', 'w1', 'b1', 'w2', 'b2')}
    del _L0_ffn_all
    return {'x': x, 'ctx_768': ctx_768, 'L0_xattn_Wq': _L0_xattn_in['Wq'], 'L0_xattn_bq': _L0_xattn_in['bq'], 'L0_xattn_Wk': _L0_xattn_in['Wk'], 'L0_xattn_bk': _L0_xattn_in['bk'], 'L0_xattn_Wv': _L0_xattn_in['Wv'], 'L0_xattn_bv': _L0_xattn_in['bv'], 'L0_xattn_Wo': _L0_xattn_in['Wo'], 'L0_xattn_bo': _L0_xattn_in['bo'], 'L0_attn_Wq': _L0_attn_in['Wq'], 'L0_attn_Wkv': _L0_attn_in['Wkv'], 'L0_attn_Wk': _L0_attn_in['Wk'], 'L0_attn_Wv': _L0_attn_in['Wv'], 'L0_attn_Wo': _L0_attn_in['Wo'], 'L0_attn_q_g': _L0_attn_in['q_g'], 'L0_attn_k_g': _L0_attn_in['k_g'], 'L0_ffn_router_w': _L0_ffn_in['router_w'], 'L0_ffn_router_b': _L0_ffn_in['router_b'], 'L0_ffn_w1': _L0_ffn_in['w1'], 'L0_ffn_b1': _L0_ffn_in['b1'], 'L0_ffn_w2': _L0_ffn_in['w2'], 'L0_ffn_b2': _L0_ffn_in['b2']}

def reference(x, ctx_768, L0_xattn_Wq, L0_xattn_bq, L0_xattn_Wk, L0_xattn_bk, L0_xattn_Wv, L0_xattn_bv, L0_xattn_Wo, L0_xattn_bo, L0_attn_Wq, L0_attn_Wkv, L0_attn_Wk, L0_attn_Wv, L0_attn_Wo, L0_attn_q_g, L0_attn_k_g, L0_ffn_router_w, L0_ffn_router_b, L0_ffn_w1, L0_ffn_b1, L0_ffn_w2, L0_ffn_b2):
    import jax
    import jax.numpy as jnp

    def _L0_xattn_ref(query, key, value, Wq, bq, Wk, bk, Wv, bv, Wo, bo):
        import jax, jax.numpy as jnp
        import numpy as np
        QUERY_DIM = 512
        KEY_DIM = 384
        NUM_HEADS = 16
        HEAD_DIM = QUERY_DIM // NUM_HEADS
        SCALE = HEAD_DIM ** (-0.5)
        B, Nq, _ = query.shape
        Nk = key.shape[1]
        q = (query @ Wq + bq).reshape(B, Nq, NUM_HEADS, HEAD_DIM).transpose(0, 2, 1, 3)
        k = (key @ Wk + bk).reshape(B, Nk, NUM_HEADS, HEAD_DIM).transpose(0, 2, 1, 3)
        v = (value @ Wv + bv).reshape(B, Nk, NUM_HEADS, HEAD_DIM).transpose(0, 2, 1, 3)
        attn = jnp.einsum('bhqd,bhkd->bhqk', q, k) * SCALE
        attn = jax.nn.softmax(attn, axis=-1)
        out = jnp.einsum('bhqk,bhkd->bhqd', attn, v)
        out = out.transpose(0, 2, 1, 3).reshape(B, Nq, QUERY_DIM)
        return out @ Wo + bo

    def _L0_attn_ref(x, Wq, Wkv, Wk, Wv, Wo, q_g, k_g):
        import jax, jax.numpy as jnp
        import numpy as np
        import math
        B, T, D = (4, 1024, 512)
        H = 16
        HD = D // H
        LAT = 128
        ROPE = 32
        EPS = 1e-06

        def rms_norm(x, g):
            rms = jnp.sqrt(jnp.mean(x * x, axis=-1, keepdims=True) + EPS)
            return g * (x / rms)
        b, t, d = x.shape
        q = (x @ Wq).reshape(b, t, H, HD).transpose(0, 2, 1, 3)
        q = rms_norm(q, q_g)
        kv = x @ Wkv
        k = (kv @ Wk).reshape(b, t, H, ROPE).transpose(0, 2, 1, 3)
        k = rms_norm(k, k_g)
        v_c = (kv @ Wv).reshape(b, t, H, HD - ROPE).transpose(0, 2, 1, 3)
        scores = jnp.einsum('bhtr,bhsr->bhts', q[..., :ROPE], k) / math.sqrt(HD)
        causal = jnp.triu(jnp.ones((t, t), dtype=bool), k=1)
        scores = jnp.where(causal, -jnp.inf, scores)
        probs = jax.nn.softmax(scores, axis=-1)
        out_c = jnp.einsum('bhts,bhsd->bhtd', probs, v_c)
        out = jnp.pad(out_c, ((0, 0), (0, 0), (0, 0), (0, ROPE)))
        out = out.transpose(0, 2, 1, 3).reshape(b, t, d)
        return out @ Wo

    def _L0_ffn_ref(x, router_w, router_b, w1, b1, w2, b2):
        import jax, jax.numpy as jnp
        import numpy as np
        NEG_INF = -1e+30

        def _moe_forward(x, router_w, router_b, w1, b1, w2, b2, top_k=2):
            B, S, D = x.shape
            E = router_w.shape[1]
            logits = jnp.einsum('bsd,de->bse', x, router_w) + router_b
            top_vals, top_idx = jax.lax.top_k(logits, top_k)
            keep = jax.nn.one_hot(top_idx, E, dtype=logits.dtype).sum(-2) > 0
            sparse_logits = jnp.where(keep, logits, NEG_INF)
            gating = jax.nn.softmax(sparse_logits, axis=-1)
            xf = x.reshape(-1, D)
            gf = gating.reshape(-1, E)
            h = jax.nn.relu(jnp.einsum('td,edh->eth', xf, w1) + b1[:, None, :])
            y = jnp.einsum('eth,ehd->etd', h, w2) + b2[:, None, :]
            out = jnp.einsum('etd,te->td', y, gf)
            return out.reshape(B, S, D)
        return _moe_forward(x, router_w, router_b, w1, b1, w2, b2, top_k=2)
    x = x + _L0_xattn_ref(_layernorm(x, axis=-1), ctx_768, ctx_768, L0_xattn_Wq, L0_xattn_bq, L0_xattn_Wk, L0_xattn_bk, L0_xattn_Wv, L0_xattn_bv, L0_xattn_Wo, L0_xattn_bo)
    x = x + _L0_attn_ref(_layernorm(x, axis=-1), L0_attn_Wq, L0_attn_Wkv, L0_attn_Wk, L0_attn_Wv, L0_attn_Wo, L0_attn_q_g, L0_attn_k_g)
    x = x + _L0_ffn_ref(_layernorm(x, axis=-1), L0_ffn_router_w, L0_ffn_router_b, L0_ffn_w1, L0_ffn_b1, L0_ffn_w2, L0_ffn_b2)
    return x

_drawn_inputs = setup_inputs


def setup_inputs(seed=0):
    import zlib

    import numpy as np

    out = dict(_drawn_inputs(seed))
    spreads = {'L0_xattn_bq': (0.0, 0.1),
     'L0_xattn_bk': (0.0, 0.1),
     'L0_xattn_bv': (0.0, 0.1),
     'L0_xattn_bo': (0.0, 0.1),
     'L0_attn_q_g': (1.0, 0.2),
     'L0_attn_k_g': (1.0, 0.2),
     'L0_ffn_router_b': (0.0, 0.1),
     'L0_ffn_b1': (0.0, 0.1),
     'L0_ffn_b2': (0.0, 0.1)}
    factors = {}
    for name, (base, spread) in spreads.items():
        noise = np.random.default_rng([zlib.crc32(name.encode()), seed]).standard_normal(out[name].shape)
        drawn = base * np.exp(spread * noise) if base else spread * noise
        out[name] = jnp.asarray(drawn.astype(out[name].dtype))
    for name, factor in factors.items():
        out[name] = (out[name] * factor).astype(out[name].dtype)
    return out
```

```python
from contextlib import ExitStack

import concourse.bass as bass
from concourse import mybir

ALU = mybir.AluOpType
ACT = mybir.ActivationFunctionType
AX = mybir.AxisListType
F32 = mybir.dt.float32
F32R = mybir.dt.float32r
U32 = mybir.dt.uint32

P = 128
BANK = 512
LN_EPS = 1e-5


def bass_perceiver_layer_kernel(nc, x, ctx_t, wq, bq_t, wk, bk_t, wv, bv_t, wo, bo, router_w, router_b,
                                w1, b1_t, w2, b2, out):
    B, NQ, D = x.shape
    DC, NK = ctx_t.shape[1:]
    T = B * NQ
    TT = T // P
    KD = D // P
    KC = DC // P
    HEADS, HD = 16, D // 16
    HPG = P // HD
    GROUPS = HEADS // HPG
    STEPS = HEADS // 2
    SCALE = float(HD) ** -0.5
    E, _, HID = w1.shape
    KT = (NK + P - 1) // P
    KLAST = NK - (KT - 1) * P
    CHUNK_TILES = [3, 3, 3, 4]
    CHUNKS = len(CHUNK_TILES)
    TILE0 = [sum(CHUNK_TILES[:c]) for c in range(CHUNKS)]
    KEY0 = [P * t for t in TILE0]
    KEYS = [min(NK, KEY0[c] + P * CHUNK_TILES[c]) - KEY0[c] for c in range(CHUNKS)]
    KEYS_EVEN = [n + n % 2 for n in KEYS]
    NKE = NK + NK % 2
    assert sum(CHUNK_TILES) == KT and max(KEYS_EVEN) <= BANK and T == BANK and D == BANK
    FULL = CHUNKS - 1
    assert len(set(KEYS[:FULL])) == 1

    UNITS = [2 + n for n in CHUNK_TILES]
    UNIT0 = [sum(UNITS[:c]) for c in range(CHUNKS)]
    HALF_UNITS = sum(UNITS)
    BATCH_UNITS = 2 * HALF_UNITS
    PROJ_BANKS = 3
    assert HALF_UNITS % PROJ_BANKS == 0
    HG = HID // (4 * P)
    HT = HID // P

    q_dram = nc.dram_tensor("q_scratch", (D, T), F32, kind="Internal").ap()
    o_dram = nc.dram_tensor("o_scratch", (D, T), F32, kind="Internal").ap()

    x_rows = x.rearrange("b q d -> (b q) d").rearrange("(t p) d -> p t d", p=P)
    out_rows = out.rearrange("b q d -> (b q) d").rearrange("(t p) d -> p t d", p=P)
    ctx_view = ctx_t.rearrange("b (c p) n -> b p c n", p=P)

    with ExitStack() as stack:
        def sb(name, shape, dt, where=stack):
            return where.enter_context(nc.sbuf_tensor(name, shape, dt))

        def sem(name):
            return stack.enter_context(nc.semaphore(name))

        ps = stack.enter_context(nc.psum_tensor("ps", [P, 8, BANK], F32))
        SCORE_BANK, PROJ_BANK, PV_BANK = 0, 4, 7

        ident = sb("ident", [P, P], F32)
        bq_sb = sb("bq_sb", [P, KD], F32)
        bk_sb = sb("bk_sb", [P, KD], F32)
        bv_sb = sb("bv_sb", [P, KD], F32)
        stat = sb("stat", [P, TT, 6], F32)
        mv = sb("mv", [P, TT, 2], F32)
        ve = sb("ve", [P, TT], F32)
        sd = sb("sd", [P, TT], F32)
        rs0 = sb("rs0", [P, TT], F32)
        sq = sb("sq", [P, TT], F32)
        sdn = sb("sdn", [P, TT], F32)
        rstd = sb("rstd", [P, TT], F32)

        attn = ExitStack()
        v_hi = sb("v_hi", [P, KT, D], F32R, attn)
        v_lo = sb("v_lo", [P, KT, D], F32R, attn)
        pt_hi = sb("pt_hi", [P, KT, 2, P], F32R, attn)
        pt_lo = sb("pt_lo", [P, KT, 2, P], F32R, attn)
        k_hi = sb("k_hi", [P, GROUPS, NKE], F32R, attn)
        k_lo = sb("k_lo", [P, GROUPS, NKE], F32R, attn)
        ctx_raw = [sb(f"ctx_raw{i}", [P, KC, max(KEYS_EVEN)], F32, attn) for i in range(2)]
        ctx_hi = [sb(f"ctx_hi{i}", [P, KC, max(KEYS_EVEN)], F32R, attn) for i in range(2)]
        ctx_lo = [sb(f"ctx_lo{i}", [P, KC, max(KEYS_EVEN)], F32R, attn) for i in range(2)]
        wk_hi = sb("wk_hi", [P, KC, D], F32R, attn)
        wk_lo = sb("wk_lo", [P, KC, D], F32R, attn)
        wv_hi = sb("wv_hi", [P, KC, D], F32R, attn)
        wv_lo = sb("wv_lo", [P, KC, D], F32R, attn)
        probs = sb("probs", [P, NK], F32, attn)
        qbd_hi = sb("qbd_hi", [P, GROUPS, HPG * NQ], F32R, attn)
        qbd_lo = sb("qbd_lo", [P, GROUPS, HPG * NQ], F32R, attn)
        no_query = sb("no_query", [P, NQ], F32, attn)
        q_stage = sb("q_stage", [P, GROUPS, NQ], F32, attn)
        o_stage = [sb(f"o_stage{i}", [P, NQ], F32, attn) for i in range(2)]
        mx = sb("mx", [P, 2], F32, attn)
        negmax = sb("negmax", [P, 1], F32, attn)
        rowsum = sb("rowsum", [P, 2], F32, attn)
        total = sb("total", [P, 1], F32, attn)
        rinv = sb("rinv", [P, 1], F32, attn)
        attn.close()

        first = ExitStack()
        wq_raw = sb("wq_raw", [P, KD, D], F32, first)
        wq_hi = sb("wq_hi", [P, KD, D], F32R, first)
        wq_lo = sb("wq_lo", [P, KD, D], F32R, first)
        wkv_raw = sb("wkv_raw", [P, 2, KC, D], F32, first)
        sb("rest_of_v", [P, 2 * KT * D - 3 * KD * D - 2 * KC * D], F32, first)
        x0 = sb("x0", [P, TT, D], F32, first)
        xn0 = sb("xn0", [P, TT, D], F32, first)
        q_out = sb("q_out", [P, KD, T], F32, first)
        sb("rest_of_pt", [P, 4 * KT * P - 3 * TT * D], F32, first)
        xt0_hi = sb("xt0_hi", [P, KD, T], F32R, first)
        xt0_lo = sb("xt0_lo", [P, KD, T], F32R, first)
        first.close()

        moe = ExitStack()
        w_raw = [sb(f"w_raw{i}", [P, 2, 4, BANK], F32, moe) for i in range(2)]
        w_hi = [sb(f"w_hi{i}", [P, 2, 4, BANK], F32R, moe) for i in range(2)]
        w_lo = [sb(f"w_lo{i}", [P, 2, 4, BANK], F32R, moe) for i in range(2)]
        h_f32 = [sb(f"h_f32_{i}", [P, T], F32, moe) for i in range(2)]
        h_hi = [sb(f"h_hi{i}", [P, T], F32R, moe) for i in range(2)]
        h_lo = [sb(f"h_lo{i}", [P, T], F32R, moe) for i in range(2)]
        wo_raw = sb("wo_raw", [P, KD, D], F32, moe)
        wo_hi = sb("wo_hi", [P, KD, D], F32R, moe)
        wo_lo = sb("wo_lo", [P, KD, D], F32R, moe)
        ot_raw = sb("ot_raw", [P, KD, T], F32, moe)
        ot_hi = sb("ot_hi", [P, KD, T], F32R, moe)
        ot_lo = sb("ot_lo", [P, KD, T], F32R, moe)
        bo_bc = sb("bo_bc", [P, D], F32, moe)
        acc = sb("acc", [P, TT, D], F32, moe)
        xn = sb("xn", [P, TT, D], F32, moe)
        xt_hi = sb("xt_hi", [P, KD, T], F32R, moe)
        xt_lo = sb("xt_lo", [P, KD, T], F32R, moe)
        rw_raw = sb("rw_raw", [P, KD, E], F32, moe)
        rw_hi = sb("rw_hi", [P, KD, E], F32R, moe)
        rw_lo = sb("rw_lo", [P, KD, E], F32R, moe)
        rb_bc = sb("rb_bc", [P, E], F32, moe)
        b2_sb = sb("b2_sb", [E, D], F32, moe)
        logits = sb("logits", [P, TT, E], F32, moe)
        top = sb("top", [P, TT, 8], F32, moe)
        top_at = sb("top_at", [P, TT, 8], U32, moe)
        top_atf = sb("top_atf", [P, TT, 8], F32, moe)
        expert_no = sb("expert_no", [P, E], F32, moe)
        negtop = sb("negtop", [P, TT], F32, moe)
        is_first = sb("is_first", [P, TT, E], F32, moe)
        keep = sb("keep", [P, TT, E], F32, moe)
        eg = sb("eg", [P, TT, E], F32, moe)
        egk = sb("egk", [P, TT, E], F32, moe)
        gsum = sb("gsum", [P, TT], F32, moe)
        ginv = sb("ginv", [P, TT], F32, moe)
        gates = sb("gates", [P, TT, E], F32, moe)
        gates_e = sb("gates_e", [P, E, TT], F32, moe)
        gates_t = sb("gates_t", [E, T], F32, moe)
        b1_sb = sb("b1_sb", [P, E, HT], F32, moe)
        b1_cur = sb("b1_cur", [P, 1, HT], F32, moe)
        gate_cur = sb("gate_cur", [P, 1, TT], F32, moe)
        moe.close()

        x_loaded, wq_loaded, bias_loaded, wkv_loaded = sem("x_loaded"), sem("wq_loaded"), sem("bias_loaded"), sem("wkv_loaded")
        ctx_loaded = [sem(f"ctx_loaded{i}") for i in range(2)]
        q_loaded, ot_loaded, wo_loaded = sem("q_loaded"), sem("ot_loaded"), sem("wo_loaded")
        x1_loaded, bo_loaded, small_loaded = sem("x1_loaded"), sem("bo_loaded"), sem("small_loaded")
        w_loaded = [sem(f"w_loaded{i}") for i in range(2)]
        out_stored = sem("out_stored")
        stored = [sem(f"stored{i}") for i in range(2)]
        zeroed, ident_ready, psum_zeroed = sem("zeroed"), sem("ident_ready"), sem("psum_zeroed")
        wq_high, wq_split, wkv_high, wkv_split = sem("wq_high"), sem("wq_split"), sem("wkv_high"), sem("wkv_split")
        q_ready, q_done = sem("q_ready"), sem("q_done")
        var_ready, sd_ready, xn_ready = sem("var_ready"), sem("sd_ready"), sem("xn_ready")
        xt_ready, xt_high, xt_split = sem("xt_ready"), sem("xt_high"), sem("xt_split")
        vector_step = sem("vector_step")
        qbd_high, qbd_ready = sem("qbd_high"), sem("qbd_ready")
        ctx_high, ctx_split = sem("ctx_high"), sem("ctx_split")
        proj_ready, proj_high, proj_split = sem("proj_ready"), sem("proj_high"), sem("proj_split")
        scores_ready, part_max, negmax_ready = sem("scores_ready"), sem("part_max"), sem("negmax_ready")
        exp_done, total_ready, rinv_ready, norm_ready = sem("exp_done"), sem("total_ready"), sem("rinv_ready"), sem("norm_ready")
        pt_ready, pt_high, pt_split = sem("pt_ready"), sem("pt_high"), sem("pt_split")
        pv_ready, pv_taken = sem("pv_ready"), sem("pv_taken")
        wo_high, wo_split, ot_high, ot_split = sem("wo_high"), sem("wo_split"), sem("ot_high"), sem("ot_split")
        x_bo_ready, x1_product = sem("x_bo_ready"), sem("x1_product")
        rw_high, rw_split, numbers_ready = sem("rw_high"), sem("rw_split"), sem("numbers_ready")
        logits_product, negtop_ready, eg_ready = sem("logits_product"), sem("negtop_ready"), sem("eg_ready")
        gates_ready, gates_turned, gates_t_ready = sem("gates_ready"), sem("gates_turned"), sem("gates_t_ready")
        b2_product = sem("b2_product")
        w_high, w_split, w_used = sem("w_high"), sem("w_split"), sem("w_used")
        b1_set, gate_set = sem("b1_set"), sem("gate_set")
        h_ready, h_high, h_split = sem("h_ready"), sem("h_high"), sem("h_split")
        y_ready, y_taken = sem("y_ready"), sem("y_taken")

        def job_no(b, s):
            return CHUNKS + STEPS * b + s

        def unit_no(b, s, k):
            return HALF_UNITS + BATCH_UNITS * b + HALF_UNITS * (s // CHUNKS) + UNIT0[s % CHUNKS] + k

        def key_units_done(b, g):
            return BATCH_UNITS * b + HALF_UNITS * (g // 2) + UNIT0[CHUNKS - 1] + g % 2 + 1

        def value_units_done(b, g):
            return BATCH_UNITS * b + HALF_UNITS * (g // 2 + 1)

        def units_of(s):
            half, c = (1 - s // CHUNKS) if s >= 0 else 0, s % CHUNKS
            return [("keys", 2 * half + i, c) for i in range(2)] + \
                   [("values", TILE0[c] + i, half) for i in range(CHUNK_TILES[c])]

        def rows_of(t):
            return P if t < KT - 1 else KLAST

        def three_pass(pe, acc_ap, a_hi, a_lo, b_hi, b_lo, start, stop):
            pe.matmul(acc_ap, a_hi, b_hi, start=start, stop=False)
            pe.matmul(acc_ap, a_hi, b_lo, start=False, stop=False)
            return pe.matmul(acc_ap, a_lo, b_hi, start=False, stop=stop)

        block = stack.enter_context(nc.Block())

        @block.sync
        def _(sp):
            def load_ctx(b, c, slot):
                n = KEYS[c]
                sp.dma_start(ctx_raw[slot][:, :, 0:n],
                             ctx_view[b, :, :, KEY0[c]:KEY0[c] + n] if isinstance(b, int) else
                             ctx_view[bass.ds(b, 1), :, :, KEY0[c]:KEY0[c] + n].rearrange("o p c n -> (o p) c n")
                             ).then_inc(ctx_loaded[slot], 16)

            def load_queries(b):
                sp.dma_start(q_stage[:], q_dram.rearrange("(g p) t -> p g t", p=P)[:, :, bass.ds(b * NQ, NQ)]
                             ).then_inc(q_loaded, 16)

            def store_context(b, g):
                slot = g % 2
                sp.dma_start(o_dram[g * P:(g + 1) * P, bass.ds(b * NQ, NQ)], o_stage[slot][:]).then_inc(stored[slot], 16)

            sp.dma_start(x0[:], x_rows).then_inc(x_loaded, 16)
            sp.dma_start(wq_raw[:], wq.rearrange("(k p) n -> p k n", p=P)).then_inc(wq_loaded, 16)
            sp.dma_start(bq_sb[:], bq_t).then_inc(bias_loaded, 16)
            sp.dma_start(bk_sb[:], bk_t).then_inc(bias_loaded, 16)
            sp.dma_start(bv_sb[:], bv_t).then_inc(bias_loaded, 16)
            sp.dma_start(wkv_raw[:, 0], wk.rearrange("(k p) n -> p k n", p=P)).then_inc(wkv_loaded, 16)
            sp.dma_start(wkv_raw[:, 1], wv.rearrange("(k p) n -> p k n", p=P)).then_inc(wkv_loaded, 16)
            load_ctx(0, 0, 0)
            load_ctx(0, 1, 1)
            for m in range(2, CHUNKS):
                sp.wait_ge(ctx_split, m - 1)
                load_ctx(0, m, m % 2)
            sp.wait_ge(q_done, KD - 1)
            sp.wait_ge(pv_taken, 1)
            for i in range(2):
                half = slice(i * KD // 2, (i + 1) * KD // 2)
                sp.dma_start(q_dram.rearrange("(g p) t -> p g t", p=P)[:, half], q_out[:, half]).then_inc(stored[i], 16)
            for c in range(2):
                sp.wait_ge(ctx_split, CHUNKS - 1 + c)
                load_ctx(0, c, c % 2)
            for i in range(2):
                sp.wait_ge(stored[i], 16)
            load_queries(0)

            def batch(b, last):
                for s in range(STEPS):
                    if s == 0 and not last:
                        sp.wait_ge(qbd_ready, GROUPS * (b + 1))
                        load_queries(b + 1)
                    if s % 2 == 0 and s >= 2:
                        sp.wait_ge(pv_taken, GROUPS * b + s // 2 + 1)
                        store_context(b, s // 2 - 1)
                    if not (last and s + 2 >= CHUNKS):
                        sp.wait_ge(ctx_split, job_no(b, s) + 1)
                        nb = b if s + 2 < CHUNKS or s + 2 >= STEPS else b + 1
                        if s + 2 >= STEPS:
                            nb = b + 1
                        load_ctx(nb, (s + 2) % CHUNKS, s % 2)
                    if s == STEPS - 1:
                        sp.wait_ge(pv_taken, GROUPS * (b + 1) + 1)
                        store_context(b, GROUPS - 1)

            with sp.Fori(0, B - 1) as b:
                batch(b, False)
            batch(B - 1, True)

            for i in range(2):
                sp.wait_ge(stored[i], 16 * (2 * B + 1))
            sp.dma_start(ot_raw[:], o_dram.rearrange("(k p) t -> p k t", p=P)).then_inc(ot_loaded, 16)
            sp.dma_start(wo_raw[:], wo.rearrange("(k p) n -> p k n", p=P)).then_inc(wo_loaded, 16)
            sp.dma_start(acc[:], x_rows).then_inc(x1_loaded, 16)
            sp.dma_start(bo_bc[:], bo.rearrange("(o n) -> o n", o=1).broadcast_to([P, D])).then_inc(bo_loaded, 16)
            sp.dma_start(rw_raw[:], router_w.rearrange("(k p) e -> p k e", p=P)).then_inc(small_loaded, 16)
            sp.dma_start(rb_bc[:], router_b.rearrange("(o n) -> o n", o=1).broadcast_to([P, E])).then_inc(small_loaded, 16)
            sp.dma_start(b2_sb[:], b2).then_inc(small_loaded, 16)
            sp.dma_start(b1_sb[:], b1_t).then_inc(small_loaded, 16)

            def load_weights(e, g, slot):
                cols = slice(g * BANK, (g + 1) * BANK)
                w1_src = w1.rearrange("e (k p) h -> e p k h", p=P)
                w2_src = w2.rearrange("e (g j p) d -> e g p j d", p=P, j=4)
                if isinstance(e, int):
                    w1_src, w2_src = w1_src[e, :, :, cols], w2_src[e, g]
                else:
                    w1_src = w1_src[bass.ds(e, 1), :, :, cols].rearrange("o p k h -> (o p) k h")
                    w2_src = w2_src[bass.ds(e, 1), g].rearrange("o p j d -> (o p) j d")
                sp.dma_start(w_raw[slot][:, 0], w1_src).then_inc(w_loaded[slot], 16)
                sp.dma_start(w_raw[slot][:, 1], w2_src).then_inc(w_loaded[slot], 16)

            load_weights(0, 0, 0)
            load_weights(0, 1, 1)

            def expert(e, last):
                for g in range(HG):
                    if last and g + 2 >= HG:
                        break
                    sp.wait_ge(w_split, 4 * (HG * e + g + 1))
                    load_weights(e if g + 2 < HG else e + 1, (g + 2) % HG, g % 2)

            with sp.Fori(0, E - 1) as e:
                expert(e, False)
            expert(E - 1, True)

            for t in range(TT):
                sp.wait_ge(y_taken, TT * E + t + 1)
                sp.dma_start(out_rows[:, t], acc[:, t]).then_inc(out_stored, 16)
            sp.wait_ge(out_stored, 16 * TT)

        @block.gpsimd
        def _(pool):
            nc.gpsimd.memset(ident[:], 0.0).then_inc(zeroed, 1)
            nc.gpsimd.memset(qbd_hi[:].bitcast(F32), 0.0).then_inc(zeroed, 1)
            nc.gpsimd.memset(qbd_lo[:].bitcast(F32), 0.0).then_inc(zeroed, 1)
            nc.gpsimd.memset(no_query[:], 0.0).then_inc(zeroed, 1)
            nc.gpsimd.memset(ctx_raw[(CHUNKS - 1) % 2][:, :, KEYS[-1]:KEYS_EVEN[-1]], 0.0).then_inc(zeroed, 1)
            pool.wait_ge(zeroed, 5)
            nc.gpsimd.affine_select(out=ident[:], in_=ident[:], compare_op=ALU.not_equal, fill=1.0, base=0,
                                    pattern=[[-1, P]], channel_multiplier=1).then_inc(ident_ready, 1)
            pool.wait_ge(wkv_loaded, 32)
            nc.gpsimd.tensor_copy(wk_hi[:], wkv_raw[:, 0]).then_inc(wkv_high, 1)
            nc.gpsimd.tensor_copy(wv_hi[:], wkv_raw[:, 1]).then_inc(wkv_high, 1)
            pool.wait_ge(wkv_high, 2)
            nc.gpsimd.tensor_tensor(wk_lo[:], wkv_raw[:, 0], wk_hi[:].bitcast(F32), ALU.subtract).then_inc(wkv_split, 1)
            nc.gpsimd.tensor_tensor(wv_lo[:], wkv_raw[:, 1], wv_hi[:].bitcast(F32), ALU.subtract).then_inc(wkv_split, 1)

            def split_ctx_low(job_plus_1, c):
                slot, n = c % 2, KEYS_EVEN[c]
                pool.wait_ge(ctx_high, job_plus_1)
                nc.gpsimd.tensor_tensor(ctx_lo[slot][:, :, 0:n], ctx_raw[slot][:, :, 0:n],
                                        ctx_hi[slot][:, :, 0:n].bitcast(F32), ALU.subtract).then_inc(ctx_split, 1)

            def place_queries(b, g):
                for half in range(2):
                    for h in range(HPG):
                        rows, cols = slice(HD * h, HD * (h + 1)), slice(NQ * h, NQ * (h + 1))
                        if half == 0:
                            last = nc.gpsimd.tensor_tensor(qbd_hi[rows, g, cols], q_stage[rows, g, :], no_query[rows, :],
                                                           ALU.add)
                        else:
                            last = nc.gpsimd.tensor_tensor(qbd_lo[rows, g, cols], q_stage[rows, g, :],
                                                           qbd_hi[rows, g, cols].bitcast(F32), ALU.subtract)
                    if half == 0:
                        last.then_inc(qbd_high, 1)
                        pool.wait_ge(qbd_high, GROUPS * b + g + 1)
                    else:
                        last.then_inc(qbd_ready, 1)
                        pool.wait_ge(qbd_ready, GROUPS * b + g + 1)

            for m in range(CHUNKS):
                split_ctx_low(m + 1, m)
            pool.wait_ge(q_loaded, 16)
            pool.wait_ge(ctx_split, CHUNKS)
            for g in range(GROUPS):
                place_queries(0, g)
            split_ctx_low(CHUNKS + 1, 0)

            def batch(b, last):
                for s in range(STEPS):
                    if not (last and s + 1 >= CHUNKS):
                        split_ctx_low(job_no(b, s + 1) + 1, (s + 1) % CHUNKS)
                    if s % 2 == 1 and not last:
                        pool.wait_ge(scores_ready, 2 * (STEPS * b + s + 1))
                        pool.wait_ge(ctx_split, job_no(b, s + 1) + 1)
                        if s == 1:
                            pool.wait_ge(q_loaded, 16 * (b + 2))
                        place_queries(b + 1, s // 2)

            with pool.Fori(0, B - 1) as b:
                batch(b, False)
            batch(B - 1, True)

            pool.wait_ge(small_loaded, 64)
            nc.gpsimd.iota(expert_no[:], pattern=[[1, E]], base=0, channel_multiplier=0,
                           allow_small_or_imprecise_dtypes=True).then_inc(numbers_ready, 1)
            nc.gpsimd.tensor_copy(rw_hi[:], rw_raw[:]).then_inc(rw_high, 1)
            pool.wait_ge(rw_high, 1)
            nc.gpsimd.tensor_tensor(rw_lo[:], rw_raw[:], rw_hi[:].bitcast(F32), ALU.subtract).then_inc(rw_split, 1)
            pool.wait_ge(wo_high, 1)
            nc.gpsimd.tensor_tensor(wo_lo[:], wo_raw[:], wo_hi[:].bitcast(F32), ALU.subtract).then_inc(wo_split, 1)

            def split_low(n_plus_1, slot):
                for i in range(4):
                    pool.wait_ge(w_high, 4 * n_plus_1 - 3 + i)
                    nc.gpsimd.tensor_tensor(w_lo[slot][:, :, i, :], w_raw[slot][:, :, i, :],
                                            w_hi[slot][:, :, i, :].bitcast(F32), ALU.subtract).then_inc(w_split, 1)

            split_low(1, 0)

            def expert(e, last):
                for g in range(HG):
                    if not (last and g == HG - 1):
                        split_low(HG * e + g + 2, (g + 1) % 2)

            with pool.Fori(0, E - 1) as e:
                expert(e, False)
            expert(E - 1, True)

        @block.scalar
        def _(act):
            act.wait_ge(wq_loaded, 16)
            nc.scalar.copy(wq_hi[:], wq_raw[:]).then_inc(wq_high, 1)
            act.wait_ge(var_ready, 1)
            nc.scalar.activation(sd[:], ve[:], ACT.Sqrt).then_inc(sd_ready, 1)
            for k in range(KD):
                act.wait_ge(xt_ready, k + 1)
                nc.scalar.copy(xt0_hi[:, k, :], ps[:, k, :]).then_inc(xt_high, 1)

            def proj_high_part(unit, n, bank):
                kind, a, c = unit
                act.wait_ge(proj_ready, n + 1)
                if kind == "keys":
                    m = KEYS_EVEN[c]
                    nc.scalar.activation(k_hi[:, a, KEY0[c]:KEY0[c] + m], ps[:, bank, 0:m], ACT.Identity,
                                         bias=bk_sb[:, a:a + 1]).then_inc(proj_high, 1)
                else:
                    r, w = rows_of(a), D // 2
                    nc.scalar.copy(v_hi[0:r, a, c * w:(c + 1) * w], ps[0:r, bank, 0:w]).then_inc(proj_high, 1)

            def job_high(b, s, ks):
                for k in ks:
                    n = UNIT0[s % CHUNKS] + k
                    bank = PROJ_BANK + (n % PROJ_BANKS)
                    proj_high_part(units_of(s if b is not None else CHUNKS + s)[k],
                                   unit_no(b, s, k) if b is not None else n, bank)

            act.wait_ge(bias_loaded, 48)
            for c in range(CHUNKS):
                job_high(None, c, range(UNITS[c]))

            def batch(b, last):
                for s in range(STEPS):
                    act.wait_ge(negmax_ready, STEPS * b + s + 1)
                    w = KEY0[FULL]
                    nc.scalar.activation(probs[:, 0:w].rearrange("p (c k) -> p c k", c=FULL),
                                         ps[:, SCORE_BANK:SCORE_BANK + FULL, 0:KEYS[0]], ACT.Exp,
                                         bias=negmax[:, 0:1], accum_out=rowsum[:, 0:1])
                    nc.scalar.activation(probs[:, w:NK], ps[:, SCORE_BANK + FULL, 0:KEYS[FULL]], ACT.Exp,
                                         bias=negmax[:, 0:1], accum_out=rowsum[:, 1:2]).then_inc(exp_done, 1)
                    has_job = not (last and s >= CHUNKS)
                    u = UNITS[s % CHUNKS]
                    if has_job:
                        job_high(b, s, range(u - 1))
                    for c in range(CHUNKS):
                        act.wait_ge(pt_ready, CHUNKS * (STEPS * b + s) + c + 1)
                        n = CHUNK_TILES[c]
                        nc.scalar.copy(pt_hi[:, TILE0[c]:TILE0[c] + n, s % 2, :],
                                       ps[:, SCORE_BANK + c, 0:n * P].rearrange("p (t r) -> p t r", t=n)
                                       ).then_inc(pt_high, 1)
                    if has_job:
                        job_high(b, s, [u - 1])

            with act.Fori(0, B - 1) as b:
                batch(b, False)
            batch(B - 1, True)

            act.wait_ge(ot_loaded, 16)
            nc.scalar.copy(ot_hi[:], ot_raw[:]).then_inc(ot_high, 1)
            act.wait_ge(wo_loaded, 16)
            nc.scalar.copy(wo_hi[:], wo_raw[:]).then_inc(wo_high, 1)

            def split_high(slot, i, loaded, used=None, products=None):
                act.wait_ge(w_loaded[slot], loaded)
                if used is not None:
                    act.wait_ge(w_used, used)
                if products is not None:
                    act.wait_ge(y_taken, products)
                nc.scalar.copy(w_hi[slot][:, :, i, :], w_raw[slot][:, :, i, :]).then_inc(w_high, 1)

            for i in range(4):
                split_high(0, i, 32)
            act.wait_ge(var_ready, 2)
            nc.scalar.activation(sd[:], ve[:], ACT.Sqrt).then_inc(sd_ready, 1)
            for k in range(KD):
                act.wait_ge(xt_ready, KD + k + 1)
                nc.scalar.copy(xt_hi[:, k, :], ps[:, 4 + k, :]).then_inc(xt_high, 1)
            act.wait_ge(negtop_ready, 1)
            for t in range(TT):
                last = nc.scalar.activation(eg[:, t, :], logits[:, t, :], ACT.Exp, bias=negtop[:, t:t + 1])
            last.then_inc(eg_ready, 1)

            def expert(e, last):
                for c in range(HT):
                    g, i = c // 4, c % 4
                    if c == 0:
                        act.wait_ge(b1_set, e + 1)
                    act.wait_ge(h_ready, HT * e + c + 1)
                    nc.scalar.activation(h_f32[c % 2][:], ps[:, 4 + c % 2, :], ACT.Relu, bias=b1_cur[:, 0, c:c + 1])
                    nc.scalar.activation(h_hi[c % 2][:], ps[:, 4 + c % 2, :], ACT.Relu,
                                         bias=b1_cur[:, 0, c:c + 1]).then_inc(h_high, 1)
                    if not (last and g == HG - 1):
                        split_high((g + 1) % 2, i, 32 * (HG // 2 * e + (g + 1) // 2 + 1),
                                   used=(HG - 1) * e + g if g > 0 else None, products=TT * (e + 1) if g == 0 else None)

            with act.Fori(0, E - 1) as e:
                expert(e, False)
            expert(E - 1, True)

        @block.vector
        def _(dve):
            steps = [0]

            def step(ins):
                steps[0] += 1
                ins.then_inc(vector_step, 1)
                dve.wait_ge(vector_step, steps[0])

            def layernorm(src, dst, n):
                for t in range(TT):
                    last = nc.vector.bn_stats(stat[:, t, :], src[:, t, :])
                step(last)
                for t in range(TT):
                    last = nc.vector.bn_aggr(mv[:, t, :], stat[:, t, :])
                step(last)
                nc.vector.tensor_scalar(ve[:], mv[:, :, 1], LN_EPS, None, ALU.add).then_inc(var_ready, 1)
                dve.wait_ge(sd_ready, n)
                step(nc.vector.reciprocal(rs0[:], sd[:]))
                step(nc.vector.tensor_tensor(sq[:], ve[:], rs0[:], ALU.mult))
                step(nc.vector.tensor_tensor(sdn[:], sd[:], sq[:], ALU.add))
                step(nc.vector.tensor_scalar(sq[:], sdn[:], 0.5, None, ALU.mult))
                step(nc.vector.reciprocal(rstd[:], sq[:]))
                for t in range(TT):
                    nc.vector.tensor_scalar(dst[:, t, :], src[:, t, :], mv[:, t, 0:1], rstd[:, t:t + 1],
                                            ALU.subtract, ALU.mult).then_inc(xn_ready, 1)

            nc.vector.memset(ps[:, SCORE_BANK + CHUNKS - 1, :], 0.0).then_inc(psum_zeroed, 1)
            dve.wait_ge(x_loaded, 16)
            layernorm(x0, xn0, 1)
            dve.wait_ge(wq_high, 1)
            nc.vector.tensor_tensor(wq_lo[:], wq_raw[:], wq_hi[:].bitcast(F32), ALU.subtract).then_inc(wq_split, 1)
            for k in range(KD):
                dve.wait_ge(xt_high, k + 1)
                nc.vector.tensor_tensor(xt0_lo[:, k, :], ps[:, k, :], xt0_hi[:, k, :].bitcast(F32),
                                        ALU.subtract).then_inc(xt_split, 1)
            dve.wait_ge(bias_loaded, 48)
            for m in range(KD):
                dve.wait_ge(q_ready, m + 1)
                nc.vector.tensor_scalar(q_out[:, m, :], ps[:, 4 + m, :], bq_sb[:, m:m + 1], SCALE,
                                        ALU.add, ALU.mult).then_inc(q_done if m < KD - 1 else pv_taken, 1)

            def proj_low_part(unit, n, bank):
                kind, a, c = unit
                dve.wait_ge(proj_high, n + 1)
                if kind == "keys":
                    m = KEYS_EVEN[c]
                    cols = slice(KEY0[c], KEY0[c] + m)
                    nc.vector.scalar_tensor_tensor(out=k_lo[:, a, cols], in0=ps[:, bank, 0:m], scalar=bk_sb[:, a:a + 1],
                                                   in1=k_hi[:, a, cols].bitcast(F32), op0=ALU.add,
                                                   op1=ALU.subtract).then_inc(proj_split, 1)
                else:
                    r, w = rows_of(a), D // 2
                    cols = slice(c * w, (c + 1) * w)
                    nc.vector.tensor_tensor(v_lo[0:r, a, cols], ps[0:r, bank, 0:w], v_hi[0:r, a, cols].bitcast(F32),
                                            ALU.subtract).then_inc(proj_split, 1)

            def job_low(b, s, ks):
                for k in ks:
                    n = UNIT0[s % CHUNKS] + k
                    bank = PROJ_BANK + (n % PROJ_BANKS)
                    proj_low_part(units_of(s if b is not None else CHUNKS + s)[k],
                                  unit_no(b, s, k) if b is not None else n, bank)

            def take_context(b, g):
                dve.wait_ge(pv_ready, GROUPS * b + g + 1)
                slot = g % 2
                dve.wait_ge(stored[slot], 16 * (2 * b + g // 2 + 1))
                for h in range(HPG):
                    rows = slice(HD * h, HD * (h + 1))
                    last = nc.vector.tensor_scalar(o_stage[slot][rows, :], ps[rows, PV_BANK, NQ * h:NQ * (h + 1)],
                                                   bv_sb[rows, g:g + 1], None, ALU.add)
                last.then_inc(pv_taken, 1)

            def ctx_high_part(c, loaded, free=None):
                slot, n = c % 2, KEYS_EVEN[c]
                dve.wait_ge(ctx_loaded[slot], loaded)
                if free is not None:
                    dve.wait_ge(proj_ready, free)
                nc.vector.tensor_copy(ctx_hi[slot][:, :, 0:n], ctx_raw[slot][:, :, 0:n]).then_inc(ctx_high, 1)

            dve.wait_ge(zeroed, 5)
            ctx_high_part(0, 16)
            ctx_high_part(1, 16)
            for c in range(CHUNKS):
                if c >= 1:
                    ctx_high_part((c + 1) % CHUNKS, 16 * ((c + 1) // 2 + 1), UNIT0[c])
                job_low(None, c, range(UNITS[c]))

            def batch(b, last, first_batch=False):
                for s in range(STEPS):
                    n = STEPS * b + s
                    dve.wait_ge(scores_ready, 2 * n + 1)
                    nc.vector.tensor_reduce(mx[:, 0:1], ps[:, SCORE_BANK:SCORE_BANK + FULL, 0:KEYS[0]], AX.XY,
                                            ALU.max)
                    dve.wait_ge(scores_ready, 2 * n + 2)
                    nc.vector.tensor_reduce(mx[:, 1:2], ps[:, SCORE_BANK + FULL, 0:KEYS[FULL]], AX.X,
                                            ALU.max).then_inc(part_max, 1)
                    dve.wait_ge(part_max, n + 1)
                    nc.vector.tensor_reduce(negmax[:], mx[:], AX.X, ALU.max, negate=True).then_inc(negmax_ready, 1)
                    if not (last and s + 1 >= CHUNKS):
                        ctx_high_part((s + 1) % CHUNKS, 16 * (CHUNKS // 2 + 1 + (STEPS // 2) * b + (s + 1) // 2),
                                      unit_no(b, s, 0))
                    if s % 2 == 0 and s >= 2:
                        take_context(b, s // 2 - 1)
                    dve.wait_ge(exp_done, n + 1)
                    nc.vector.tensor_reduce(total[:], rowsum[:], AX.X, ALU.add).then_inc(total_ready, 1)
                    dve.wait_ge(total_ready, n + 1)
                    nc.vector.reciprocal(rinv[:], total[:]).then_inc(rinv_ready, 1)
                    dve.wait_ge(rinv_ready, n + 1)
                    for c in range(CHUNKS):
                        part = probs[:, KEY0[c]:KEY0[c] + KEYS[c]]
                        nc.vector.tensor_scalar(part, part, rinv[:, 0:1], None, ALU.mult).then_inc(norm_ready, 1)
                    has_job = not (last and s >= CHUNKS)
                    u = UNITS[s % CHUNKS]
                    if has_job:
                        job_low(b, s, range(u - 1))
                    for c in range(CHUNKS):
                        dve.wait_ge(pt_high, CHUNKS * n + c + 1)
                        m = CHUNK_TILES[c]
                        nc.vector.tensor_tensor(pt_lo[:, TILE0[c]:TILE0[c] + m, s % 2, :],
                                                ps[:, SCORE_BANK + c, 0:m * P].rearrange("p (t r) -> p t r", t=m),
                                                pt_hi[:, TILE0[c]:TILE0[c] + m, s % 2, :].bitcast(F32),
                                                ALU.subtract).then_inc(pt_split, 1)
                    if has_job:
                        job_low(b, s, [u - 1])
                take_context(b, GROUPS - 1)

            with dve.Fori(0, B - 1) as b:
                batch(b, False)
            batch(B - 1, True)

            dve.wait_ge(ot_high, 1)
            nc.vector.tensor_tensor(ot_lo[:], ot_raw[:], ot_hi[:].bitcast(F32), ALU.subtract).then_inc(ot_split, 1)
            dve.wait_ge(x1_loaded, 16)
            dve.wait_ge(bo_loaded, 16)
            for t in range(TT):
                last = nc.vector.tensor_tensor(acc[:, t, :], acc[:, t, :], bo_bc[:], ALU.add)
            step(last)
            for t in range(TT):
                dve.wait_ge(x1_product, t + 1)
                last = nc.vector.tensor_tensor(acc[:, t, :], ps[:, t, :], acc[:, t, :], ALU.add)
            step(last)
            layernorm(acc, xn, 2)
            for k in range(KD):
                dve.wait_ge(xt_high, KD + k + 1)
                nc.vector.tensor_tensor(xt_lo[:, k, :], ps[:, 4 + k, :], xt_hi[:, k, :].bitcast(F32),
                                        ALU.subtract).then_inc(xt_split, 1)
            dve.wait_ge(small_loaded, 64)
            dve.wait_ge(numbers_ready, 1)
            dve.wait_ge(logits_product, 1)
            for t in range(TT):
                last = nc.vector.tensor_tensor(logits[:, t, :], ps[:, 0, t * E:(t + 1) * E], rb_bc[:], ALU.add)
            step(last)
            for t in range(TT):
                last = nc.vector.max(top[:, t, :], logits[:, t, :])
            step(last)
            nc.vector.tensor_scalar(negtop[:], top[:, :, 0], -1.0, None, ALU.mult).then_inc(negtop_ready, 1)
            for t in range(TT):
                last = nc.vector.max_index(top_at[:, t, :], top[:, t, :], logits[:, t, :])
            step(last)
            step(nc.vector.tensor_copy(top_atf[:], top_at[:]))
            for t in range(TT):
                last = nc.vector.tensor_scalar(is_first[:, t, :], expert_no[:], top_atf[:, t, 0:1], None, ALU.is_equal)
            step(last)
            for t in range(TT):
                last = nc.vector.scalar_tensor_tensor(out=keep[:, t, :], in0=expert_no[:], scalar=top_atf[:, t, 1:2],
                                                      in1=is_first[:, t, :], op0=ALU.is_equal, op1=ALU.add)
            step(last)
            dve.wait_ge(eg_ready, 1)
            step(nc.vector.tensor_tensor(egk[:], eg[:], keep[:], ALU.mult))
            step(nc.vector.tensor_reduce(gsum[:], egk[:], AX.X, ALU.add))
            step(nc.vector.reciprocal(ginv[:], gsum[:]))
            for t in range(TT):
                last = nc.vector.tensor_scalar(gates[:, t, :], egk[:, t, :], ginv[:, t:t + 1], None, ALU.mult)
            last.then_inc(gates_ready, 1)
            dve.wait_ge(gates_ready, 1)
            step(nc.vector.tensor_copy(gates_e[:], gates[:].rearrange("p t e -> p e t")))
            dve.wait_ge(gates_turned, 1)
            nc.vector.tensor_copy(gates_t[:], ps[0:E, 1, :]).then_inc(gates_t_ready, 1)
            for t in range(TT):
                dve.wait_ge(b2_product, t + 1)
                nc.vector.tensor_tensor(acc[:, t, :], ps[:, 4 + t, :], acc[:, t, :], ALU.add).then_inc(y_taken, 1)
            dve.wait_ge(y_taken, TT)

            def expert(e):
                if isinstance(e, int):
                    b1_e, gate_e = b1_sb[:, e:e + 1, :], gates_e[:, e:e + 1, :]
                else:
                    b1_e, gate_e = b1_sb[:, bass.ds(e, 1), :], gates_e[:, bass.ds(e, 1), :]
                nc.vector.tensor_copy(b1_cur[:], b1_e).then_inc(b1_set, 1)
                nc.vector.tensor_copy(gate_cur[:], gate_e).then_inc(gate_set, 1)
                for c in range(HT):
                    dve.wait_ge(h_high, HT * e + c + 1)
                    nc.vector.tensor_tensor(h_lo[c % 2][:], h_f32[c % 2][:], h_hi[c % 2][:].bitcast(F32),
                                            ALU.subtract).then_inc(h_split, 1)
                dve.wait_ge(gate_set, e + 1)
                for t in range(TT):
                    dve.wait_ge(y_ready, TT * e + t + 1)
                    nc.vector.scalar_tensor_tensor(out=acc[:, t, :], in0=ps[:, t, :], scalar=gate_cur[:, 0, t:t + 1],
                                                   in1=acc[:, t, :], op0=ALU.mult, op1=ALU.add).then_inc(y_taken, 1)
                dve.wait_ge(y_taken, TT * (e + 2))

            with dve.Fori(0, E - 1) as e:
                expert(e)
            expert(E - 1)

        @block.tensor
        def _(pe):
            def turn(src, bank0, n):
                pe.wait_ge(xn_ready, n)
                for k in range(KD):
                    for t in range(TT):
                        last = pe.transpose(ps[:, bank0 + k, t * P:(t + 1) * P], src[:, t, k * P:(k + 1) * P], ident[:])
                    last.then_inc(xt_ready, 1)

            pe.wait_ge(ident_ready, 1)
            pe.wait_ge(psum_zeroed, 1)
            turn(xn0, 0, TT)
            pe.wait_ge(wq_split, 1)
            pe.wait_ge(xt_split, KD)
            for m in range(KD):
                for k in range(KD):
                    last = three_pass(pe, ps[:, 4 + m, :], wq_hi[:, k, m * P:(m + 1) * P], wq_lo[:, k, m * P:(m + 1) * P],
                                      xt0_hi[:, k, :], xt0_lo[:, k, :], k == 0, k == KD - 1)
                last.then_inc(q_ready, 1)

            def project(unit, n, bank):
                kind, a, c = unit
                for k in range(KC):
                    if kind == "keys":
                        slot, m, cols = c % 2, KEYS_EVEN[c], slice(a * P, (a + 1) * P)
                        last = three_pass(pe, ps[:, bank, 0:m], wk_hi[:, k, cols], wk_lo[:, k, cols],
                                          ctx_hi[slot][:, k, 0:m], ctx_lo[slot][:, k, 0:m], k == 0, k == KC - 1)
                    else:
                        chunk = max(i for i in range(CHUNKS) if TILE0[i] <= a)
                        slot, r, w = chunk % 2, rows_of(a), D // 2
                        keys = slice((a - TILE0[chunk]) * P, (a - TILE0[chunk]) * P + r)
                        cols = slice(c * w, (c + 1) * w)
                        last = three_pass(pe, ps[0:r, bank, 0:w], ctx_hi[slot][:, k, keys], ctx_lo[slot][:, k, keys],
                                          wv_hi[:, k, cols], wv_lo[:, k, cols], k == 0, k == KC - 1)
                last.then_inc(proj_ready, 1)

            def run_job(b, s, ks):
                for k in ks:
                    local = UNIT0[s % CHUNKS] + k
                    n = unit_no(b, s, k) if b is not None else local
                    if k == 0:
                        pe.wait_ge(ctx_split, job_no(b, s) + 1 if b is not None else s + 1)
                    if b is not None or local >= PROJ_BANKS:
                        pe.wait_ge(proj_split, n - PROJ_BANKS + 1)
                    project(units_of(s if b is not None else CHUNKS + s)[k], n, PROJ_BANK + local % PROJ_BANKS)

            pe.wait_ge(wkv_split, 2)
            pe.wait_ge(q_done, KD - 1)
            for c in range(CHUNKS):
                run_job(None, c, range(UNITS[c]))

            def context(b, g):
                pe.wait_ge(proj_split, value_units_done(b, g))
                pe.wait_ge(pv_taken, GROUPS * b + g + 1)
                for t in range(KT):
                    r, cols = rows_of(t), slice(g * P, (g + 1) * P)
                    last = three_pass(pe, ps[:, PV_BANK, 0:HPG * NQ], v_hi[0:r, t, cols], v_lo[0:r, t, cols],
                                      pt_hi[0:r, t, :, :], pt_lo[0:r, t, :, :], t == 0, t == KT - 1)
                last.then_inc(pv_ready, 1)

            def batch(b, last_batch):
                for s in range(STEPS):
                    g, n = s // 2, STEPS * b + s
                    if s % 2 == 0:
                        pe.wait_ge(qbd_ready, GROUPS * b + g + 1)
                        pe.wait_ge(proj_split, key_units_done(b, g))
                    rows = slice((s % 2) * P, (s % 2 + 1) * P)
                    for c in range(CHUNKS):
                        if s > 0:
                            pe.wait_ge(pt_split, CHUNKS * (n - 1) + c + 1)
                        m = KEYS_EVEN[c]
                        cols = slice(KEY0[c], KEY0[c] + m)
                        last = three_pass(pe, ps[:, SCORE_BANK + c, 0:m], qbd_hi[:, g, rows], qbd_lo[:, g, rows],
                                          k_hi[:, g, cols], k_lo[:, g, cols], True, True)
                        if c >= FULL - 1:
                            last.then_inc(scores_ready, 1)
                    if s % 2 == 0 and s >= 2:
                        context(b, g - 1)
                    has_job = not (last_batch and s >= CHUNKS)
                    u = UNITS[s % CHUNKS]
                    if has_job:
                        run_job(b, s, range(u - 1))
                    for c in range(CHUNKS):
                        pe.wait_ge(norm_ready, CHUNKS * n + c + 1)
                        for i in range(CHUNK_TILES[c]):
                            r = rows_of(TILE0[c] + i)
                            key = KEY0[c] + i * P
                            last = pe.transpose(ps[0:r, SCORE_BANK + c, i * P:(i + 1) * P], probs[:, key:key + r], ident[:])
                        last.then_inc(pt_ready, 1)
                    if has_job:
                        run_job(b, s, [u - 1])
                pe.wait_ge(pt_split, CHUNKS * STEPS * (b + 1))
                context(b, GROUPS - 1)

            with pe.Fori(0, B - 1) as b:
                batch(b, False)
            batch(B - 1, True)

            pe.wait_ge(ot_split, 1)
            pe.wait_ge(wo_split, 1)
            for t in range(TT):
                for k in range(KD):
                    rows = slice(t * P, (t + 1) * P)
                    last = three_pass(pe, ps[:, t, :], ot_hi[:, k, rows], ot_lo[:, k, rows], wo_hi[:, k, :], wo_lo[:, k, :],
                                      k == 0, k == KD - 1)
                last.then_inc(x1_product, 1)
            turn(xn, 4, 2 * TT)
            pe.wait_ge(xt_split, 2 * KD)
            pe.wait_ge(rw_split, 1)
            for t in range(TT):
                for k in range(KD):
                    rows = slice(t * P, (t + 1) * P)
                    last = three_pass(pe, ps[:, 0, t * E:(t + 1) * E], xt_hi[:, k, rows], xt_lo[:, k, rows],
                                      rw_hi[:, k, :], rw_lo[:, k, :], k == 0, k == KD - 1)
            last.then_inc(logits_product, 1)
            pe.wait_ge(gates_ready, 1)
            for t in range(TT):
                last = pe.transpose(ps[0:E, 1, t * P:(t + 1) * P], gates[:, t, :], ident[:])
            last.then_inc(gates_turned, 1)
            pe.wait_ge(gates_t_ready, 1)
            for t in range(TT):
                pe.matmul(ps[:, 4 + t, :], gates_t[:, t * P:(t + 1) * P], b2_sb[:], start=True,
                          stop=True).then_inc(b2_product, 1)
            pe.wait_ge(y_taken, TT)

            def hidden(e, c):
                g, i = c // 4, c % 4
                if i == 0:
                    pe.wait_ge(w_split, 4 * (HG * e + g + 1))
                if c >= 2:
                    pe.wait_ge(h_split, HT * e + c - 1)
                cols = slice(i * P, (i + 1) * P)
                for k in range(KD):
                    last = three_pass(pe, ps[:, 4 + c % 2, :], w_hi[g % 2][:, 0, k, cols], w_lo[g % 2][:, 0, k, cols],
                                      xt_hi[:, k, :], xt_lo[:, k, :], k == 0, k == KD - 1)
                last.then_inc(h_ready, 1)

            def outputs(e, c):
                g, i = c // 4, c % 4
                pe.wait_ge(h_split, HT * e + c + 1)
                if c == 0:
                    pe.wait_ge(y_taken, TT * (e + 1))
                for t in range(TT):
                    rows = slice(t * P, (t + 1) * P)
                    last = three_pass(pe, ps[:, t, :], h_hi[c % 2][:, rows], h_lo[c % 2][:, rows],
                                      w_hi[g % 2][:, 1, i, :], w_lo[g % 2][:, 1, i, :], c == 0, c == HT - 1)
                    if c == HT - 1:
                        last.then_inc(y_ready, 1)
                if i == 3 and c < HT - 1:
                    last.then_inc(w_used, 1)

            def expert(e):
                hidden(e, 0)
                for c in range(1, HT):
                    hidden(e, c)
                    outputs(e, c - 1)
                outputs(e, HT - 1)

            with pe.Fori(0, E - 1) as e:
                expert(e)
            expert(E - 1)


_INS = ["x", "ctx_t", "wq", "bq_t", "wk", "bk_t", "wv", "bv_t", "wo", "bo", "router_w", "router_b",
        "w1", "b1_t", "w2", "b2"]


def kernel(**inputs):
    import numpy as _np
    import concourse.bacc as _bacc
    from concourse import mybir as _mybir
    from concourse.bass_utils import run_bass_kernel_spmd as _run

    a = {k: _np.asarray(v) for k, v in inputs.items()}

    def columns(v):
        return v.reshape(-1, 128).T

    laid = {
        "x": a["x"],
        "ctx_t": a["ctx_768"].transpose(0, 2, 1),
        "wq": a["L0_xattn_Wq"], "bq_t": columns(a["L0_xattn_bq"]),
        "wk": a["L0_xattn_Wk"], "bk_t": columns(a["L0_xattn_bk"]),
        "wv": a["L0_xattn_Wv"], "bv_t": columns(a["L0_xattn_bv"]),
        "wo": a["L0_xattn_Wo"], "bo": a["L0_xattn_bo"],
        "router_w": a["L0_ffn_router_w"], "router_b": a["L0_ffn_router_b"],
        "w1": a["L0_ffn_w1"],
        "b1_t": a["L0_ffn_b1"].reshape(8, 16, 128).transpose(2, 0, 1),
        "w2": a["L0_ffn_w2"], "b2": a["L0_ffn_b2"],
    }
    nc = _bacc.Bacc("TRN2", target_bir_lowering=False, num_devices=1)
    arrays, args = {}, []
    for name in _INS:
        v = _np.ascontiguousarray(laid[name])
        arrays[f"in_{name}_dram"] = v
        args.append(nc.dram_tensor(f"in_{name}_dram", v.shape, _mybir.dt.from_np(v.dtype), kind="ExternalInput").ap())
    args.append(nc.dram_tensor("out_0_dram", a["x"].shape, _mybir.dt.float32, kind="ExternalOutput").ap())
    bass_perceiver_layer_kernel(nc, *args)
    r = _run(nc, [arrays], core_ids=[0])
    return r.results[0]["out_0_dram"]
```

```python
from contextlib import ExitStack

import concourse.bass as bass
from concourse import mybir

ALU = mybir.AluOpType
ACT = mybir.ActivationFunctionType
AX = mybir.AxisListType
F32 = mybir.dt.float32
F32R = mybir.dt.float32r
U32 = mybir.dt.uint32
I32 = mybir.dt.int32

P = 128
BANK = 512
LN_EPS = 1e-5


def bass_perceiver_layer_kernel(nc, x, ctx_t, wq, bq_t, wk, bk_t, wv, bv_t, wo, bo, router_w, router_b,
                                w1, b1_t, w2, b2, out):
    B, NQ, D = x.shape
    DC, NK = ctx_t.shape[1:]
    T = B * NQ
    TT = T // P
    KD = D // P
    KC = DC // P
    HEADS, HD = 16, D // 16
    HPG = P // HD
    GROUPS = HEADS // HPG
    STEPS = HEADS // 2
    SCALE = float(HD) ** -0.5
    E, _, HID = w1.shape
    KT = (NK + P - 1) // P
    KLAST = NK - (KT - 1) * P
    CHUNK_TILES = [3, 3, 3, 4]
    CHUNKS = len(CHUNK_TILES)
    TILE0 = [sum(CHUNK_TILES[:c]) for c in range(CHUNKS)]
    KEY0 = [P * t for t in TILE0]
    KEYS = [min(NK, KEY0[c] + P * CHUNK_TILES[c]) - KEY0[c] for c in range(CHUNKS)]
    KEYS_EVEN = [n + n % 2 for n in KEYS]
    NKE = NK + NK % 2
    assert sum(CHUNK_TILES) == KT and max(KEYS_EVEN) <= BANK and T == BANK and D == BANK
    FULL = CHUNKS - 1
    assert len(set(KEYS[:FULL])) == 1

    UNITS = [2 + n for n in CHUNK_TILES]
    UNIT0 = [sum(UNITS[:c]) for c in range(CHUNKS)]
    HALF_UNITS = sum(UNITS)
    BATCH_UNITS = 2 * HALF_UNITS
    PROJ_BANKS = 3
    assert HALF_UNITS % PROJ_BANKS == 0
    HG = HID // (4 * P)
    HT = HID // P
    TOP_K = 2
    BLOCK = 2 * P
    BT = BLOCK // P
    assert T <= 2 * BLOCK
    MAX_BLOCKS = (TOP_K * T + (E - 1) * (BLOCK - 1)) // BLOCK + 1
    TABLE = MAX_BLOCKS + 1

    q_dram = nc.dram_tensor("q_scratch", (D, T), F32, kind="Internal").ap()
    o_dram = nc.dram_tensor("o_scratch", (D, T), F32, kind="Internal").ap()

    x_rows = x.rearrange("b q d -> (b q) d").rearrange("(t p) d -> p t d", p=P)
    out_rows = out.rearrange("b q d -> (b q) d").rearrange("(t p) d -> p t d", p=P)
    ctx_view = ctx_t.rearrange("b (c p) n -> b p c n", p=P)

    with ExitStack() as stack:
        def sb(name, shape, dt, where=stack):
            return where.enter_context(nc.sbuf_tensor(name, shape, dt))

        def sem(name):
            return stack.enter_context(nc.semaphore(name))

        ps = stack.enter_context(nc.psum_tensor("ps", [P, 8, BANK], F32))
        SCORE_BANK, PROJ_BANK, PV_BANK = 0, 4, 7

        ident = sb("ident", [P, P], F32)
        bq_sb = sb("bq_sb", [P, KD], F32)
        bk_sb = sb("bk_sb", [P, KD], F32)
        bv_sb = sb("bv_sb", [P, KD], F32)
        stat = sb("stat", [P, TT, 6], F32)
        mv = sb("mv", [P, TT, 2], F32)
        ve = sb("ve", [P, TT], F32)
        sd = sb("sd", [P, TT], F32)
        rs0 = sb("rs0", [P, TT], F32)
        sq = sb("sq", [P, TT], F32)
        sdn = sb("sdn", [P, TT], F32)
        rstd = sb("rstd", [P, TT], F32)

        attn = ExitStack()
        v_hi = sb("v_hi", [P, KT, D], F32R, attn)
        v_lo = sb("v_lo", [P, KT, D], F32R, attn)
        pt_hi = sb("pt_hi", [P, KT, 2, P], F32R, attn)
        pt_lo = sb("pt_lo", [P, KT, 2, P], F32R, attn)
        k_hi = sb("k_hi", [P, GROUPS, NKE], F32R, attn)
        k_lo = sb("k_lo", [P, GROUPS, NKE], F32R, attn)
        ctx_raw = [sb(f"ctx_raw{i}", [P, KC, max(KEYS_EVEN)], F32, attn) for i in range(2)]
        ctx_hi = [sb(f"ctx_hi{i}", [P, KC, max(KEYS_EVEN)], F32R, attn) for i in range(2)]
        ctx_lo = [sb(f"ctx_lo{i}", [P, KC, max(KEYS_EVEN)], F32R, attn) for i in range(2)]
        wk_hi = sb("wk_hi", [P, KC, D], F32R, attn)
        wk_lo = sb("wk_lo", [P, KC, D], F32R, attn)
        wv_hi = sb("wv_hi", [P, KC, D], F32R, attn)
        wv_lo = sb("wv_lo", [P, KC, D], F32R, attn)
        probs = sb("probs", [P, NK], F32, attn)
        qbd_hi = sb("qbd_hi", [P, GROUPS, HPG * NQ], F32R, attn)
        qbd_lo = sb("qbd_lo", [P, GROUPS, HPG * NQ], F32R, attn)
        no_query = sb("no_query", [P, NQ], F32, attn)
        q_stage = sb("q_stage", [P, GROUPS, NQ], F32, attn)
        o_stage = [sb(f"o_stage{i}", [P, NQ], F32, attn) for i in range(2)]
        mx = sb("mx", [P, 2], F32, attn)
        negmax = sb("negmax", [P, 1], F32, attn)
        rowsum = sb("rowsum", [P, 2], F32, attn)
        total = sb("total", [P, 1], F32, attn)
        rinv = sb("rinv", [P, 1], F32, attn)
        attn.close()

        first = ExitStack()
        wq_raw = sb("wq_raw", [P, KD, D], F32, first)
        wq_hi = sb("wq_hi", [P, KD, D], F32R, first)
        wq_lo = sb("wq_lo", [P, KD, D], F32R, first)
        wkv_raw = sb("wkv_raw", [P, 2, KC, D], F32, first)
        sb("rest_of_v", [P, 2 * KT * D - 3 * KD * D - 2 * KC * D], F32, first)
        x0 = sb("x0", [P, TT, D], F32, first)
        xn0 = sb("xn0", [P, TT, D], F32, first)
        q_out = sb("q_out", [P, KD, T], F32, first)
        sb("rest_of_pt", [P, 4 * KT * P - 3 * TT * D], F32, first)
        xt0_hi = sb("xt0_hi", [P, KD, T], F32R, first)
        xt0_lo = sb("xt0_lo", [P, KD, T], F32R, first)
        first.close()

        moe = ExitStack()
        w_raw = [sb(f"w_raw{i}", [P, 2, 4, BANK], F32, moe) for i in range(2)]
        w_hi = [sb(f"w_hi{i}", [P, 2, 4, BANK], F32R, moe) for i in range(2)]
        w_lo = [sb(f"w_lo{i}", [P, 2, 4, BANK], F32R, moe) for i in range(2)]
        h_f32 = [sb(f"h_f32_{i}", [P, BLOCK], F32, moe) for i in range(2)]
        h_hi = [sb(f"h_hi{i}", [P, BLOCK], F32R, moe) for i in range(2)]
        h_lo = [sb(f"h_lo{i}", [P, BLOCK], F32R, moe) for i in range(2)]
        bo_bc = sb("bo_bc", [P, D], F32, moe)
        acc = sb("acc", [P, TT, D], F32, moe)
        xn = sb("xn", [P, TT, D], F32, moe)
        xt_hi = sb("xt_hi", [P, KD, T], F32R, moe)
        xt_lo = sb("xt_lo", [P, KD, T], F32R, moe)
        rw_raw = sb("rw_raw", [P, KD, E], F32, moe)
        rw_hi = sb("rw_hi", [P, KD, E], F32R, moe)
        rw_lo = sb("rw_lo", [P, KD, E], F32R, moe)
        rb_bc = sb("rb_bc", [P, E], F32, moe)
        b2_sb = sb("b2_sb", [E, D], F32, moe)
        logits = sb("logits", [P, TT, E], F32, moe)
        top = sb("top", [P, TT, 8], F32, moe)
        top_at = sb("top_at", [P, TT, 8], U32, moe)
        top_atf = sb("top_atf", [P, TT, 8], F32, moe)
        expert_no = sb("expert_no", [P, E], F32, moe)
        negtop = sb("negtop", [P, TT], F32, moe)
        is_first = sb("is_first", [P, TT, E], F32, moe)
        keep = sb("keep", [P, TT, E], F32, moe)
        eg = sb("eg", [P, TT, E], F32, moe)
        egk = sb("egk", [P, TT, E], F32, moe)
        gsum = sb("gsum", [P, TT], F32, moe)
        ginv = sb("ginv", [P, TT], F32, moe)
        gates = sb("gates", [P, TT, E], F32, moe)
        gates_e = sb("gates_e", [P, E, TT], F32, moe)
        gates_t = sb("gates_t", [E, T], F32, moe)
        b1_sb = sb("b1_sb", [P, E, HT], F32, moe)
        b1_cur = sb("b1_cur", [P, 1, HT], F32, moe)
        gate_cur = sb("gate_cur", [P, 1, TT], F32, moe)
        before = sb("before", [P, P], F32, moe)
        ones = sb("ones", [P, P], F32, moe)
        slot_no = sb("slot_no", [P, BLOCK], F32, moe)
        block_no = sb("block_no", [P, TABLE], F32, moe)
        seen = sb("seen", [P, TT + 1, E], F32, moe)
        in_tile = sb("in_tile", [P, TT, E], F32, moe)
        rank1 = sb("rank1", [P, TT, E], F32, moe)
        rankk = sb("rankk", [P, TT, E], F32, moe)
        rank_e = sb("rank_e", [P, E, TT], F32, moe)
        some = sb("some", [P, E], F32, moe)
        PAD = E // 2
        sums = [sb(f"sums{i}", [P, PAD + E], F32, moe) for i in range(4)]
        past = sb("past", [P, TABLE, E], F32, moe)
        past_n = sb("past_n", [P, TABLE, E], F32, moe)
        owner = sb("owner", [P, TABLE], F32, moe)
        start = sb("start", [P, TABLE], F32, moe)
        start2 = sb("start2", [P, TABLE], F32, moe)
        base = sb("base", [P, TABLE], F32, moe)
        table_f = sb("table_f", [P, TABLE + 1], F32, moe)
        table = sb("table", [P, TABLE + 1], I32, moe)
        key_cur = sb("key_cur", [P, 1, TT], F32, moe)
        stage2 = ExitStack()
        wo_raw = sb("wo_raw", [P, KD, D], F32, stage2)
        wo_hi = sb("wo_hi", [P, KD, D], F32R, stage2)
        wo_lo = sb("wo_lo", [P, KD, D], F32R, stage2)
        ot_raw = sb("ot_raw", [P, KD, T], F32, stage2)
        ot_hi = sb("ot_hi", [P, KD, T], F32R, stage2)
        ot_lo = sb("ot_lo", [P, KD, T], F32R, stage2)
        stage2.close()
        xn_hi = sb("xn_hi", [P, TT, D], F32R, moe)
        xn_lo = sb("xn_lo", [P, TT, D], F32R, moe)
        sel = sb("sel", [P, TT, BLOCK], F32R, moe)
        sel_t = sb("sel_t", [P, BT, T], F32R, moe)
        xg_hi = sb("xg_hi", [P, KD, BLOCK], F32R, moe)
        xg_lo = sb("xg_lo", [P, KD, BLOCK], F32R, moe)
        y_hi = sb("y_hi", [P, BT, D], F32R, moe)
        y_lo = sb("y_lo", [P, BT, D], F32R, moe)
        moe.close()

        x_loaded, wq_loaded, bias_loaded, wkv_loaded = sem("x_loaded"), sem("wq_loaded"), sem("bias_loaded"), sem("wkv_loaded")
        ctx_loaded = [sem(f"ctx_loaded{i}") for i in range(2)]
        q_loaded, ot_loaded, wo_loaded = sem("q_loaded"), sem("ot_loaded"), sem("wo_loaded")
        x1_loaded, bo_loaded, small_loaded = sem("x1_loaded"), sem("bo_loaded"), sem("small_loaded")
        w_loaded = [sem(f"w_loaded{i}") for i in range(2)]
        out_stored = sem("out_stored")
        stored = [sem(f"stored{i}") for i in range(2)]
        zeroed, ident_ready, psum_zeroed = sem("zeroed"), sem("ident_ready"), sem("psum_zeroed")
        wq_high, wq_split, wkv_high, wkv_split = sem("wq_high"), sem("wq_split"), sem("wkv_high"), sem("wkv_split")
        q_ready, q_done = sem("q_ready"), sem("q_done")
        var_ready, sd_ready, xn_ready = sem("var_ready"), sem("sd_ready"), sem("xn_ready")
        xt_ready, xt_high, xt_split = sem("xt_ready"), sem("xt_high"), sem("xt_split")
        vector_step = sem("vector_step")
        qbd_high, qbd_ready = sem("qbd_high"), sem("qbd_ready")
        ctx_high, ctx_split = sem("ctx_high"), sem("ctx_split")
        proj_ready, proj_high, proj_split = sem("proj_ready"), sem("proj_high"), sem("proj_split")
        scores_ready, part_max, negmax_ready = sem("scores_ready"), sem("part_max"), sem("negmax_ready")
        exp_done, total_ready, rinv_ready, norm_ready = sem("exp_done"), sem("total_ready"), sem("rinv_ready"), sem("norm_ready")
        pt_ready, pt_high, pt_split = sem("pt_ready"), sem("pt_high"), sem("pt_split")
        pv_ready, pv_taken = sem("pv_ready"), sem("pv_taken")
        wo_high, wo_split, ot_high, ot_split = sem("wo_high"), sem("wo_split"), sem("ot_high"), sem("ot_split")
        x_bo_ready, x1_product = sem("x_bo_ready"), sem("x1_product")
        rw_high, rw_split, numbers_ready = sem("rw_high"), sem("rw_split"), sem("numbers_ready")
        logits_product, negtop_ready, eg_ready = sem("logits_product"), sem("negtop_ready"), sem("eg_ready")
        gates_ready, gates_turned, gates_t_ready = sem("gates_ready"), sem("gates_turned"), sem("gates_t_ready")
        b2_product = sem("b2_product")
        counts_product, table_ready, xn_high, xn_split = sem("counts_product"), sem("table_ready"), sem("xn_high"), sem("xn_split")
        w1_high, w1_split, w2_high, w2_split = sem("w1_high"), sem("w1_split"), sem("w2_high"), sem("w2_split")
        w_used, b1_set, gate_set, key_set, sel_ready = sem("w_used"), sem("b1_set"), sem("gate_set"), sem("key_set"), sem("sel_ready")
        sel_turned, sel_t_taken = sem("sel_turned"), [sem(f"sel_t_taken{i}") for i in range(BT)]
        gather_ready, xg_high, xg_low = sem("gather_ready"), sem("xg_high"), sem("xg_low")
        h_ready, h_high, h_split = sem("h_ready"), sem("h_high"), sem("h_split")
        y_ready, y_high, y_split, scatter_ready = sem("y_ready"), sem("y_high"), sem("y_split"), sem("scatter_ready")
        y_taken = sem("y_taken")

        def job_no(b, s):
            return CHUNKS + STEPS * b + s

        def unit_no(b, s, k):
            return HALF_UNITS + BATCH_UNITS * b + HALF_UNITS * (s // CHUNKS) + UNIT0[s % CHUNKS] + k

        def key_units_done(b, g):
            return BATCH_UNITS * b + HALF_UNITS * (g // 2) + UNIT0[CHUNKS - 1] + g % 2 + 1

        def value_units_done(b, g):
            return BATCH_UNITS * b + HALF_UNITS * (g // 2 + 1)

        def units_of(s):
            half, c = (1 - s // CHUNKS) if s >= 0 else 0, s % CHUNKS
            return [("keys", 2 * half + i, c) for i in range(2)] + \
                   [("values", TILE0[c] + i, half) for i in range(CHUNK_TILES[c])]

        def rows_of(t):
            return P if t < KT - 1 else KLAST

        def three_pass(pe, acc_ap, a_hi, a_lo, b_hi, b_lo, start, stop):
            pe.matmul(acc_ap, a_hi, b_hi, start=start, stop=False)
            pe.matmul(acc_ap, a_hi, b_lo, start=False, stop=False)
            return pe.matmul(acc_ap, a_lo, b_hi, start=False, stop=stop)

        block = stack.enter_context(nc.Block())

        @block.sync
        def _(sp):
            def load_ctx(b, c, slot):
                n = KEYS[c]
                sp.dma_start(ctx_raw[slot][:, :, 0:n],
                             ctx_view[b, :, :, KEY0[c]:KEY0[c] + n] if isinstance(b, int) else
                             ctx_view[bass.ds(b, 1), :, :, KEY0[c]:KEY0[c] + n].rearrange("o p c n -> (o p) c n")
                             ).then_inc(ctx_loaded[slot], 16)

            def load_queries(b):
                sp.dma_start(q_stage[:], q_dram.rearrange("(g p) t -> p g t", p=P)[:, :, bass.ds(b * NQ, NQ)]
                             ).then_inc(q_loaded, 16)

            def store_context(b, g):
                slot = g % 2
                sp.dma_start(o_dram[g * P:(g + 1) * P, bass.ds(b * NQ, NQ)], o_stage[slot][:]).then_inc(stored[slot], 16)

            sp.dma_start(x0[:], x_rows).then_inc(x_loaded, 16)
            sp.dma_start(wq_raw[:], wq.rearrange("(k p) n -> p k n", p=P)).then_inc(wq_loaded, 16)
            sp.dma_start(bq_sb[:], bq_t).then_inc(bias_loaded, 16)
            sp.dma_start(bk_sb[:], bk_t).then_inc(bias_loaded, 16)
            sp.dma_start(bv_sb[:], bv_t).then_inc(bias_loaded, 16)
            sp.dma_start(wkv_raw[:, 0], wk.rearrange("(k p) n -> p k n", p=P)).then_inc(wkv_loaded, 16)
            sp.dma_start(wkv_raw[:, 1], wv.rearrange("(k p) n -> p k n", p=P)).then_inc(wkv_loaded, 16)
            load_ctx(0, 0, 0)
            load_ctx(0, 1, 1)
            for m in range(2, CHUNKS):
                sp.wait_ge(ctx_split, m - 1)
                load_ctx(0, m, m % 2)
            sp.wait_ge(q_done, KD - 1)
            sp.wait_ge(pv_taken, 1)
            for i in range(2):
                half = slice(i * KD // 2, (i + 1) * KD // 2)
                sp.dma_start(q_dram.rearrange("(g p) t -> p g t", p=P)[:, half], q_out[:, half]).then_inc(stored[i], 16)
            for c in range(2):
                sp.wait_ge(ctx_split, CHUNKS - 1 + c)
                load_ctx(0, c, c % 2)
            for i in range(2):
                sp.wait_ge(stored[i], 16)
            load_queries(0)

            def batch(b, last):
                for s in range(STEPS):
                    if s == 0 and not last:
                        sp.wait_ge(qbd_ready, GROUPS * (b + 1))
                        load_queries(b + 1)
                    if s % 2 == 0 and s >= 2:
                        sp.wait_ge(pv_taken, GROUPS * b + s // 2 + 1)
                        store_context(b, s // 2 - 1)
                    if not (last and s + 2 >= CHUNKS):
                        sp.wait_ge(ctx_split, job_no(b, s) + 1)
                        nb = b if s + 2 < CHUNKS or s + 2 >= STEPS else b + 1
                        if s + 2 >= STEPS:
                            nb = b + 1
                        load_ctx(nb, (s + 2) % CHUNKS, s % 2)
                    if s == STEPS - 1:
                        sp.wait_ge(pv_taken, GROUPS * (b + 1) + 1)
                        store_context(b, GROUPS - 1)

            with sp.Fori(0, B - 1) as b:
                batch(b, False)
            batch(B - 1, True)

            for i in range(2):
                sp.wait_ge(stored[i], 16 * (2 * B + 1))
            sp.dma_start(ot_raw[:], o_dram.rearrange("(k p) t -> p k t", p=P)).then_inc(ot_loaded, 16)
            sp.dma_start(wo_raw[:], wo.rearrange("(k p) n -> p k n", p=P)).then_inc(wo_loaded, 16)
            sp.dma_start(acc[:], x_rows).then_inc(x1_loaded, 16)
            sp.dma_start(bo_bc[:], bo.rearrange("(o n) -> o n", o=1).broadcast_to([P, D])).then_inc(bo_loaded, 16)
            sp.dma_start(rw_raw[:], router_w.rearrange("(k p) e -> p k e", p=P)).then_inc(small_loaded, 16)
            sp.dma_start(rb_bc[:], router_b.rearrange("(o n) -> o n", o=1).broadcast_to([P, E])).then_inc(small_loaded, 16)
            sp.dma_start(b2_sb[:], b2).then_inc(small_loaded, 16)
            sp.dma_start(b1_sb[:], b1_t).then_inc(small_loaded, 16)

            def load_weights(e, g, slot):
                cols = slice(g * BANK, (g + 1) * BANK)
                w1_src = w1.rearrange("e (k p) h -> e p k h", p=P)
                w2_src = w2.rearrange("e (g j p) d -> e g p j d", p=P, j=4)
                if isinstance(e, int):
                    w1_src, w2_src = w1_src[e, :, :, cols], w2_src[e, g]
                else:
                    w1_src = w1_src[bass.ds(e, 1), :, :, cols].rearrange("o p k h -> (o p) k h")
                    w2_src = w2_src[bass.ds(e, 1), g].rearrange("o p j d -> (o p) j d")
                sp.dma_start(w_raw[slot][:, 0], w1_src).then_inc(w_loaded[slot], 16)
                sp.dma_start(w_raw[slot][:, 1], w2_src).then_inc(w_loaded[slot], 16)

            load_weights(0, 0, 0)
            load_weights(0, 1, 1)
            sp.wait_ge(table_ready, 1)
            blocks = sp.value_load(table[0:1, TABLE:TABLE + 1], min_val=1, max_val=MAX_BLOCKS)
            with sp.Fori(0, blocks) as b:
                expert = sp.value_load(table[0:1, bass.ds(b, 1)], min_val=0, max_val=E - 1)
                expert_next = sp.value_load(table[0:1, bass.ds(b + 1, 1)], min_val=0, max_val=E - 1)
                for g in range(HG):
                    sp.wait_ge(w1_split, 4 * (HG * b + g + 1))
                    sp.wait_ge(w2_split, 4 * (HG * b + g + 1))
                    load_weights(expert if g + 2 < HG else expert_next, (g + 2) % HG, g % 2)

            for i in range(2):
                sp.wait_ge(w_loaded[i], 32 * (HG // 2 * blocks + 1))
            sp.wait_ge(y_taken, TT * (blocks + 1))
            sp.dma_start(out_rows, acc[:]).then_inc(out_stored, 16)
            sp.wait_ge(out_stored, 16)

        @block.gpsimd
        def _(pool):
            nc.gpsimd.memset(ident[:], 0.0).then_inc(zeroed, 1)
            nc.gpsimd.memset(qbd_hi[:].bitcast(F32), 0.0).then_inc(zeroed, 1)
            nc.gpsimd.memset(qbd_lo[:].bitcast(F32), 0.0).then_inc(zeroed, 1)
            nc.gpsimd.memset(no_query[:], 0.0).then_inc(zeroed, 1)
            nc.gpsimd.memset(ctx_raw[(CHUNKS - 1) % 2][:, :, KEYS[-1]:KEYS_EVEN[-1]], 0.0).then_inc(zeroed, 1)
            pool.wait_ge(zeroed, 5)
            nc.gpsimd.affine_select(out=ident[:], in_=ident[:], compare_op=ALU.not_equal, fill=1.0, base=0,
                                    pattern=[[-1, P]], channel_multiplier=1).then_inc(ident_ready, 1)
            pool.wait_ge(wkv_loaded, 32)
            nc.gpsimd.tensor_copy(wk_hi[:], wkv_raw[:, 0]).then_inc(wkv_high, 1)
            nc.gpsimd.tensor_copy(wv_hi[:], wkv_raw[:, 1]).then_inc(wkv_high, 1)
            pool.wait_ge(wkv_high, 2)
            nc.gpsimd.tensor_tensor(wk_lo[:], wkv_raw[:, 0], wk_hi[:].bitcast(F32), ALU.subtract).then_inc(wkv_split, 1)
            nc.gpsimd.tensor_tensor(wv_lo[:], wkv_raw[:, 1], wv_hi[:].bitcast(F32), ALU.subtract).then_inc(wkv_split, 1)

            def split_ctx_low(job_plus_1, c):
                slot, n = c % 2, KEYS_EVEN[c]
                pool.wait_ge(ctx_high, job_plus_1)
                nc.gpsimd.tensor_tensor(ctx_lo[slot][:, :, 0:n], ctx_raw[slot][:, :, 0:n],
                                        ctx_hi[slot][:, :, 0:n].bitcast(F32), ALU.subtract).then_inc(ctx_split, 1)

            def place_queries(b, g):
                for half in range(2):
                    for h in range(HPG):
                        rows, cols = slice(HD * h, HD * (h + 1)), slice(NQ * h, NQ * (h + 1))
                        if half == 0:
                            last = nc.gpsimd.tensor_tensor(qbd_hi[rows, g, cols], q_stage[rows, g, :], no_query[rows, :],
                                                           ALU.add)
                        else:
                            last = nc.gpsimd.tensor_tensor(qbd_lo[rows, g, cols], q_stage[rows, g, :],
                                                           qbd_hi[rows, g, cols].bitcast(F32), ALU.subtract)
                    if half == 0:
                        last.then_inc(qbd_high, 1)
                        pool.wait_ge(qbd_high, GROUPS * b + g + 1)
                    else:
                        last.then_inc(qbd_ready, 1)
                        pool.wait_ge(qbd_ready, GROUPS * b + g + 1)

            for m in range(CHUNKS):
                split_ctx_low(m + 1, m)
            pool.wait_ge(q_loaded, 16)
            pool.wait_ge(ctx_split, CHUNKS)
            for g in range(GROUPS):
                place_queries(0, g)
            split_ctx_low(CHUNKS + 1, 0)

            def batch(b, last):
                for s in range(STEPS):
                    if not (last and s + 1 >= CHUNKS):
                        split_ctx_low(job_no(b, s + 1) + 1, (s + 1) % CHUNKS)
                    if s % 2 == 1 and not last:
                        pool.wait_ge(scores_ready, 2 * (STEPS * b + s + 1))
                        pool.wait_ge(ctx_split, job_no(b, s + 1) + 1)
                        if s == 1:
                            pool.wait_ge(q_loaded, 16 * (b + 2))
                        place_queries(b + 1, s // 2)

            with pool.Fori(0, B - 1) as b:
                batch(b, False)
            batch(B - 1, True)

            pool.wait_ge(small_loaded, 64)
            nc.gpsimd.iota(expert_no[:], pattern=[[1, E]], base=0, channel_multiplier=0,
                           allow_small_or_imprecise_dtypes=True).then_inc(numbers_ready, 1)
            nc.gpsimd.tensor_copy(rw_hi[:], rw_raw[:]).then_inc(rw_high, 1)
            pool.wait_ge(rw_high, 1)
            nc.gpsimd.tensor_tensor(rw_lo[:], rw_raw[:], rw_hi[:].bitcast(F32), ALU.subtract).then_inc(rw_split, 1)
            pool.wait_ge(wo_high, 1)
            nc.gpsimd.tensor_tensor(wo_lo[:], wo_raw[:], wo_hi[:].bitcast(F32), ALU.subtract).then_inc(wo_split, 1)

            nc.gpsimd.memset(ones[:], 1.0).then_inc(numbers_ready, 1)
            nc.gpsimd.iota(slot_no[:], pattern=[[1, BLOCK]], base=0, channel_multiplier=0,
                           allow_small_or_imprecise_dtypes=True).then_inc(numbers_ready, 1)
            nc.gpsimd.iota(block_no[:], pattern=[[1, TABLE]], base=0, channel_multiplier=0,
                           allow_small_or_imprecise_dtypes=True).then_inc(numbers_ready, 1)
            pool.wait_ge(numbers_ready, 4)
            nc.gpsimd.affine_select(out=before[:], in_=ones[:], compare_op=ALU.is_gt, fill=0.0, base=0,
                                    pattern=[[1, P]], channel_multiplier=-1).then_inc(numbers_ready, 1)

            def split_w1(n_plus_1, slot):
                for i in range(4):
                    pool.wait_ge(w1_high, 4 * n_plus_1 - 3 + i)
                    nc.gpsimd.tensor_tensor(w_lo[slot][:, 0, i, :], w_raw[slot][:, 0, i, :],
                                            w_hi[slot][:, 0, i, :].bitcast(F32), ALU.subtract).then_inc(w1_split, 1)

            split_w1(1, 0)
            pool.wait_ge(table_ready, 1)
            blocks = pool.value_load(table[0:1, TABLE:TABLE + 1], min_val=1, max_val=MAX_BLOCKS)
            with pool.Fori(0, blocks) as b:
                for g in range(HG):
                    split_w1(HG * b + g + 2, (g + 1) % 2)

        @block.scalar
        def _(act):
            act.wait_ge(wq_loaded, 16)
            nc.scalar.copy(wq_hi[:], wq_raw[:]).then_inc(wq_high, 1)
            act.wait_ge(var_ready, 1)
            nc.scalar.activation(sd[:], ve[:], ACT.Sqrt).then_inc(sd_ready, 1)
            for k in range(KD):
                act.wait_ge(xt_ready, k + 1)
                nc.scalar.copy(xt0_hi[:, k, :], ps[:, k, :]).then_inc(xt_high, 1)

            def proj_high_part(unit, n, bank):
                kind, a, c = unit
                act.wait_ge(proj_ready, n + 1)
                if kind == "keys":
                    m = KEYS_EVEN[c]
                    nc.scalar.activation(k_hi[:, a, KEY0[c]:KEY0[c] + m], ps[:, bank, 0:m], ACT.Identity,
                                         bias=bk_sb[:, a:a + 1]).then_inc(proj_high, 1)
                else:
                    r, w = rows_of(a), D // 2
                    nc.scalar.copy(v_hi[0:r, a, c * w:(c + 1) * w], ps[0:r, bank, 0:w]).then_inc(proj_high, 1)

            def job_high(b, s, ks):
                for k in ks:
                    n = UNIT0[s % CHUNKS] + k
                    bank = PROJ_BANK + (n % PROJ_BANKS)
                    proj_high_part(units_of(s if b is not None else CHUNKS + s)[k],
                                   unit_no(b, s, k) if b is not None else n, bank)

            act.wait_ge(bias_loaded, 48)
            for c in range(CHUNKS):
                job_high(None, c, range(UNITS[c]))

            def batch(b, last):
                for s in range(STEPS):
                    act.wait_ge(negmax_ready, STEPS * b + s + 1)
                    w = KEY0[FULL]
                    nc.scalar.activation(probs[:, 0:w].rearrange("p (c k) -> p c k", c=FULL),
                                         ps[:, SCORE_BANK:SCORE_BANK + FULL, 0:KEYS[0]], ACT.Exp,
                                         bias=negmax[:, 0:1], accum_out=rowsum[:, 0:1])
                    nc.scalar.activation(probs[:, w:NK], ps[:, SCORE_BANK + FULL, 0:KEYS[FULL]], ACT.Exp,
                                         bias=negmax[:, 0:1], accum_out=rowsum[:, 1:2]).then_inc(exp_done, 1)
                    has_job = not (last and s >= CHUNKS)
                    u = UNITS[s % CHUNKS]
                    if has_job:
                        job_high(b, s, range(u - 1))
                    for c in range(CHUNKS):
                        act.wait_ge(pt_ready, CHUNKS * (STEPS * b + s) + c + 1)
                        n = CHUNK_TILES[c]
                        nc.scalar.copy(pt_hi[:, TILE0[c]:TILE0[c] + n, s % 2, :],
                                       ps[:, SCORE_BANK + c, 0:n * P].rearrange("p (t r) -> p t r", t=n)
                                       ).then_inc(pt_high, 1)
                    if has_job:
                        job_high(b, s, [u - 1])

            with act.Fori(0, B - 1) as b:
                batch(b, False)
            batch(B - 1, True)

            act.wait_ge(ot_loaded, 16)
            nc.scalar.copy(ot_hi[:], ot_raw[:]).then_inc(ot_high, 1)
            act.wait_ge(wo_loaded, 16)
            nc.scalar.copy(wo_hi[:], wo_raw[:]).then_inc(wo_high, 1)

            def wait_slot(eng, b, g, i):
                if i == 0:
                    eng.wait_ge(w_loaded[(g + 1) % 2], 32 * (HG // 2 * b + (g + 1) // 2 + 1))
                    if g > 0:
                        eng.wait_ge(w_used, (HG - 1) * b + g)
                    else:
                        eng.wait_ge(gather_ready, KD * (b + 1))

            def split_w1_high(slot, i):
                nc.scalar.copy(w_hi[slot][:, 0, i, :], w_raw[slot][:, 0, i, :]).then_inc(w1_high, 1)

            act.wait_ge(w_loaded[0], 32)
            for i in range(4):
                split_w1_high(0, i)
            act.wait_ge(var_ready, 2)
            nc.scalar.activation(sd[:], ve[:], ACT.Sqrt).then_inc(sd_ready, 1)
            for k in range(KD):
                act.wait_ge(xt_ready, KD + k + 1)
                nc.scalar.copy(xt_hi[:, k, :], ps[:, 4 + k, :]).then_inc(xt_high, 1)
            act.wait_ge(negtop_ready, 1)
            for t in range(TT):
                last = nc.scalar.activation(eg[:, t, :], logits[:, t, :], ACT.Exp, bias=negtop[:, t:t + 1])
            last.then_inc(eg_ready, 1)

            nc.scalar.copy(xn_hi[:], xn[:]).then_inc(xn_high, 1)
            act.wait_ge(table_ready, 1)
            blocks = act.value_load(table[0:1, TABLE:TABLE + 1], min_val=1, max_val=MAX_BLOCKS)

            def gathered_high(b):
                for k in range(KD):
                    act.wait_ge(gather_ready, KD * b + k + 1)
                    nc.scalar.copy(xg_hi[:, k, :], ps[:, 4 + k, 0:BLOCK]).then_inc(xg_high, 1)

            gathered_high(0)
            with act.Fori(0, blocks) as b:
                act.wait_ge(b1_set, b + 1)
                for c in range(HT):
                    g, i = c // 4, c % 4
                    act.wait_ge(h_ready, HT * b + c + 1)
                    nc.scalar.activation(h_f32[c % 2][:], ps[:, 2 + c % 2, 0:BLOCK], ACT.Relu, bias=b1_cur[:, 0, c:c + 1])
                    nc.scalar.activation(h_hi[c % 2][:], ps[:, 2 + c % 2, 0:BLOCK], ACT.Relu,
                                         bias=b1_cur[:, 0, c:c + 1]).then_inc(h_high, 1)
                    wait_slot(act, b, g, i)
                    split_w1_high((g + 1) % 2, i)
                    if c == 0:
                        act.wait_ge(sel_turned, BT * b + 1)
                        nc.scalar.copy(sel_t[:, 0, :], ps[:, 6, :]).then_inc(sel_t_taken[0], 1)
                for t in range(BT):
                    act.wait_ge(y_ready, BT * b + t + 1)
                    nc.scalar.copy(y_hi[:, t, :], ps[:, t, :]).then_inc(y_high, 1)
                gathered_high(b + 1)

        @block.vector
        def _(dve):
            steps = [0]

            def step(ins):
                steps[0] += 1
                ins.then_inc(vector_step, 1)
                dve.wait_ge(vector_step, steps[0])

            def layernorm(src, dst, n):
                for t in range(TT):
                    last = nc.vector.bn_stats(stat[:, t, :], src[:, t, :])
                step(last)
                for t in range(TT):
                    last = nc.vector.bn_aggr(mv[:, t, :], stat[:, t, :])
                step(last)
                nc.vector.tensor_scalar(ve[:], mv[:, :, 1], LN_EPS, None, ALU.add).then_inc(var_ready, 1)
                dve.wait_ge(sd_ready, n)
                step(nc.vector.reciprocal(rs0[:], sd[:]))
                step(nc.vector.tensor_tensor(sq[:], ve[:], rs0[:], ALU.mult))
                step(nc.vector.tensor_tensor(sdn[:], sd[:], sq[:], ALU.add))
                step(nc.vector.tensor_scalar(sq[:], sdn[:], 0.5, None, ALU.mult))
                step(nc.vector.reciprocal(rstd[:], sq[:]))
                for t in range(TT):
                    nc.vector.tensor_scalar(dst[:, t, :], src[:, t, :], mv[:, t, 0:1], rstd[:, t:t + 1],
                                            ALU.subtract, ALU.mult).then_inc(xn_ready, 1)

            nc.vector.memset(ps[:, SCORE_BANK + CHUNKS - 1, :], 0.0).then_inc(psum_zeroed, 1)
            dve.wait_ge(x_loaded, 16)
            layernorm(x0, xn0, 1)
            dve.wait_ge(wq_high, 1)
            nc.vector.tensor_tensor(wq_lo[:], wq_raw[:], wq_hi[:].bitcast(F32), ALU.subtract).then_inc(wq_split, 1)
            for k in range(KD):
                dve.wait_ge(xt_high, k + 1)
                nc.vector.tensor_tensor(xt0_lo[:, k, :], ps[:, k, :], xt0_hi[:, k, :].bitcast(F32),
                                        ALU.subtract).then_inc(xt_split, 1)
            dve.wait_ge(bias_loaded, 48)
            for m in range(KD):
                dve.wait_ge(q_ready, m + 1)
                nc.vector.tensor_scalar(q_out[:, m, :], ps[:, 4 + m, :], bq_sb[:, m:m + 1], SCALE,
                                        ALU.add, ALU.mult).then_inc(q_done if m < KD - 1 else pv_taken, 1)

            def proj_low_part(unit, n, bank):
                kind, a, c = unit
                dve.wait_ge(proj_high, n + 1)
                if kind == "keys":
                    m = KEYS_EVEN[c]
                    cols = slice(KEY0[c], KEY0[c] + m)
                    nc.vector.scalar_tensor_tensor(out=k_lo[:, a, cols], in0=ps[:, bank, 0:m], scalar=bk_sb[:, a:a + 1],
                                                   in1=k_hi[:, a, cols].bitcast(F32), op0=ALU.add,
                                                   op1=ALU.subtract).then_inc(proj_split, 1)
                else:
                    r, w = rows_of(a), D // 2
                    cols = slice(c * w, (c + 1) * w)
                    nc.vector.tensor_tensor(v_lo[0:r, a, cols], ps[0:r, bank, 0:w], v_hi[0:r, a, cols].bitcast(F32),
                                            ALU.subtract).then_inc(proj_split, 1)

            def job_low(b, s, ks):
                for k in ks:
                    n = UNIT0[s % CHUNKS] + k
                    bank = PROJ_BANK + (n % PROJ_BANKS)
                    proj_low_part(units_of(s if b is not None else CHUNKS + s)[k],
                                  unit_no(b, s, k) if b is not None else n, bank)

            def take_context(b, g):
                dve.wait_ge(pv_ready, GROUPS * b + g + 1)
                slot = g % 2
                dve.wait_ge(stored[slot], 16 * (2 * b + g // 2 + 1))
                for h in range(HPG):
                    rows = slice(HD * h, HD * (h + 1))
                    last = nc.vector.tensor_scalar(o_stage[slot][rows, :], ps[rows, PV_BANK, NQ * h:NQ * (h + 1)],
                                                   bv_sb[rows, g:g + 1], None, ALU.add)
                last.then_inc(pv_taken, 1)

            def ctx_high_part(c, loaded, free=None):
                slot, n = c % 2, KEYS_EVEN[c]
                dve.wait_ge(ctx_loaded[slot], loaded)
                if free is not None:
                    dve.wait_ge(proj_ready, free)
                nc.vector.tensor_copy(ctx_hi[slot][:, :, 0:n], ctx_raw[slot][:, :, 0:n]).then_inc(ctx_high, 1)

            dve.wait_ge(zeroed, 5)
            ctx_high_part(0, 16)
            ctx_high_part(1, 16)
            for c in range(CHUNKS):
                if c >= 1:
                    ctx_high_part((c + 1) % CHUNKS, 16 * ((c + 1) // 2 + 1), UNIT0[c])
                job_low(None, c, range(UNITS[c]))

            def batch(b, last, first_batch=False):
                for s in range(STEPS):
                    n = STEPS * b + s
                    dve.wait_ge(scores_ready, 2 * n + 1)
                    nc.vector.tensor_reduce(mx[:, 0:1], ps[:, SCORE_BANK:SCORE_BANK + FULL, 0:KEYS[0]], AX.XY,
                                            ALU.max)
                    dve.wait_ge(scores_ready, 2 * n + 2)
                    nc.vector.tensor_reduce(mx[:, 1:2], ps[:, SCORE_BANK + FULL, 0:KEYS[FULL]], AX.X,
                                            ALU.max).then_inc(part_max, 1)
                    dve.wait_ge(part_max, n + 1)
                    nc.vector.tensor_reduce(negmax[:], mx[:], AX.X, ALU.max, negate=True).then_inc(negmax_ready, 1)
                    if not (last and s + 1 >= CHUNKS):
                        ctx_high_part((s + 1) % CHUNKS, 16 * (CHUNKS // 2 + 1 + (STEPS // 2) * b + (s + 1) // 2),
                                      unit_no(b, s, 0))
                    if s % 2 == 0 and s >= 2:
                        take_context(b, s // 2 - 1)
                    dve.wait_ge(exp_done, n + 1)
                    nc.vector.tensor_reduce(total[:], rowsum[:], AX.X, ALU.add).then_inc(total_ready, 1)
                    dve.wait_ge(total_ready, n + 1)
                    nc.vector.reciprocal(rinv[:], total[:]).then_inc(rinv_ready, 1)
                    dve.wait_ge(rinv_ready, n + 1)
                    for c in range(CHUNKS):
                        part = probs[:, KEY0[c]:KEY0[c] + KEYS[c]]
                        nc.vector.tensor_scalar(part, part, rinv[:, 0:1], None, ALU.mult).then_inc(norm_ready, 1)
                    has_job = not (last and s >= CHUNKS)
                    u = UNITS[s % CHUNKS]
                    if has_job:
                        job_low(b, s, range(u - 1))
                    for c in range(CHUNKS):
                        dve.wait_ge(pt_high, CHUNKS * n + c + 1)
                        m = CHUNK_TILES[c]
                        nc.vector.tensor_tensor(pt_lo[:, TILE0[c]:TILE0[c] + m, s % 2, :],
                                                ps[:, SCORE_BANK + c, 0:m * P].rearrange("p (t r) -> p t r", t=m),
                                                pt_hi[:, TILE0[c]:TILE0[c] + m, s % 2, :].bitcast(F32),
                                                ALU.subtract).then_inc(pt_split, 1)
                    if has_job:
                        job_low(b, s, [u - 1])
                take_context(b, GROUPS - 1)

            with dve.Fori(0, B - 1) as b:
                batch(b, False)
            batch(B - 1, True)

            dve.wait_ge(ot_high, 1)
            nc.vector.tensor_tensor(ot_lo[:], ot_raw[:], ot_hi[:].bitcast(F32), ALU.subtract).then_inc(ot_split, 1)
            dve.wait_ge(x1_loaded, 16)
            dve.wait_ge(bo_loaded, 16)
            for t in range(TT):
                last = nc.vector.tensor_tensor(acc[:, t, :], acc[:, t, :], bo_bc[:], ALU.add)
            step(last)
            for t in range(TT):
                dve.wait_ge(x1_product, t + 1)
                last = nc.vector.tensor_tensor(acc[:, t, :], ps[:, t, :], acc[:, t, :], ALU.add)
            step(last)
            layernorm(acc, xn, 2)
            for k in range(KD):
                dve.wait_ge(xt_high, KD + k + 1)
                nc.vector.tensor_tensor(xt_lo[:, k, :], ps[:, 4 + k, :], xt_hi[:, k, :].bitcast(F32),
                                        ALU.subtract).then_inc(xt_split, 1)
            dve.wait_ge(small_loaded, 64)
            dve.wait_ge(numbers_ready, 1)
            dve.wait_ge(logits_product, 1)
            for t in range(TT):
                last = nc.vector.tensor_tensor(logits[:, t, :], ps[:, 0, t * E:(t + 1) * E], rb_bc[:], ALU.add)
            step(last)
            for t in range(TT):
                last = nc.vector.max(top[:, t, :], logits[:, t, :])
            step(last)
            nc.vector.tensor_scalar(negtop[:], top[:, :, 0], -1.0, None, ALU.mult).then_inc(negtop_ready, 1)
            for t in range(TT):
                last = nc.vector.max_index(top_at[:, t, :], top[:, t, :], logits[:, t, :])
            step(last)
            step(nc.vector.tensor_copy(top_atf[:], top_at[:]))
            for t in range(TT):
                last = nc.vector.tensor_scalar(is_first[:, t, :], expert_no[:], top_atf[:, t, 0:1], None, ALU.is_equal)
            step(last)
            for t in range(TT):
                last = nc.vector.scalar_tensor_tensor(out=keep[:, t, :], in0=expert_no[:], scalar=top_atf[:, t, 1:2],
                                                      in1=is_first[:, t, :], op0=ALU.is_equal, op1=ALU.add)
            step(last)
            dve.wait_ge(eg_ready, 1)
            step(nc.vector.tensor_tensor(egk[:], eg[:], keep[:], ALU.mult))
            step(nc.vector.tensor_reduce(gsum[:], egk[:], AX.X, ALU.add))
            step(nc.vector.reciprocal(ginv[:], gsum[:]))
            for t in range(TT):
                last = nc.vector.tensor_scalar(gates[:, t, :], egk[:, t, :], ginv[:, t:t + 1], None, ALU.mult)
            last.then_inc(gates_ready, 1)
            dve.wait_ge(gates_ready, 1)
            step(nc.vector.tensor_copy(gates_e[:], gates[:].rearrange("p t e -> p e t")))

            dve.wait_ge(counts_product, 2)
            nc.vector.memset(seen[:, 0, :], 0.0)
            nc.vector.tensor_copy(in_tile[:], ps[:, 3, TT * E:2 * TT * E].rearrange("p (t e) -> p t e", t=TT))
            for i in range(3):
                nc.vector.memset(sums[i][:, 0:PAD], 0.0)
            step(nc.vector.tensor_scalar(rank1[:], ps[:, 3, 0:TT * E].rearrange("p (t e) -> p t e", t=TT), 1.0, None,
                                         ALU.add))
            for t in range(TT):
                step(nc.vector.tensor_tensor(seen[:, t + 1, :], seen[:, t, :], in_tile[:, t, :], ALU.add))
            step(nc.vector.tensor_tensor(rankk[:], rank1[:], seen[:, 0:TT, :], ALU.add))
            step(nc.vector.tensor_tensor(rank1[:], rankk[:], keep[:], ALU.mult))
            nc.vector.tensor_scalar(rank_e[:], rank1[:].rearrange("p t e -> p e t"), 1.0, None, ALU.subtract)
            count = seen[:, TT, :]
            step(nc.vector.tensor_scalar(some[:], count, 0.0, None, ALU.is_gt))
            step(nc.vector.memset(some[:, 0:1], 1.0))
            step(nc.vector.scalar_tensor_tensor(out=sums[0][:, PAD:], in0=count, scalar=float(BLOCK), in1=some[:],
                                                op0=ALU.is_gt, op1=ALU.add))
            for i in range(3):
                d = 1 << i
                step(nc.vector.tensor_tensor(sums[i + 1][:, PAD:], sums[i][:, PAD:], sums[i][:, PAD - d:PAD - d + E],
                                             ALU.add))
            blocks_to = sums[3][:, PAD:].rearrange("p (o e) -> p o e", o=1).broadcast_to([P, TABLE, E])
            blocks_of = sums[0][:, PAD:].rearrange("p (o e) -> p o e", o=1).broadcast_to([P, TABLE, E])
            numbers = block_no[:].rearrange("p (b o) -> p b o", o=1).broadcast_to([P, TABLE, E])
            step(nc.vector.tensor_tensor(past[:], blocks_to, numbers, ALU.is_le))
            nc.vector.tensor_tensor(past_n[:], past[:], blocks_of, ALU.mult)
            step(nc.vector.tensor_reduce(owner[:], past[:], AX.X, ALU.add))
            nc.vector.tensor_scalar(table_f[:, 0:TABLE], owner[:], float(E - 1), None, ALU.min)
            step(nc.vector.tensor_copy(table_f[:, TABLE:TABLE + 1], sums[3][:, PAD + E - 1:PAD + E]))
            nc.vector.tensor_copy(table[:], table_f[:]).then_inc(table_ready, 1)
            step(nc.vector.tensor_reduce(start[:], past_n[:], AX.X, ALU.add))
            step(nc.vector.tensor_tensor(start2[:], block_no[:], start[:], ALU.subtract))
            step(nc.vector.tensor_scalar(base[:], start2[:], float(BLOCK), None, ALU.mult))

            dve.wait_ge(gates_turned, 1)
            nc.vector.tensor_copy(gates_t[:], ps[0:E, 1, :]).then_inc(gates_t_ready, 1)

            def select(b, expert):
                if isinstance(b, int):
                    ranks, first_rank = rank_e[:, expert:expert + 1, :], base[:, b:b + 1]
                else:
                    ranks, first_rank = rank_e[:, bass.ds(expert, 1), :], base[:, bass.ds(b, 1)]
                nc.vector.tensor_scalar(key_cur[:], ranks, first_rank, None, ALU.subtract).then_inc(key_set, 1)
                dve.wait_ge(key_set, b + 1)
                for t in range(TT):
                    last = nc.vector.tensor_scalar(sel[:, t, :], slot_no[:], key_cur[:, 0, t:t + 1], None, ALU.is_equal)
                last.then_inc(sel_ready, 1)

            def gathered_low(b):
                for k in range(KD):
                    dve.wait_ge(xg_high, KD * b + k + 1)
                    nc.vector.tensor_copy(xg_lo[:, k, :], ps[:, 4 + k, BLOCK:2 * BLOCK]).then_inc(xg_low, 1)

            dve.wait_ge(xn_high, 1)
            nc.vector.tensor_tensor(xn_lo[:], xn[:], xn_hi[:].bitcast(F32), ALU.subtract).then_inc(xn_split, 1)
            select(0, 0)
            for t in range(TT):
                dve.wait_ge(b2_product, t + 1)
                nc.vector.tensor_tensor(acc[:, t, :], ps[:, 4 + t, :], acc[:, t, :], ALU.add).then_inc(y_taken, 1)
            dve.wait_ge(w_loaded[0], 32)
            for i in range(4):
                nc.vector.tensor_copy(w_hi[0][:, 1, i, :], w_raw[0][:, 1, i, :]).then_inc(w2_high, 1)
            for i in range(4):
                dve.wait_ge(w2_high, i + 1)
                nc.vector.tensor_tensor(w_lo[0][:, 1, i, :], w_raw[0][:, 1, i, :], w_hi[0][:, 1, i, :].bitcast(F32),
                                        ALU.subtract).then_inc(w2_split, 1)
            gathered_low(0)
            dve.wait_ge(table_ready, 1)
            blocks = dve.value_load(table[0:1, TABLE:TABLE + 1], min_val=1, max_val=MAX_BLOCKS)

            with dve.Fori(0, blocks) as b:
                expert = dve.value_load(table[0:1, bass.ds(b, 1)], min_val=0, max_val=E - 1)
                nc.vector.tensor_copy(b1_cur[:], b1_sb[:, bass.ds(expert, 1), :]).then_inc(b1_set, 1)
                dve.wait_ge(y_taken, TT * (b + 1))
                nc.vector.tensor_copy(gate_cur[:], gates_e[:, bass.ds(expert, 1), :]).then_inc(gate_set, 1)
                for c in range(HT):
                    g, i = c // 4, c % 4
                    slot = (g + 1) % 2
                    dve.wait_ge(h_high, HT * b + c + 1)
                    nc.vector.tensor_tensor(h_lo[c % 2][:], h_f32[c % 2][:], h_hi[c % 2][:].bitcast(F32),
                                            ALU.subtract).then_inc(h_split, 1)
                    if i == 0:
                        dve.wait_ge(w_loaded[slot], 32 * (HG // 2 * b + (g + 1) // 2 + 1))
                        if g > 0:
                            dve.wait_ge(w_used, (HG - 1) * b + g)
                    nc.vector.tensor_copy(w_hi[slot][:, 1, i, :], w_raw[slot][:, 1, i, :]).then_inc(w2_high, 1)
                    if c == 1:
                        dve.wait_ge(sel_turned, BT * b + 2)
                        nc.vector.tensor_copy(sel_t[:, 1, :], ps[:, 7, :]).then_inc(sel_t_taken[1], 1)
                    if c == HT // 2:
                        expert_next = dve.value_load(table[0:1, bass.ds(b + 1, 1)], min_val=0, max_val=E - 1)
                        select(b + 1, expert_next)
                    dve.wait_ge(w2_high, 4 * (HG * b + g + 1) + i + 1)
                    nc.vector.tensor_tensor(w_lo[slot][:, 1, i, :], w_raw[slot][:, 1, i, :],
                                            w_hi[slot][:, 1, i, :].bitcast(F32), ALU.subtract).then_inc(w2_split, 1)
                for t in range(BT):
                    dve.wait_ge(y_high, BT * b + t + 1)
                    nc.vector.tensor_tensor(y_lo[:, t, :], ps[:, t, :], y_hi[:, t, :].bitcast(F32),
                                            ALU.subtract).then_inc(y_split, 1)
                gathered_low(b + 1)
                dve.wait_ge(gate_set, b + 1)
                for t in range(TT):
                    dve.wait_ge(scatter_ready, TT * b + t + 1)
                    bank = t if t < 2 else 2 + t
                    nc.vector.scalar_tensor_tensor(out=acc[:, t, :], in0=ps[:, bank, :], scalar=gate_cur[:, 0, t:t + 1],
                                                   in1=acc[:, t, :], op0=ALU.mult, op1=ALU.add).then_inc(y_taken, 1)

        @block.tensor
        def _(pe):
            def turn(src, bank0, n):
                pe.wait_ge(xn_ready, n)
                for k in range(KD):
                    for t in range(TT):
                        last = pe.transpose(ps[:, bank0 + k, t * P:(t + 1) * P], src[:, t, k * P:(k + 1) * P], ident[:])
                    last.then_inc(xt_ready, 1)

            pe.wait_ge(ident_ready, 1)
            pe.wait_ge(psum_zeroed, 1)
            turn(xn0, 0, TT)
            pe.wait_ge(wq_split, 1)
            pe.wait_ge(xt_split, KD)
            for m in range(KD):
                for k in range(KD):
                    last = three_pass(pe, ps[:, 4 + m, :], wq_hi[:, k, m * P:(m + 1) * P], wq_lo[:, k, m * P:(m + 1) * P],
                                      xt0_hi[:, k, :], xt0_lo[:, k, :], k == 0, k == KD - 1)
                last.then_inc(q_ready, 1)

            def project(unit, n, bank):
                kind, a, c = unit
                for k in range(KC):
                    if kind == "keys":
                        slot, m, cols = c % 2, KEYS_EVEN[c], slice(a * P, (a + 1) * P)
                        last = three_pass(pe, ps[:, bank, 0:m], wk_hi[:, k, cols], wk_lo[:, k, cols],
                                          ctx_hi[slot][:, k, 0:m], ctx_lo[slot][:, k, 0:m], k == 0, k == KC - 1)
                    else:
                        chunk = max(i for i in range(CHUNKS) if TILE0[i] <= a)
                        slot, r, w = chunk % 2, rows_of(a), D // 2
                        keys = slice((a - TILE0[chunk]) * P, (a - TILE0[chunk]) * P + r)
                        cols = slice(c * w, (c + 1) * w)
                        last = three_pass(pe, ps[0:r, bank, 0:w], ctx_hi[slot][:, k, keys], ctx_lo[slot][:, k, keys],
                                          wv_hi[:, k, cols], wv_lo[:, k, cols], k == 0, k == KC - 1)
                last.then_inc(proj_ready, 1)

            def run_job(b, s, ks):
                for k in ks:
                    local = UNIT0[s % CHUNKS] + k
                    n = unit_no(b, s, k) if b is not None else local
                    if k == 0:
                        pe.wait_ge(ctx_split, job_no(b, s) + 1 if b is not None else s + 1)
                    if b is not None or local >= PROJ_BANKS:
                        pe.wait_ge(proj_split, n - PROJ_BANKS + 1)
                    project(units_of(s if b is not None else CHUNKS + s)[k], n, PROJ_BANK + local % PROJ_BANKS)

            pe.wait_ge(wkv_split, 2)
            pe.wait_ge(q_done, KD - 1)
            for c in range(CHUNKS):
                run_job(None, c, range(UNITS[c]))

            def context(b, g):
                pe.wait_ge(proj_split, value_units_done(b, g))
                pe.wait_ge(pv_taken, GROUPS * b + g + 1)
                for t in range(KT):
                    r, cols = rows_of(t), slice(g * P, (g + 1) * P)
                    last = three_pass(pe, ps[:, PV_BANK, 0:HPG * NQ], v_hi[0:r, t, cols], v_lo[0:r, t, cols],
                                      pt_hi[0:r, t, :, :], pt_lo[0:r, t, :, :], t == 0, t == KT - 1)
                last.then_inc(pv_ready, 1)

            def batch(b, last_batch):
                for s in range(STEPS):
                    g, n = s // 2, STEPS * b + s
                    if s % 2 == 0:
                        pe.wait_ge(qbd_ready, GROUPS * b + g + 1)
                        pe.wait_ge(proj_split, key_units_done(b, g))
                    rows = slice((s % 2) * P, (s % 2 + 1) * P)
                    for c in range(CHUNKS):
                        if s > 0:
                            pe.wait_ge(pt_split, CHUNKS * (n - 1) + c + 1)
                        m = KEYS_EVEN[c]
                        cols = slice(KEY0[c], KEY0[c] + m)
                        last = three_pass(pe, ps[:, SCORE_BANK + c, 0:m], qbd_hi[:, g, rows], qbd_lo[:, g, rows],
                                          k_hi[:, g, cols], k_lo[:, g, cols], True, True)
                        if c >= FULL - 1:
                            last.then_inc(scores_ready, 1)
                    if s % 2 == 0 and s >= 2:
                        context(b, g - 1)
                    has_job = not (last_batch and s >= CHUNKS)
                    u = UNITS[s % CHUNKS]
                    if has_job:
                        run_job(b, s, range(u - 1))
                    for c in range(CHUNKS):
                        pe.wait_ge(norm_ready, CHUNKS * n + c + 1)
                        for i in range(CHUNK_TILES[c]):
                            r = rows_of(TILE0[c] + i)
                            key = KEY0[c] + i * P
                            last = pe.transpose(ps[0:r, SCORE_BANK + c, i * P:(i + 1) * P], probs[:, key:key + r], ident[:])
                        last.then_inc(pt_ready, 1)
                    if has_job:
                        run_job(b, s, [u - 1])
                pe.wait_ge(pt_split, CHUNKS * STEPS * (b + 1))
                context(b, GROUPS - 1)

            with pe.Fori(0, B - 1) as b:
                batch(b, False)
            batch(B - 1, True)

            pe.wait_ge(ot_split, 1)
            pe.wait_ge(wo_split, 1)
            for t in range(TT):
                for k in range(KD):
                    rows = slice(t * P, (t + 1) * P)
                    last = three_pass(pe, ps[:, t, :], ot_hi[:, k, rows], ot_lo[:, k, rows], wo_hi[:, k, :], wo_lo[:, k, :],
                                      k == 0, k == KD - 1)
                last.then_inc(x1_product, 1)
            turn(xn, 4, 2 * TT)
            pe.wait_ge(xt_split, 2 * KD)
            pe.wait_ge(rw_split, 1)
            for t in range(TT):
                for k in range(KD):
                    rows = slice(t * P, (t + 1) * P)
                    last = three_pass(pe, ps[:, 0, t * E:(t + 1) * E], xt_hi[:, k, rows], xt_lo[:, k, rows],
                                      rw_hi[:, k, :], rw_lo[:, k, :], k == 0, k == KD - 1)
            last.then_inc(logits_product, 1)
            pe.wait_ge(gates_ready, 1)
            pe.wait_ge(numbers_ready, 5)
            for i, m in enumerate([before, ones]):
                pe.matmul(ps[:, 3, i * TT * E:(i + 1) * TT * E], m[:], keep[:].rearrange("p t e -> p (t e)"), start=True,
                          stop=True).then_inc(counts_product, 1)
            for t in range(TT):
                last = pe.transpose(ps[0:E, 1, t * P:(t + 1) * P], gates[:, t, :], ident[:])
            last.then_inc(gates_turned, 1)
            pe.wait_ge(gates_t_ready, 1)
            for t in range(TT):
                pe.matmul(ps[:, 4 + t, :], gates_t[:, t * P:(t + 1) * P], b2_sb[:], start=True,
                          stop=True).then_inc(b2_product, 1)

            def gather(b):
                pe.wait_ge(sel_ready, b + 1)
                for k in range(KD):
                    for i, part in enumerate([xn_hi, xn_lo]):
                        for t in range(TT):
                            last = pe.matmul(ps[:, 4 + k, i * BLOCK:(i + 1) * BLOCK], part[:, t, k * P:(k + 1) * P],
                                             sel[:, t, :], start=(t == 0), stop=(t == TT - 1))
                    last.then_inc(gather_ready, 1)

            def hidden(b, c):
                g, i = c // 4, c % 4
                if i == 0:
                    pe.wait_ge(w1_split, 4 * (HG * b + g + 1))
                    pe.wait_ge(w2_split, 4 * (HG * b + g + 1))
                if c >= 2:
                    pe.wait_ge(h_split, HT * b + c - 1)
                cols = slice(i * P, (i + 1) * P)
                for k in range(KD):
                    if c == 0:
                        pe.wait_ge(xg_low, KD * b + k + 1)
                    last = three_pass(pe, ps[:, 2 + c % 2, 0:BLOCK], w_hi[g % 2][:, 0, k, cols], w_lo[g % 2][:, 0, k, cols],
                                      xg_hi[:, k, :], xg_lo[:, k, :], k == 0, k == KD - 1)
                last.then_inc(h_ready, 1)

            def outputs(b, c):
                g, i = c // 4, c % 4
                pe.wait_ge(h_split, HT * b + c + 1)
                if c == 0:
                    pe.wait_ge(y_taken, TT * (b + 1))
                for t in range(BT):
                    rows = slice(t * P, (t + 1) * P)
                    last = three_pass(pe, ps[:, t, :], h_hi[c % 2][:, rows], h_lo[c % 2][:, rows],
                                      w_hi[g % 2][:, 1, i, :], w_lo[g % 2][:, 1, i, :], c == 0, c == HT - 1)
                    if c == HT - 1:
                        last.then_inc(y_ready, 1)
                if i == 3 and c < HT - 1:
                    last.then_inc(w_used, 1)

            def scatter(b):
                for t in range(TT):
                    bank = t if t < 2 else 2 + t
                    if t == 0:
                        pe.wait_ge(y_split, BT * (b + 1))
                    if t == 2:
                        pe.wait_ge(xg_low, KD * (b + 1) + 2)
                    rows = slice(t * P, (t + 1) * P)
                    for u in range(BT):
                        pe.matmul(ps[:, bank, :], sel_t[:, u, rows], y_hi[:, u, :], start=(u == 0), stop=False)
                        last = pe.matmul(ps[:, bank, :], sel_t[:, u, rows], y_lo[:, u, :], start=False, stop=(u == BT - 1))
                    last.then_inc(scatter_ready, 1)

            pe.wait_ge(xn_split, 1)
            pe.wait_ge(y_taken, TT)
            gather(0)
            pe.wait_ge(table_ready, 1)
            blocks = pe.value_load(table[0:1, TABLE:TABLE + 1], min_val=1, max_val=MAX_BLOCKS)
            with pe.Fori(0, blocks) as b:
                hidden(b, 0)
                for u in range(BT):
                    for t in range(TT):
                        last = pe.transpose(ps[:, 6 + u, t * P:(t + 1) * P], sel[:, t, u * P:(u + 1) * P].bitcast(F32),
                                            ident[:])
                    last.then_inc(sel_turned, 1)
                for c in range(1, HT):
                    hidden(b, c)
                    outputs(b, c - 1)
                outputs(b, HT - 1)
                for i in range(BT):
                    pe.wait_ge(sel_t_taken[i], b + 1)
                gather(b + 1)
                scatter(b)


_INS = ["x", "ctx_t", "wq", "bq_t", "wk", "bk_t", "wv", "bv_t", "wo", "bo", "router_w", "router_b",
        "w1", "b1_t", "w2", "b2"]


def kernel(**inputs):
    import numpy as _np
    import concourse.bacc as _bacc
    from concourse import mybir as _mybir
    from concourse.bass_utils import run_bass_kernel_spmd as _run

    a = {k: _np.asarray(v) for k, v in inputs.items()}

    def columns(v):
        return v.reshape(-1, 128).T

    laid = {
        "x": a["x"],
        "ctx_t": a["ctx_768"].transpose(0, 2, 1),
        "wq": a["L0_xattn_Wq"], "bq_t": columns(a["L0_xattn_bq"]),
        "wk": a["L0_xattn_Wk"], "bk_t": columns(a["L0_xattn_bk"]),
        "wv": a["L0_xattn_Wv"], "bv_t": columns(a["L0_xattn_bv"]),
        "wo": a["L0_xattn_Wo"], "bo": a["L0_xattn_bo"],
        "router_w": a["L0_ffn_router_w"], "router_b": a["L0_ffn_router_b"],
        "w1": a["L0_ffn_w1"],
        "b1_t": a["L0_ffn_b1"].reshape(8, 16, 128).transpose(2, 0, 1),
        "w2": a["L0_ffn_w2"], "b2": a["L0_ffn_b2"],
    }
    nc = _bacc.Bacc("TRN2", target_bir_lowering=False, num_devices=1)
    arrays, args = {}, []
    for name in _INS:
        v = _np.ascontiguousarray(laid[name])
        arrays[f"in_{name}_dram"] = v
        args.append(nc.dram_tensor(f"in_{name}_dram", v.shape, _mybir.dt.from_np(v.dtype), kind="ExternalInput").ap())
    args.append(nc.dram_tensor("out_0_dram", a["x"].shape, _mybir.dt.float32, kind="ExternalOutput").ap())
    bass_perceiver_layer_kernel(nc, *args)
    r = _run(nc, [arrays], core_ids=[0])
    return r.results[0]["out_0_dram"]
```

```python
from contextlib import ExitStack

import concourse.bass as bass
from concourse import mybir

ALU = mybir.AluOpType
ACT = mybir.ActivationFunctionType
AX = mybir.AxisListType
F32 = mybir.dt.float32
F32R = mybir.dt.float32r
U32 = mybir.dt.uint32
I32 = mybir.dt.int32

P = 128
BANK = 512
LN_EPS = 1e-5


def bass_perceiver_layer_kernel(nc, x, ctx_t, wq, bq_t, wk, bk_t, wv, bv_t, wo, bo, router_w, router_b,
                                w1, b1_t, w2, b2, out):
    B, NQ, D = x.shape
    DC, NK = ctx_t.shape[1:]
    T = B * NQ
    TT = T // P
    KD = D // P
    KC = DC // P
    HEADS, HD = 16, D // 16
    HPG = P // HD
    GROUPS = HEADS // HPG
    STEPS = HEADS // 2
    SCALE = float(HD) ** -0.5
    E, _, HID = w1.shape
    KT = (NK + P - 1) // P
    KLAST = NK - (KT - 1) * P
    CHUNK_TILES = [3, 3, 3, 4]
    CHUNKS = len(CHUNK_TILES)
    TILE0 = [sum(CHUNK_TILES[:c]) for c in range(CHUNKS)]
    KEY0 = [P * t for t in TILE0]
    KEYS = [min(NK, KEY0[c] + P * CHUNK_TILES[c]) - KEY0[c] for c in range(CHUNKS)]
    KEYS_EVEN = [n + n % 2 for n in KEYS]
    NKE = NK + NK % 2
    NK_PAD = -(-NK // 16) * 16
    KEYS_PAD = -(-max(KEYS_EVEN) // 16) * 16
    HALF = P // 2
    assert sum(CHUNK_TILES) == KT and max(KEYS_EVEN) <= BANK and T == BANK and D == BANK
    FULL = CHUNKS - 1
    assert len(set(KEYS[:FULL])) == 1

    UNITS = [2 + n for n in CHUNK_TILES]
    UNIT0 = [sum(UNITS[:c]) for c in range(CHUNKS)]
    HALF_UNITS = sum(UNITS)
    BATCH_UNITS = 2 * HALF_UNITS
    PROJ_BANKS = 3
    assert HALF_UNITS % PROJ_BANKS == 0
    HG = HID // (4 * P)
    HT = HID // P
    TOP_K = 2
    BLOCK = 2 * P
    BT = BLOCK // P
    assert T <= 2 * BLOCK
    MAX_BLOCKS = (TOP_K * T + (E - 1) * (BLOCK - 1)) // BLOCK + 1
    TABLE = MAX_BLOCKS + 1

    q_dram = nc.dram_tensor("q_scratch", (D, T), F32, kind="Internal").ap()

    x_rows = x.rearrange("b q d -> (b q) d").rearrange("(t p) d -> p t d", p=P)
    out_rows = out.rearrange("b q d -> (b q) d").rearrange("(t p) d -> p t d", p=P)
    ctx_view = ctx_t.rearrange("b (c p) n -> b p c n", p=P)

    with ExitStack() as stack:
        def sb(name, shape, dt, where=stack):
            return where.enter_context(nc.sbuf_tensor(name, shape, dt))

        def sem(name):
            return stack.enter_context(nc.semaphore(name))

        ps = stack.enter_context(nc.psum_tensor("ps", [P, 8, BANK], F32))
        SCORE_BANK, PROJ_BANK, PV_BANK = 0, 4, 7

        ident = sb("ident", [P, P], F32)
        ones = sb("ones", [P, P], F32)
        bq_sb = sb("bq_sb", [P, KD], F32)
        bk_sb = sb("bk_sb", [P, KD], F32)
        bv_sb = sb("bv_sb", [P, KD], F32)
        stat = sb("stat", [P, TT, 6], F32)
        mv = sb("mv", [P, TT, 2], F32)
        ve = sb("ve", [P, TT], F32)
        sd = sb("sd", [P, TT], F32)
        rs0 = sb("rs0", [P, TT], F32)
        sq = sb("sq", [P, TT], F32)
        sdn = sb("sdn", [P, TT], F32)
        rstd = sb("rstd", [P, TT], F32)
        no_query = sb("no_query", [P, 1], F32)
        warmed = sb("warmed", [P, 4], F32)
        mx = sb("mx", [P, CHUNKS], F32)
        negmax = sb("negmax", [P, 1], F32)
        rowsum = sb("rowsum", [P, 2], F32)
        total = sb("total", [P, 1], F32)
        rinv = sb("rinv", [P, 1], F32)
        rinv_diag = sb("rinv_diag", [P, P], F32)
        rinv_rows = sb("rinv_rows", [P, P], F32)
        pv_high, pv_low, pv_sum = (sb(n, [HALF, P], F32) for n in ("pv_high", "pv_low", "pv_sum"))
        ot_raw = sb("ot_raw", [P, KD, T], F32)

        LOW = 4 * (2 * KT * D + STEPS * NKE + 2 * KT * P + NK_PAD + 2 * STEPS * P + STEPS * NQ)
        used = [0]

        def place(name, shape, dt, where):
            n = 4
            for m in shape[1:]:
                n *= m
            used[0] += n
            return sb(name, shape, dt, where)

        def pad_to(n, name, where):
            assert used[0] <= n, (name, used[0], n)
            if used[0] < n:
                place(name, [P, (n - used[0]) // 4], F32, where)

        attn = ExitStack()
        v_mix = place("v_mix", [P, KT, STEPS, 2, HALF], F32R, attn)
        k_mix = place("k_mix", [P, STEPS, NKE], F32R, attn)
        pt_mix = place("pt_mix", [P, KT, 2, P], F32R, attn)
        probs = place("probs", [P, NK_PAD], F32, attn)
        qbd_hi = place("qbd_hi", [P, STEPS, P], F32R, attn)
        qbd_lo = place("qbd_lo", [P, STEPS, P], F32R, attn)
        q_both = place("q_both", [P, STEPS, NQ], F32, attn)
        pad_to(LOW, "attn_pad", attn)
        ctx_raw = [place(f"ctx_raw{i}", [P, KC, KEYS_PAD], F32, attn) for i in range(2)]
        ctx_hi = [place(f"ctx_hi{i}", [P, KC, KEYS_PAD], F32R, attn) for i in range(2)]
        ctx_lo = [place(f"ctx_lo{i}", [P, KC, KEYS_PAD], F32R, attn) for i in range(2)]
        wk_hi = place("wk_hi", [P, KC, D], F32R, attn)
        wk_lo = place("wk_lo", [P, KC, D], F32R, attn)
        wv_hi = place("wv_hi", [P, KC, D], F32R, attn)
        wv_lo = place("wv_lo", [P, KC, D], F32R, attn)
        attn.close()

        first, used[0] = ExitStack(), 0
        wq_raw = place("wq_raw", [P, KD, D], F32, first)
        wq_hi = place("wq_hi", [P, KD, D], F32R, first)
        wq_lo = place("wq_lo", [P, KD, D], F32R, first)
        wkv_raw = place("wkv_raw", [P, 2, KC, D], F32, first)
        x0 = place("x0", [P, TT, D], F32, first)
        xn0 = place("xn0", [P, TT, D], F32, first)
        xt0_hi = place("xt0_hi", [P, KD, T], F32R, first)
        xt0_lo = place("xt0_lo", [P, KD, T], F32R, first)
        pad_to(4 * (2 * KT * D + STEPS * NKE), "first_pad", first)
        q_out = place("q_out", [P, KD, T], F32, first)
        first.close()

        moe, used[0] = ExitStack(), 0
        w_raw = [None, place("w_raw1", [P, 2, 4, BANK], F32, moe)]
        w_hi = [place("w_hi0", [P, 2, 4, BANK], F32R, moe)]
        w_lo = [place("w_lo0", [P, 2, 4, BANK], F32R, moe)]
        h_f32 = place("h_f32", [P, 2 * BLOCK], F32, moe)
        h_hi = place("h_hi", [P, 2 * BLOCK], F32R, moe)
        h_lo = place("h_lo", [P, 2 * BLOCK], F32R, moe)
        stage2, at = ExitStack(), used[0]
        assert used[0] >= 4 * 2 * KT * D and used[0] + 4 * 2 * KD * T <= 4 * (2 * KT * D + STEPS // 2 * NKE)
        ot_hi = place("ot_hi", [P, KD, T], F32R, stage2)
        ot_lo = place("ot_lo", [P, KD, T], F32R, stage2)
        stage2.close()
        used[0] = at
        w_hi.append(place("w_hi1", [P, 2, 4, BANK], F32R, moe))
        w_lo.append(place("w_lo1", [P, 2, 4, BANK], F32R, moe))
        xn = place("xn", [P, TT, D], F32, moe)
        xt_hi = place("xt_hi", [P, KD, T], F32R, moe)
        xt_lo = place("xt_lo", [P, KD, T], F32R, moe)
        sel = place("sel", [P, TT, BLOCK], F32R, moe)
        sel_t = place("sel_t", [P, BT, T], F32R, moe)
        xg_hi = place("xg_hi", [P, KD, BLOCK], F32R, moe)
        xg_lo = place("xg_lo", [P, KD, BLOCK], F32R, moe)
        h_pre = place("h_pre", [P, BANK], F32, moe)
        pad_to(LOW, "moe_pad", moe)
        acc = place("acc", [P, TT, D], F32, moe)
        w_raw[0] = place("w_raw0", [P, 2, 4, BANK], F32, moe)
        bo_bc = place("bo_bc", [P, D], F32, moe)
        stage2, at = ExitStack(), used[0]
        wo_raw = place("wo_raw", [P, KD, D], F32, stage2)
        wo_hi = place("wo_hi", [P, KD, D], F32R, stage2)
        wo_lo = place("wo_lo", [P, KD, D], F32R, stage2)
        stage2.close()
        used[0] = at
        xn_hi = place("xn_hi", [P, TT, D], F32R, moe)
        xn_lo = place("xn_lo", [P, TT, D], F32R, moe)
        y_hi = place("y_hi", [P, BT, D], F32R, moe)
        y_lo = place("y_lo", [P, BT, D], F32R, moe)
        rw_raw = place("rw_raw", [P, KD, E], F32, moe)
        rw_hi = place("rw_hi", [P, KD, E], F32R, moe)
        rw_lo = place("rw_lo", [P, KD, E], F32R, moe)
        b1_sb = place("b1_sb", [P, E, HT], F32, moe)
        rb_bc = place("rb_bc", [P, E], F32, moe)
        assert used[0] <= LOW + 4 * (6 * KC * KEYS_PAD + 4 * KC * D)
        b2_sb = place("b2_sb", [E, D], F32, moe)
        before = place("before", [P, P], F32, moe)
        slot_no = place("slot_no", [P, BLOCK], F32, moe)
        b1_cur = sb("b1_cur", [P, 1, HT], F32, moe)
        gate_cur = sb("gate_cur", [P, 1, TT], F32, moe)
        key_cur = sb("key_cur", [P, 1, TT], F32, moe)
        logits_t = sb("logits_t", [E, T], F32, moe)
        logits = sb("logits", [P, TT, E], F32, moe)
        top = sb("top", [P, TT, 8], F32, moe)
        top_at = sb("top_at", [P, TT, 8], U32, moe)
        top_atf = sb("top_atf", [P, TT, 8], F32, moe)
        expert_no = sb("expert_no", [P, E], F32, moe)
        negtop = sb("negtop", [P, TT], F32, moe)
        is_first = sb("is_first", [P, TT, E], F32, moe)
        keep = sb("keep", [P, TT, E], F32, moe)
        eg = sb("eg", [P, TT, E], F32, moe)
        egk = sb("egk", [P, TT, E], F32, moe)
        gsum = sb("gsum", [P, TT], F32, moe)
        ginv = sb("ginv", [P, TT], F32, moe)
        gates = sb("gates", [P, TT, E], F32, moe)
        gates_e = sb("gates_e", [P, E, TT], F32, moe)
        gates_t = sb("gates_t", [E, T], F32, moe)
        block_no = sb("block_no", [P, TABLE], F32, moe)
        seen = sb("seen", [P, TT + 1, E], F32, moe)
        in_tile = sb("in_tile", [P, TT, E], F32, moe)
        rank1 = sb("rank1", [P, TT, E], F32, moe)
        rankk = sb("rankk", [P, TT, E], F32, moe)
        rank_e = sb("rank_e", [P, E, TT], F32, moe)
        some = sb("some", [P, E], F32, moe)
        PAD = E // 2
        sums = [sb(f"sums{i}", [P, PAD + E], F32, moe) for i in range(4)]
        past = sb("past", [P, TABLE, E], F32, moe)
        past_n = sb("past_n", [P, TABLE, E], F32, moe)
        owner = sb("owner", [P, TABLE], F32, moe)
        start = sb("start", [P, TABLE], F32, moe)
        start2 = sb("start2", [P, TABLE], F32, moe)
        base = sb("base", [P, TABLE], F32, moe)
        table_f = sb("table_f", [P, TABLE + 1], F32, moe)
        table = sb("table", [P, TABLE + 1], I32, moe)
        owned = sb("owned", [P, TABLE, E], F32, moe)
        owned_n = sb("owned_n", [P, TABLE, E], F32, moe)
        left = sb("left", [P, TABLE], F32, moe)
        left2 = sb("left2", [P, TABLE], F32, moe)
        wide = sb("wide", [P, TABLE], I32, moe)
        moe.close()

        x_loaded, wq_loaded, bias_loaded, wkv_loaded = sem("x_loaded"), sem("wq_loaded"), sem("bias_loaded"), sem("wkv_loaded")
        ctx_loaded = [sem(f"ctx_loaded{i}") for i in range(2)]
        q_loaded, wo_loaded = sem("q_loaded"), sem("wo_loaded")
        x1_loaded, bo_loaded, small_loaded = sem("x1_loaded"), sem("bo_loaded"), sem("small_loaded")
        w1_loaded = [sem(f"w1_loaded{i}") for i in range(2)]
        w2_loaded = [sem(f"w2_loaded{i}") for i in range(2)]
        out_stored = sem("out_stored")
        q_stored = sem("q_stored")
        zeroed, ident_ready, psum_zeroed = sem("zeroed"), sem("ident_ready"), sem("psum_zeroed")
        wq_high, wq_split, wkv_high, wkv_split = sem("wq_high"), sem("wq_split"), sem("wkv_high"), sem("wkv_split")
        q_ready, q_done = sem("q_ready"), sem("q_done")
        var_ready, sd_ready, xn_ready = sem("var_ready"), sem("sd_ready"), sem("xn_ready")
        xt_ready, xt_high, xt_split = sem("xt_ready"), sem("xt_high"), sem("xt_split")
        vector_step = sem("vector_step")
        qbd_high, qbd_ready = sem("qbd_high"), sem("qbd_ready")
        ctx_high, ctx_split = sem("ctx_high"), sem("ctx_split")
        proj_ready, proj_high, proj_split = sem("proj_ready"), sem("proj_high"), sem("proj_split")
        scores_ready, part_max, negmax_ready = sem("scores_ready"), sem("part_max"), sem("negmax_ready")
        exp_done, total_ready, rinv_ready, diag_ready = sem("exp_done"), sem("total_ready"), sem("rinv_ready"), sem("diag_ready")
        pv_added, pv_pieces, rows_taken = sem("pv_added"), sem("pv_pieces"), sem("rows_taken")
        pt_ready, pt_high, pt_split = sem("pt_ready"), sem("pt_high"), sem("pt_split")
        pv_ready, pv_taken = sem("pv_ready"), sem("pv_taken")
        wo_high, wo_split, ot_high, ot_split = sem("wo_high"), sem("wo_split"), sem("ot_high"), sem("ot_split")
        x1_product = sem("x1_product")
        rw_high, rw_split, numbers_ready = sem("rw_high"), sem("rw_split"), sem("numbers_ready")
        logits_product, negtop_ready, eg_ready = sem("logits_product"), sem("negtop_ready"), sem("eg_ready")
        logits_t_ready, logits_turned, counts_taken = sem("logits_t_ready"), sem("logits_turned"), sem("counts_taken")
        gates_ready, gates_turned, gates_t_ready = sem("gates_ready"), sem("gates_turned"), sem("gates_t_ready")
        b2_product = sem("b2_product")
        counts_product, table_ready, xn_high, xn_split = sem("counts_product"), sem("table_ready"), sem("xn_high"), sem("xn_split")
        wide_ready = sem("wide_ready")
        w1_high, w1_split, w2_high, w2_split = sem("w1_high"), sem("w1_split"), sem("w2_high"), sem("w2_split")
        w_used, b1_set, gate_set, key_set, sel_ready = sem("w_used"), sem("b1_set"), sem("gate_set"), sem("key_set"), sem("sel_ready")
        sel_turned, sel_t_taken = sem("sel_turned"), [sem(f"sel_t_taken{i}") for i in range(BT)]
        gather_ready, xg_high, xg_low = sem("gather_ready"), sem("xg_high"), sem("xg_low")
        h_ready, h_high, h_split = sem("h_ready"), sem("h_high"), sem("h_split")
        y_ready, y_high, y_split, scatter_ready = sem("y_ready"), sem("y_high"), sem("y_split"), sem("scatter_ready")
        y_taken = sem("y_taken")

        def job_no(b, s):
            return CHUNKS + STEPS * b + s

        KEY_UNITS = [0, 1]

        def unit_no(b, s, k):
            return HALF_UNITS + BATCH_UNITS * b + HALF_UNITS * (s // CHUNKS) + UNIT0[s % CHUNKS] + k

        def key_units_done(b, g):
            return BATCH_UNITS * b + HALF_UNITS * (g // 2) + UNIT0[CHUNKS - 1] + KEY_UNITS[g % 2] + 1

        def value_units_done(b, s):
            return BATCH_UNITS * b + HALF_UNITS * (s // CHUNKS + 1)

        AHEAD = 8
        NEXT_FREE = 5
        LAST_UNITS = BATCH_UNITS * B
        TILES_BEFORE = 3
        assert TILES_BEFORE * P <= (B - 1) * NQ and TT == TILES_BEFORE + 1
        EARLY = 3

        def units_of(s):
            half, c = (1 - s // CHUNKS) if s >= 0 else 0, s % CHUNKS
            units = [("values", TILE0[c] + i, half) for i in range(CHUNK_TILES[c])]
            for i in range(2):
                units.insert(KEY_UNITS[i], ("keys", 2 * half + i, c))
            return units

        def first_queries(quad, copy):
            to = (quad + 2 * copy) % HPG
            return (slice(HD * quad, HD * (quad + 1)), slice(HD * to, HD * (to + 1)), slice(quad // 2, STEPS, 2),
                    slice(NQ * (quad % 2), NQ * (quad % 2 + 1)))

        def x1_bank(t):
            return PROJ_BANK + t if t < TILES_BEFORE else t - TILES_BEFORE

        def h_cols(c):
            return slice(c % 2 * BLOCK, (c % 2 + 1) * BLOCK)

        def rows_of(t):
            return P if t < KT - 1 else KLAST

        def three_pass(pe, acc_ap, a_hi, a_lo, b_hi, b_lo, start, stop):
            pe.matmul(acc_ap, a_hi, b_hi, start=start, stop=False)
            pe.matmul(acc_ap, a_hi, b_lo, start=False, stop=False)
            return pe.matmul(acc_ap, a_lo, b_hi, start=False, stop=stop)

        block = stack.enter_context(nc.Block())

        @block.sync
        def _(sp):
            def load_ctx(b, c, slot):
                n = KEYS[c]
                sp.dma_start(ctx_raw[slot][:, :, 0:n],
                             ctx_view[b, :, :, KEY0[c]:KEY0[c] + n] if isinstance(b, int) else
                             ctx_view[bass.ds(b, 1), :, :, KEY0[c]:KEY0[c] + n].rearrange("o p c n -> (o p) c n")
                             ).then_inc(ctx_loaded[slot], 16)

            def load_queries(b):
                for half in range(2):
                    sp.dma_start(q_both[half * HALF:(half + 1) * HALF],
                                 q_dram.rearrange("(s p) t -> p s t", p=HALF)[:, :, bass.ds(b * NQ, NQ)]
                                 ).then_inc(q_loaded, 16)

            sp.dma_start(x0[:], x_rows).then_inc(x_loaded, 16)
            sp.dma_start(wq_raw[:], wq.rearrange("(k p) n -> p k n", p=P)).then_inc(wq_loaded, 16)
            sp.dma_start(bq_sb[:], bq_t).then_inc(bias_loaded, 16)
            sp.dma_start(bk_sb[:], bk_t).then_inc(bias_loaded, 16)
            sp.dma_start(bv_sb[:], bv_t).then_inc(bias_loaded, 16)
            sp.dma_start(wkv_raw[:, 0], wk.rearrange("(k p) n -> p k n", p=P)).then_inc(wkv_loaded, 16)
            sp.dma_start(wkv_raw[:, 1], wv.rearrange("(k p) n -> p k n", p=P)).then_inc(wkv_loaded, 16)
            load_ctx(0, 0, 0)
            load_ctx(0, 1, 1)
            for m in range(2, CHUNKS):
                sp.wait_ge(ctx_split, m - 1)
                load_ctx(0, m, m % 2)
            sp.wait_ge(q_done, KD - 1)
            sp.wait_ge(pv_taken, 1)
            sp.dma_start(q_dram.rearrange("(g p) t -> p g t", p=P), q_out[:]).then_inc(q_stored, 16)
            for c in range(2):
                sp.wait_ge(ctx_split, CHUNKS - 1 + c)
                load_ctx(0, c, c % 2)
            sp.wait_ge(q_stored, 16)

            def batch(b, last):
                for s in range(STEPS):
                    if s == 0 and not last:
                        sp.wait_ge(qbd_ready, GROUPS * (b + 1))
                        load_queries(b + 1)
                    if not (last and s + 2 >= CHUNKS):
                        sp.wait_ge(ctx_split, job_no(b, s) + 1)
                        nb = b if s + 2 < CHUNKS or s + 2 >= STEPS else b + 1
                        if s + 2 >= STEPS:
                            nb = b + 1
                        load_ctx(nb, (s + 2) % CHUNKS, s % 2)

            with sp.Fori(0, B - 1) as b:
                batch(b, False)
            batch(B - 1, True)

            sp.wait_ge(proj_split, LAST_UNITS)
            sp.dma_start(wo_raw[:], wo.rearrange("(k p) n -> p k n", p=P)).then_inc(wo_loaded, 16)
            sp.dma_start(acc[:], x_rows).then_inc(x1_loaded, 16)
            sp.dma_start(bo_bc[:], bo.rearrange("(o n) -> o n", o=1).broadcast_to([P, D])).then_inc(bo_loaded, 16)
            sp.dma_start(rw_raw[:], router_w.rearrange("(k p) e -> p k e", p=P)).then_inc(small_loaded, 16)
            sp.dma_start(rb_bc[:], router_b.rearrange("(o n) -> o n", o=1).broadcast_to([P, E])).then_inc(small_loaded, 16)
            sp.dma_start(b2_sb[:], b2).then_inc(small_loaded, 16)
            sp.dma_start(b1_sb[:], b1_t).then_inc(small_loaded, 16)

            w1_view = w1.rearrange("e (k p) h -> e p k h", p=P)
            w2_view = w2.rearrange("e (g j p) d -> e g p j d", p=P, j=4)

            def load_w1(e, g, slot):
                cols = slice(g * BANK, (g + 1) * BANK)
                src = w1_view[e, :, :, cols] if isinstance(e, int) else \
                    w1_view[bass.ds(e, 1), :, :, cols].rearrange("o p k h -> (o p) k h")
                sp.dma_start(w_raw[slot][:, 0], src).then_inc(w1_loaded[slot], 16)

            def load_w2(e, g, slot):
                src = w2_view[e, g] if isinstance(e, int) else \
                    w2_view[bass.ds(e, 1), g].rearrange("o p j d -> (o p) j d")
                sp.dma_start(w_raw[slot][:, 1], src).then_inc(w2_loaded[slot], 16)

            load_w1(0, 0, 0)
            load_w2(0, 0, 0)
            sp.wait_ge(pv_taken, STEPS * B + 1)
            load_w1(0, 1, 1)
            load_w2(0, 1, 1)
            sp.wait_ge(table_ready, 1)
            blocks = sp.value_load(table[0:1, TABLE:TABLE + 1], min_val=1, max_val=MAX_BLOCKS)
            with sp.Fori(0, blocks) as b:
                expert = sp.value_load(table[0:1, bass.ds(b, 1)], min_val=0, max_val=E - 1)
                expert_next = sp.value_load(table[0:1, bass.ds(b + 1, 1)], min_val=0, max_val=E - 1)
                for g in range(HG):
                    owner_next = expert if g + 2 < HG else expert_next
                    sp.wait_ge(w1_split, 4 * (HG * b + g + 1))
                    load_w1(owner_next, (g + 2) % HG, g % 2)
                    sp.wait_ge(w2_split, 4 * (HG * b + g + 1))
                    load_w2(owner_next, (g + 2) % HG, g % 2)

            for i in range(2):
                sp.wait_ge(w1_loaded[i], 16 * (HG // 2 * blocks + 1))
                sp.wait_ge(w2_loaded[i], 16 * (HG // 2 * blocks + 1))
            sp.wait_ge(y_taken, TT * (blocks + 1))
            sp.dma_start(out_rows, acc[:]).then_inc(out_stored, 16)
            sp.wait_ge(out_stored, 16)

        @block.gpsimd
        def _(pool):
            nc.gpsimd.memset(ident[:], 0.0).then_inc(zeroed, 1)
            nc.gpsimd.memset(qbd_hi[:].bitcast(F32), 0.0).then_inc(zeroed, 1)
            nc.gpsimd.memset(qbd_lo[:].bitcast(F32), 0.0).then_inc(zeroed, 1)
            nc.gpsimd.memset(no_query[:], 0.0).then_inc(zeroed, 1)
            nc.gpsimd.memset(ones[:], 1.0).then_inc(zeroed, 1)
            nc.gpsimd.memset(ctx_raw[(CHUNKS - 1) % 2][:, :, KEYS[-1]:KEYS_EVEN[-1]], 0.0).then_inc(zeroed, 1)
            pool.wait_ge(zeroed, 6)
            nc.gpsimd.affine_select(out=ident[:], in_=ident[:], compare_op=ALU.not_equal, fill=1.0, base=0,
                                    pattern=[[-1, P]], channel_multiplier=1).then_inc(ident_ready, 1)

            def split_ctx(job_plus_1, c, loaded, free=None):
                slot, n = c % 2, KEYS_EVEN[c]
                pool.wait_ge(ctx_loaded[slot], loaded)
                if free is not None:
                    pool.wait_ge(proj_ready, free)
                nc.gpsimd.tensor_tensor(ctx_hi[slot][:, :, 0:n], ctx_raw[slot][:, :, 0:n],
                                        no_query[:].rearrange("p (o i) -> p o i", o=1).broadcast_to([P, KC, n]),
                                        ALU.add).then_inc(ctx_high, 1)
                pool.wait_ge(ctx_high, job_plus_1)
                nc.gpsimd.tensor_tensor(ctx_lo[slot][:, :, 0:n], ctx_raw[slot][:, :, 0:n],
                                        ctx_hi[slot][:, :, 0:n].bitcast(F32), ALU.subtract).then_inc(ctx_split, 1)

            def place_queries(b, g):
                for half in range(2):
                    for quad in range(HPG):
                        rows, cols = slice(HD * quad, HD * (quad + 1)), slice(NQ * (quad % 2), NQ * (quad % 2 + 1))
                        pairs = slice(2 * g, 2 * g + 2)
                        if half == 0:
                            last = nc.gpsimd.tensor_tensor(qbd_hi[rows, pairs, cols], q_both[rows, pairs, :],
                                                           no_query[rows, :].rearrange("p (o i) -> p o i", o=1
                                                                                       ).broadcast_to([HD, 2, NQ]),
                                                           ALU.add)
                        else:
                            last = nc.gpsimd.tensor_tensor(qbd_lo[rows, pairs, cols], q_both[rows, pairs, :],
                                                           qbd_hi[rows, pairs, cols].bitcast(F32), ALU.subtract)
                    if half == 0:
                        last.then_inc(qbd_high, 1)
                        pool.wait_ge(qbd_high, GROUPS * b + g + 1)
                    else:
                        last.then_inc(qbd_ready, 1)
                        pool.wait_ge(qbd_ready, GROUPS * b + g + 1)

            for m in range(CHUNKS):
                split_ctx(m + 1, m, 16 * (m // 2 + 1), UNIT0[m - 1] if m >= 2 else None)
            split_ctx(CHUNKS + 1, 0, 16 * (CHUNKS // 2 + 1), UNIT0[CHUNKS - 1])

            def batch(b, last):
                for s in range(STEPS):
                    if not (last and s + 1 >= CHUNKS):
                        split_ctx(job_no(b, s + 1) + 1, (s + 1) % CHUNKS,
                                  16 * (CHUNKS // 2 + 1 + (STEPS // 2) * b + (s + 1) // 2), unit_no(b, s, 0))
                    if s % 2 == 1 and not last:
                        pool.wait_ge(scores_ready, CHUNKS * (STEPS * b + s + 1))
                        pool.wait_ge(ctx_split, job_no(b, s + 1) + 1)
                        if s == 1:
                            pool.wait_ge(q_loaded, 32 * (b + 1))
                        place_queries(b + 1, s // 2)

            with pool.Fori(0, B - 1) as b:
                batch(b, False)
            batch(B - 1, True)

            pool.wait_ge(small_loaded, 64)
            pool.wait_ge(pv_taken, STEPS * B + 1)
            nc.gpsimd.iota(expert_no[:], pattern=[[1, E]], base=0, channel_multiplier=0,
                           allow_small_or_imprecise_dtypes=True).then_inc(numbers_ready, 1)
            nc.gpsimd.tensor_copy(rw_hi[:], rw_raw[:]).then_inc(rw_high, 1)
            pool.wait_ge(rw_high, 1)
            nc.gpsimd.tensor_tensor(rw_lo[:], rw_raw[:], rw_hi[:].bitcast(F32), ALU.subtract).then_inc(rw_split, 1)
            nc.gpsimd.iota(slot_no[:], pattern=[[1, BLOCK]], base=0, channel_multiplier=0,
                           allow_small_or_imprecise_dtypes=True).then_inc(numbers_ready, 1)
            nc.gpsimd.iota(block_no[:], pattern=[[1, TABLE]], base=0, channel_multiplier=0,
                           allow_small_or_imprecise_dtypes=True).then_inc(numbers_ready, 1)
            nc.gpsimd.affine_select(out=before[:], in_=ones[:], compare_op=ALU.is_gt, fill=0.0, base=0,
                                    pattern=[[1, P]], channel_multiplier=-1).then_inc(numbers_ready, 1)

            def split_w1(part_no, j):
                slot, i = j // 4 % 2, j % 4
                pool.wait_ge(w1_high, part_no + 1)
                nc.gpsimd.tensor_tensor(w_lo[slot][:, 0, i, :], w_raw[slot][:, 0, i, :],
                                        w_hi[slot][:, 0, i, :].bitcast(F32), ALU.subtract).then_inc(w1_split, 1)

            for j in range(4):
                split_w1(j, j)
            pool.wait_ge(xn_high, 1)
            nc.gpsimd.tensor_tensor(xn_lo[:], xn[:], xn_hi[:].bitcast(F32), ALU.subtract).then_inc(xn_split, 1)
            for j in range(4, AHEAD):
                split_w1(j, j)
            pool.wait_ge(table_ready, 1)
            blocks = pool.value_load(table[0:1, TABLE:TABLE + 1], min_val=1, max_val=MAX_BLOCKS)
            with pool.Fori(0, blocks) as b:
                for c in range(HT):
                    split_w1(HT * b + c + AHEAD, c + AHEAD)

        @block.scalar
        def _(act):
            def warm(fn, i):
                nc.scalar.activation(warmed[:, i:i + 1], ones[:, 0:1], fn)

            act.wait_ge(zeroed, 6)
            warm(ACT.Sqrt, 0)
            act.wait_ge(wq_loaded, 16)
            nc.scalar.copy(wq_hi[:], wq_raw[:]).then_inc(wq_high, 1)
            act.wait_ge(var_ready, 1)
            nc.scalar.activation(sd[:], ve[:], ACT.Sqrt).then_inc(sd_ready, 1)
            warm(ACT.Exp, 1)
            for k in range(KD):
                act.wait_ge(xt_ready, k + 1)
                nc.scalar.copy(xt0_hi[:, k, :], ps[:, k, :]).then_inc(xt_high, 1)

            def proj_high_part(unit, n, bank):
                kind, a, c = unit
                act.wait_ge(proj_ready, n + 1)
                if kind == "keys":
                    m = KEYS_EVEN[c]
                    for i in range(2):
                        rows = slice(i * HALF, (i + 1) * HALF)
                        last = nc.scalar.activation(k_mix[rows, 2 * a + i, KEY0[c]:KEY0[c] + m], ps[rows, bank, 0:m],
                                                    ACT.Identity, bias=bk_sb[rows, a:a + 1])
                    last.then_inc(proj_high, 1)
                else:
                    r, w, pairs = rows_of(a), D // 2, slice(c * STEPS // 2, (c + 1) * STEPS // 2)
                    nc.scalar.copy(v_mix[0:r, a, pairs, 0, :], ps[0:r, bank, 0:w].rearrange("p (s c) -> p s c", c=HALF)
                                   ).then_inc(proj_high, 1)

            def job_high(b, s, ks):
                for k in ks:
                    n = UNIT0[s % CHUNKS] + k
                    bank = PROJ_BANK + (n % PROJ_BANKS)
                    proj_high_part(units_of(s if b is not None else CHUNKS + s)[k],
                                   unit_no(b, s, k) if b is not None else n, bank)

            act.wait_ge(wkv_loaded, 32)
            nc.scalar.copy(wk_hi[:], wkv_raw[:, 0]).then_inc(wkv_high, 1)
            nc.scalar.copy(wv_hi[:], wkv_raw[:, 1]).then_inc(wkv_high, 1)
            act.wait_ge(bias_loaded, 48)
            for c in range(CHUNKS):
                job_high(None, c, range(UNITS[c]))
                if c == 0:
                    act.wait_ge(q_done, KD - 1)
                    act.wait_ge(pv_taken, 1)
                    act.wait_ge(zeroed, 6)
                    for copy in range(2):
                        for quad in range(HPG):
                            src, to, pairs, cols = first_queries(quad, copy)
                            last = nc.scalar.copy(qbd_hi[to, pairs, cols], q_out[src, :, 0:NQ])
                    last.then_inc(qbd_high, GROUPS)

            def take_rows(b, s):
                act.wait_ge(pv_pieces, STEPS * b + s + 1)
                nc.scalar.copy(rinv_rows[:], ps[:, PV_BANK, 2 * P:3 * P]).then_inc(rows_taken, 1)

            def context_high(cols):
                for g in range(GROUPS):
                    nc.scalar.activation(ot_hi[:, g, cols], ot_raw[:, g, cols], ACT.Identity,
                                         bias=bv_sb[:, g:g + 1]).then_inc(ot_high, 1)

            def step(b, s, before, last=False):
                act.wait_ge(negmax_ready, STEPS * b + s + 1)
                w = KEY0[FULL]
                nc.scalar.activation(probs[:, 0:w].rearrange("p (c k) -> p c k", c=FULL),
                                     ps[:, SCORE_BANK:SCORE_BANK + FULL, 0:KEYS[0]], ACT.Exp,
                                     bias=negmax[:, 0:1], accum_out=rowsum[:, 0:1]).then_inc(exp_done, 1)
                nc.scalar.activation(probs[:, w:NK], ps[:, SCORE_BANK + FULL, 0:KEYS[FULL]], ACT.Exp,
                                     bias=negmax[:, 0:1], accum_out=rowsum[:, 1:2]).then_inc(exp_done, 1)
                has_job = not (last and s >= CHUNKS)
                if before is not None:
                    take_rows(*before)
                if has_job:
                    job_high(b, s, range(EARLY))
                for c in range(CHUNKS):
                    act.wait_ge(pt_ready, CHUNKS * (STEPS * b + s) + c + 1)
                    n = CHUNK_TILES[c]
                    nc.scalar.copy(pt_mix[:, TILE0[c]:TILE0[c] + n, 0, :],
                                   ps[:, SCORE_BANK + c, 0:n * P].rearrange("p (t r) -> p t r", t=n)
                                   ).then_inc(pt_high, 1)
                if has_job:
                    job_high(b, s, range(EARLY, UNITS[s % CHUNKS]))
                if last and s == CHUNKS:
                    act.wait_ge(pv_taken, STEPS * (B - 1) + 1)
                    context_high(slice(0, TILES_BEFORE * P))
                if last and s == CHUNKS + 1:
                    act.wait_ge(wo_loaded, 16)
                    nc.scalar.copy(wo_hi[:], wo_raw[:]).then_inc(wo_high, 1)

            act.wait_ge(q_stored, 16)
            step(0, 0, None)
            with act.Fori(0, B - 1) as b:
                for s in range(1, STEPS):
                    step(b, s, (b, s - 1))
                step(b + 1, 0, (b, STEPS - 1))
            for s in range(1, STEPS):
                step(B - 1, s, (B - 1, s - 1), last=True)
            take_rows(B - 1, STEPS - 1)

            act.wait_ge(pv_taken, STEPS * B + 1)
            context_high(slice(TILES_BEFORE * P, T))

            def split_w1_high(j, b=None):
                slot, i = j // 4 % 2, j % 4
                if i == 0:
                    n = j // 8 + 1
                    act.wait_ge(w1_loaded[slot], 16 * (HG // 2 * b + n if b is not None else n))
                nc.scalar.copy(w_hi[slot][:, 0, i, :], w_raw[slot][:, 0, i, :]).then_inc(w1_high, 1)

            for j in range(4):
                split_w1_high(j)
            warm(ACT.Sqrt, 2)
            act.wait_ge(var_ready, 2)
            nc.scalar.activation(sd[:], ve[:], ACT.Sqrt).then_inc(sd_ready, 1)
            warm(ACT.Exp, 3)
            for k in range(KD):
                act.wait_ge(xt_ready, KD + k + 1)
                nc.scalar.copy(xt_hi[:, k, :], ps[:, 4 + k, :]).then_inc(xt_high, 1)
            nc.scalar.copy(xn_hi[:], xn[:]).then_inc(xn_high, 1)
            act.wait_ge(negtop_ready, 1)
            for t in range(TT):
                last = nc.scalar.activation(eg[:, t, :], logits[:, t, :], ACT.Exp, bias=negtop[:, t:t + 1])
            last.then_inc(eg_ready, 1)

            for j in range(4, AHEAD):
                split_w1_high(j)
            act.wait_ge(table_ready, 1)
            blocks = act.value_load(table[0:1, TABLE:TABLE + 1], min_val=1, max_val=MAX_BLOCKS)

            def gathered_high(b):
                for k in range(KD):
                    act.wait_ge(gather_ready, KD * b + k + 1)
                    nc.scalar.copy(xg_hi[:, k, :], ps[:, 4 + k, 0:BLOCK]).then_inc(xg_high, 1)

            def take_sel_t(b):
                act.wait_ge(sel_turned, BT * b + 1)
                nc.scalar.copy(sel_t[:, 0, :], ps[:, 6, :]).then_inc(sel_t_taken[0], 1)

            gathered_high(0)
            act.wait_ge(wide_ready, 1)
            with act.Fori(0, blocks) as b:
                act.wait_ge(b1_set, b + 1)
                is_wide = act.value_load(wide[0:1, bass.ds(b, 1)], min_val=0, max_val=1)
                with act.If(is_wide > 0):
                    for c in range(HT):
                        act.wait_ge(h_ready, HT * b + c + 1)
                        for h in (h_f32, h_hi):
                            last = nc.scalar.activation(h[:, h_cols(c)], ps[:, 2 + c % 2, 0:BLOCK], ACT.Relu,
                                                        bias=b1_cur[:, 0, c:c + 1])
                        last.then_inc(h_high, 1)
                        if c + NEXT_FREE >= AHEAD:
                            split_w1_high(c + NEXT_FREE, b)
                        if c == 0:
                            take_sel_t(b)
                with act.Else():
                    for g in range(HG):
                        done = HT * b + 4 * g
                        act.wait_ge(h_ready, done + 2)
                        nc.scalar.copy(h_pre[:], ps[:, 2, :]).then_inc(h_high, 2)
                        for i in range(3):
                            if 4 * g + i + NEXT_FREE >= AHEAD:
                                split_w1_high(4 * g + i + NEXT_FREE, b)
                        if g == 0:
                            take_sel_t(b)
                        act.wait_ge(h_ready, done + 4)
                        for h in (h_f32, h_hi):
                            for i in range(4):
                                cols = slice(i * P, (i + 1) * P)
                                last = nc.scalar.activation(h[:, cols], ps[:, 3, cols], ACT.Relu,
                                                            bias=b1_cur[:, 0, 4 * g + i:4 * g + i + 1])
                        last.then_inc(h_high, 2)
                        split_w1_high(4 * g + 3 + NEXT_FREE, b)
                for j in range(HT + NEXT_FREE, HT + AHEAD):
                    split_w1_high(j, b)
                for t in range(BT):
                    act.wait_ge(y_ready, BT * b + t + 1)
                    nc.scalar.copy(y_hi[:, t, :], ps[:, t, :]).then_inc(y_high, 1)
                gathered_high(b + 1)

        @block.vector
        def _(dve):
            steps = [0]

            def step(ins):
                steps[0] += 1
                ins.then_inc(vector_step, 1)
                dve.wait_ge(vector_step, steps[0])

            def layernorm(src, dst, n):
                for t in range(TT):
                    last = nc.vector.bn_aggr(mv[:, t, :], stat[:, t, :])
                step(last)
                nc.vector.tensor_scalar(ve[:], mv[:, :, 1], LN_EPS, None, ALU.add).then_inc(var_ready, 1)
                dve.wait_ge(sd_ready, n)
                step(nc.vector.reciprocal(rs0[:], sd[:]))
                step(nc.vector.tensor_tensor(sq[:], ve[:], rs0[:], ALU.mult))
                step(nc.vector.tensor_tensor(sdn[:], sd[:], sq[:], ALU.add))
                step(nc.vector.tensor_scalar(sq[:], sdn[:], 0.5, None, ALU.mult))
                step(nc.vector.reciprocal(rstd[:], sq[:]))
                for t in range(TT):
                    nc.vector.tensor_scalar(dst[:, t, :], src[:, t, :], mv[:, t, 0:1], rstd[:, t:t + 1],
                                            ALU.subtract, ALU.mult).then_inc(xn_ready, 1)

            nc.vector.memset(ps[:, SCORE_BANK + CHUNKS - 1, :], 0.0).then_inc(psum_zeroed, 1)
            dve.wait_ge(x_loaded, 16)
            for t in range(TT):
                last = nc.vector.bn_stats(stat[:, t, :], x0[:, t, :])
            step(last)
            layernorm(x0, xn0, 1)
            dve.wait_ge(wq_high, 1)
            nc.vector.tensor_tensor(wq_lo[:], wq_raw[:], wq_hi[:].bitcast(F32), ALU.subtract).then_inc(wq_split, 1)
            for k in range(KD):
                dve.wait_ge(xt_high, k + 1)
                nc.vector.tensor_tensor(xt0_lo[:, k, :], ps[:, k, :], xt0_hi[:, k, :].bitcast(F32),
                                        ALU.subtract).then_inc(xt_split, 1)
            for i, (hi, lo) in enumerate([(wk_hi, wk_lo), (wv_hi, wv_lo)]):
                dve.wait_ge(wkv_high, i + 1)
                nc.vector.tensor_tensor(lo[:], wkv_raw[:, i], hi[:].bitcast(F32), ALU.subtract).then_inc(wkv_split, 1)
            dve.wait_ge(bias_loaded, 48)
            for m in range(KD):
                dve.wait_ge(q_ready, m + 1)
                nc.vector.tensor_scalar(q_out[:, m, :], ps[:, 4 + m, :], bq_sb[:, m:m + 1], SCALE,
                                        ALU.add, ALU.mult).then_inc(q_done if m < KD - 1 else pv_taken, 1)

            def proj_low_part(unit, n, bank):
                kind, a, c = unit
                dve.wait_ge(proj_high, n + 1)
                if kind == "keys":
                    m = KEYS_EVEN[c]
                    cols = slice(KEY0[c], KEY0[c] + m)
                    for i in range(2):
                        rows, other = slice(i * HALF, (i + 1) * HALF), slice((1 - i) * HALF, (2 - i) * HALF)
                        last = nc.vector.scalar_tensor_tensor(out=k_mix[other, 2 * a + i, cols], in0=ps[rows, bank, 0:m],
                                                              scalar=bk_sb[rows, a:a + 1],
                                                              in1=k_mix[rows, 2 * a + i, cols].bitcast(F32),
                                                              op0=ALU.add, op1=ALU.subtract)
                    last.then_inc(proj_split, 1)
                else:
                    r, w, pairs = rows_of(a), D // 2, slice(c * STEPS // 2, (c + 1) * STEPS // 2)
                    nc.vector.tensor_tensor(v_mix[0:r, a, pairs, 1, :],
                                            ps[0:r, bank, 0:w].rearrange("p (s c) -> p s c", c=HALF),
                                            v_mix[0:r, a, pairs, 0, :].bitcast(F32), ALU.subtract).then_inc(proj_split, 1)

            def job_low(b, s, ks):
                for k in ks:
                    n = UNIT0[s % CHUNKS] + k
                    bank = PROJ_BANK + (n % PROJ_BANKS)
                    proj_low_part(units_of(s if b is not None else CHUNKS + s)[k],
                                  unit_no(b, s, k) if b is not None else n, bank)

            def take_context(b, s):
                n = STEPS * b + s
                dve.wait_ge(pv_ready, n + 1)
                for out_ap, rows in ((pv_high, slice(0, HALF)), (pv_low, slice(HALF, P))):
                    last = nc.vector.tensor_reduce(out_ap[:], ps[rows, PV_BANK, 0:2 * P].rearrange("p (i r) -> p r i", i=2),
                                                   AX.X, ALU.add)
                last.then_inc(pv_pieces, 1)
                dve.wait_ge(pv_pieces, n + 1)
                nc.vector.tensor_tensor(pv_sum[:], pv_high[:], pv_low[:], ALU.add).then_inc(pv_added, 1)
                dve.wait_ge(rows_taken, n + 1)
                dve.wait_ge(pv_added, n + 1)
                for h in range(2):
                    rows, cols = slice(HD * h, HD * (h + 1)), slice(NQ * h, NQ * (h + 1))
                    to = HALF * (s % 2) + HD * h
                    tokens = slice(b * NQ, (b + 1) * NQ) if isinstance(b, int) else bass.ds(b * NQ, NQ)
                    last = nc.vector.tensor_tensor(ot_raw[to:to + HD, s // 2, tokens], pv_sum[rows, cols],
                                                   rinv_rows[rows, cols], ALU.mult)
                last.then_inc(pv_taken, 1)

            for c in range(CHUNKS):
                job_low(None, c, range(UNITS[c]))
                if c == 0:
                    dve.wait_ge(qbd_high, GROUPS)
                    for copy in range(2):
                        for quad in range(HPG):
                            src, to, pairs, cols = first_queries(quad, copy)
                            last = nc.vector.tensor_tensor(qbd_lo[to, pairs, cols], q_out[src, :, 0:NQ],
                                                           qbd_hi[src, pairs, cols].bitcast(F32), ALU.subtract)
                    last.then_inc(qbd_ready, GROUPS)

            def context_low(cols, done):
                for g in range(GROUPS):
                    dve.wait_ge(ot_high, done + g + 1)
                    nc.vector.scalar_tensor_tensor(out=ot_lo[:, g, cols], in0=ot_raw[:, g, cols], scalar=bv_sb[:, g:g + 1],
                                                   in1=ot_hi[:, g, cols].bitcast(F32), op0=ALU.add,
                                                   op1=ALU.subtract).then_inc(ot_split, 1)

            def add_product(t, n):
                bank = x1_bank(t)
                dve.wait_ge(x1_product, n)
                step(nc.vector.tensor_tensor(acc[:, t, :], ps[:, bank, :], acc[:, t, :], ALU.add))
                step(nc.vector.bn_stats(stat[:, t, :], acc[:, t, :]))

            def softmax(b, s, before, last=False):
                n = STEPS * b + s
                for c in range(CHUNKS):
                    dve.wait_ge(scores_ready, CHUNKS * n + c + 1)
                    part = nc.vector.tensor_reduce(mx[:, c:c + 1], ps[:, SCORE_BANK + c, 0:KEYS[c]], AX.X, ALU.max)
                part.then_inc(part_max, 1)
                dve.wait_ge(part_max, n + 1)
                nc.vector.tensor_reduce(negmax[:], mx[:], AX.X, ALU.max, negate=True).then_inc(negmax_ready, 1)
                if before is not None:
                    take_context(*before)
                has_job = not (last and s >= CHUNKS)
                if has_job:
                    job_low(b, s, range(EARLY))
                dve.wait_ge(exp_done, 2 * n + 2)
                nc.vector.tensor_reduce(total[:], rowsum[:], AX.X, ALU.add).then_inc(total_ready, 1)
                for c in range(CHUNKS):
                    dve.wait_ge(pt_high, CHUNKS * n + c + 1)
                    m = CHUNK_TILES[c]
                    nc.vector.tensor_tensor(pt_mix[:, TILE0[c]:TILE0[c] + m, 1, :],
                                            ps[:, SCORE_BANK + c, 0:m * P].rearrange("p (t r) -> p t r", t=m),
                                            pt_mix[:, TILE0[c]:TILE0[c] + m, 0, :].bitcast(F32),
                                            ALU.subtract).then_inc(pt_split, 1)
                    if c == 0:
                        dve.wait_ge(total_ready, n + 1)
                        nc.vector.reciprocal(rinv[:], total[:]).then_inc(rinv_ready, 1)
                    if c == 1:
                        dve.wait_ge(rinv_ready, n + 1)
                        nc.vector.tensor_scalar(rinv_diag[:], ident[:], rinv[:, 0:1], None,
                                                ALU.mult).then_inc(diag_ready, 1)
                if has_job:
                    job_low(b, s, range(EARLY, UNITS[s % CHUNKS]))
                if last and s == CHUNKS:
                    context_low(slice(0, TILES_BEFORE * P), 0)
                if last and s == CHUNKS + 1:
                    dve.wait_ge(wo_high, 1)
                    nc.vector.tensor_tensor(wo_lo[:], wo_raw[:], wo_hi[:].bitcast(F32), ALU.subtract
                                            ).then_inc(wo_split, 1)
                if last and s == CHUNKS + 2:
                    dve.wait_ge(x1_loaded, 16)
                    dve.wait_ge(bo_loaded, 16)
                    for t in range(TT):
                        step(nc.vector.tensor_tensor(acc[:, t, :], acc[:, t, :], bo_bc[:], ALU.add))
                if last and s == CHUNKS + 3:
                    for t in range(TILES_BEFORE - 1):
                        add_product(t, t + 1)

            softmax(0, 0, None)
            with dve.Fori(0, B - 1) as b:
                for s in range(1, STEPS):
                    softmax(b, s, (b, s - 1))
                softmax(b + 1, 0, (b, STEPS - 1))
            for s in range(1, STEPS):
                softmax(B - 1, s, (B - 1, s - 1), last=True)
            take_context(B - 1, STEPS - 1)

            context_low(slice(TILES_BEFORE * P, T), GROUPS)
            for t in range(TILES_BEFORE - 1, TT):
                add_product(t, t + 1)
            layernorm(acc, xn, 2)
            dve.wait_ge(w2_loaded[0], 16)
            for i in range(4):
                nc.vector.tensor_copy(w_hi[0][:, 1, i, :], w_raw[0][:, 1, i, :]).then_inc(w2_high, 1)
            for k in range(KD):
                dve.wait_ge(xt_high, KD + k + 1)
                nc.vector.tensor_tensor(xt_lo[:, k, :], ps[:, 4 + k, :], xt_hi[:, k, :].bitcast(F32),
                                        ALU.subtract).then_inc(xt_split, 1)
            for i in range(4):
                dve.wait_ge(w2_high, i + 1)
                nc.vector.tensor_tensor(w_lo[0][:, 1, i, :], w_raw[0][:, 1, i, :], w_hi[0][:, 1, i, :].bitcast(F32),
                                        ALU.subtract).then_inc(w2_split, 1)
            dve.wait_ge(small_loaded, 64)
            dve.wait_ge(numbers_ready, 1)
            dve.wait_ge(logits_product, 1)
            nc.vector.tensor_copy(logits_t[:], ps[0:E, 0, :]).then_inc(logits_t_ready, 1)
            dve.wait_ge(logits_turned, 1)
            for t in range(TT):
                last = nc.vector.tensor_tensor(logits[:, t, :], ps[:, 1, t * E:(t + 1) * E], rb_bc[:], ALU.add)
            step(last)
            for t in range(TT):
                last = nc.vector.max(top[:, t, :], logits[:, t, :])
            step(last)
            nc.vector.tensor_scalar(negtop[:], top[:, :, 0], -1.0, None, ALU.mult).then_inc(negtop_ready, 1)
            for t in range(TT):
                last = nc.vector.max_index(top_at[:, t, :], top[:, t, :], logits[:, t, :])
            step(last)
            step(nc.vector.tensor_copy(top_atf[:], top_at[:]))
            for t in range(TT):
                last = nc.vector.tensor_scalar(is_first[:, t, :], expert_no[:], top_atf[:, t, 0:1], None, ALU.is_equal)
            step(last)
            for t in range(TT):
                last = nc.vector.scalar_tensor_tensor(out=keep[:, t, :], in0=expert_no[:], scalar=top_atf[:, t, 1:2],
                                                      in1=is_first[:, t, :], op0=ALU.is_equal, op1=ALU.add)
            step(last)
            dve.wait_ge(eg_ready, 1)
            step(nc.vector.tensor_tensor(egk[:], eg[:], keep[:], ALU.mult))
            step(nc.vector.tensor_reduce(gsum[:], egk[:], AX.X, ALU.add))
            step(nc.vector.reciprocal(ginv[:], gsum[:]))
            for t in range(TT):
                last = nc.vector.tensor_scalar(gates[:, t, :], egk[:, t, :], ginv[:, t:t + 1], None, ALU.mult)
            last.then_inc(gates_ready, 1)
            dve.wait_ge(gates_ready, 1)
            step(nc.vector.tensor_copy(gates_e[:], gates[:].rearrange("p t e -> p e t")))

            dve.wait_ge(counts_product, 2)
            nc.vector.memset(seen[:, 0, :], 0.0)
            nc.vector.tensor_copy(in_tile[:], ps[:, 2, TT * E:2 * TT * E].rearrange("p (t e) -> p t e", t=TT))
            for i in range(3):
                nc.vector.memset(sums[i][:, 0:PAD], 0.0)
            step(nc.vector.tensor_scalar(rank1[:], ps[:, 2, 0:TT * E].rearrange("p (t e) -> p t e", t=TT), 1.0, None,
                                         ALU.add))
            for t in range(TT):
                step(nc.vector.tensor_tensor(seen[:, t + 1, :], seen[:, t, :], in_tile[:, t, :], ALU.add))
            step(nc.vector.tensor_tensor(rankk[:], rank1[:], seen[:, 0:TT, :], ALU.add))
            step(nc.vector.tensor_tensor(rank1[:], rankk[:], keep[:], ALU.mult))
            step(nc.vector.tensor_scalar(rank_e[:], rank1[:].rearrange("p t e -> p e t"), 1.0, None, ALU.subtract))

            def select(b, ranks, first_rank):
                nc.vector.tensor_scalar(key_cur[:], ranks, first_rank, None, ALU.subtract).then_inc(key_set, 1)
                dve.wait_ge(key_set, b + 1)
                for t in range(TT):
                    last = nc.vector.tensor_scalar(sel[:, t, :], slot_no[:], key_cur[:, 0, t:t + 1], None, ALU.is_equal)
                last.then_inc(sel_ready, 1)

            def gathered_low(b):
                for k in range(KD):
                    dve.wait_ge(xg_high, KD * b + k + 1)
                    nc.vector.tensor_copy(xg_lo[:, k, :], ps[:, 4 + k, BLOCK:2 * BLOCK]).then_inc(xg_low, 1)

            select(0, rank_e[:, 0:1, :], 0.0)
            dve.wait_ge(gates_turned, 1)
            nc.vector.tensor_copy(gates_t[:], ps[0:E, 3, :]).then_inc(gates_t_ready, 1)

            count = seen[:, TT, :]
            step(nc.vector.tensor_scalar(some[:], count, 0.0, None, ALU.is_gt))
            step(nc.vector.memset(some[:, 0:1], 1.0))
            step(nc.vector.scalar_tensor_tensor(out=sums[0][:, PAD:], in0=count, scalar=float(BLOCK), in1=some[:],
                                                op0=ALU.is_gt, op1=ALU.add))
            for i in range(3):
                d = 1 << i
                step(nc.vector.tensor_tensor(sums[i + 1][:, PAD:], sums[i][:, PAD:], sums[i][:, PAD - d:PAD - d + E],
                                             ALU.add))
            blocks_to = sums[3][:, PAD:].rearrange("p (o e) -> p o e", o=1).broadcast_to([P, TABLE, E])
            blocks_of = sums[0][:, PAD:].rearrange("p (o e) -> p o e", o=1).broadcast_to([P, TABLE, E])
            numbers = block_no[:].rearrange("p (b o) -> p b o", o=1).broadcast_to([P, TABLE, E])
            step(nc.vector.tensor_tensor(past[:], blocks_to, numbers, ALU.is_le))
            nc.vector.tensor_tensor(past_n[:], past[:], blocks_of, ALU.mult)
            step(nc.vector.tensor_reduce(owner[:], past[:], AX.X, ALU.add))
            nc.vector.tensor_scalar(table_f[:, 0:TABLE], owner[:], float(E - 1), None, ALU.min)
            step(nc.vector.tensor_copy(table_f[:, TABLE:TABLE + 1], sums[3][:, PAD + E - 1:PAD + E]))
            nc.vector.tensor_copy(table[:], table_f[:]).then_inc(table_ready, 1)
            step(nc.vector.tensor_reduce(start[:], past_n[:], AX.X, ALU.add))
            step(nc.vector.tensor_tensor(start2[:], block_no[:], start[:], ALU.subtract))
            step(nc.vector.tensor_scalar(base[:], start2[:], float(BLOCK), None, ALU.mult))
            step(nc.vector.tensor_tensor(owned[:], owner[:].rearrange("p (b o) -> p b o", o=1).broadcast_to([P, TABLE, E]),
                                         expert_no[:].rearrange("p (o e) -> p o e", o=1).broadcast_to([P, TABLE, E]),
                                         ALU.is_equal))
            step(nc.vector.tensor_tensor(owned_n[:], owned[:],
                                         count.rearrange("p (o e) -> p o e", o=1).broadcast_to([P, TABLE, E]), ALU.mult))
            step(nc.vector.tensor_reduce(left[:], owned_n[:], AX.X, ALU.add))
            step(nc.vector.tensor_tensor(left2[:], left[:], base[:], ALU.subtract))
            nc.vector.tensor_scalar(wide[:], left2[:], float(P), None, ALU.is_gt).then_inc(wide_ready, 1)
            gathered_low(0)
            for t in range(TT):
                dve.wait_ge(b2_product, t + 1)
                nc.vector.tensor_tensor(acc[:, t, :], ps[:, t, :], acc[:, t, :], ALU.add).then_inc(y_taken, 1)
            dve.wait_ge(table_ready, 1)
            blocks = dve.value_load(table[0:1, TABLE:TABLE + 1], min_val=1, max_val=MAX_BLOCKS)

            def split_w2(b, c):
                g, i = c // 4, c % 4
                slot = (g + 1) % 2
                if i == 0:
                    dve.wait_ge(w2_loaded[slot], 16 * (HG // 2 * b + (g + 1) // 2 + 1))
                    if g > 0:
                        dve.wait_ge(w_used, (HG - 1) * b + g)
                nc.vector.tensor_copy(w_hi[slot][:, 1, i, :], w_raw[slot][:, 1, i, :]).then_inc(w2_high, 1)
                if c == 1:
                    dve.wait_ge(sel_turned, BT * b + 2)
                    nc.vector.tensor_copy(sel_t[:, 1, :], ps[:, 7, :]).then_inc(sel_t_taken[1], 1)
                if c == HT // 2:
                    expert_next = dve.value_load(table[0:1, bass.ds(b + 1, 1)], min_val=0, max_val=E - 1)
                    select(b + 1, rank_e[:, bass.ds(expert_next, 1), :], base[:, bass.ds(b + 1, 1)])
                dve.wait_ge(w2_high, 4 * (HG * b + g + 1) + i + 1)
                nc.vector.tensor_tensor(w_lo[slot][:, 1, i, :], w_raw[slot][:, 1, i, :],
                                        w_hi[slot][:, 1, i, :].bitcast(F32), ALU.subtract).then_inc(w2_split, 1)

            with dve.Fori(0, blocks) as b:
                expert = dve.value_load(table[0:1, bass.ds(b, 1)], min_val=0, max_val=E - 1)
                nc.vector.tensor_copy(b1_cur[:], b1_sb[:, bass.ds(expert, 1), :]).then_inc(b1_set, 1)
                dve.wait_ge(y_taken, TT * (b + 1))
                nc.vector.tensor_copy(gate_cur[:], gates_e[:, bass.ds(expert, 1), :]).then_inc(gate_set, 1)
                is_wide = dve.value_load(wide[0:1, bass.ds(b, 1)], min_val=0, max_val=1)
                with dve.If(is_wide > 0):
                    for c in range(HT):
                        cols = h_cols(c)
                        dve.wait_ge(h_high, HT * b + c + 1)
                        nc.vector.tensor_tensor(h_lo[:, cols], h_f32[:, cols], h_hi[:, cols].bitcast(F32),
                                                ALU.subtract).then_inc(h_split, 1)
                        split_w2(b, c)
                with dve.Else():
                    for g in range(HG):
                        for i in range(2):
                            split_w2(b, 4 * g + i)
                        dve.wait_ge(h_high, HT * b + 4 * g + 4)
                        nc.vector.tensor_tensor(h_lo[:], h_f32[:], h_hi[:].bitcast(F32), ALU.subtract).then_inc(h_split, 4)
                        for i in range(2, 4):
                            split_w2(b, 4 * g + i)
                for t in range(BT):
                    dve.wait_ge(y_high, BT * b + t + 1)
                    nc.vector.tensor_tensor(y_lo[:, t, :], ps[:, t, :], y_hi[:, t, :].bitcast(F32),
                                            ALU.subtract).then_inc(y_split, 1)
                gathered_low(b + 1)
                dve.wait_ge(gate_set, b + 1)
                for t in range(TT):
                    dve.wait_ge(scatter_ready, TT * b + t + 1)
                    bank = t if t < 2 else 2 + t
                    nc.vector.scalar_tensor_tensor(out=acc[:, t, :], in0=ps[:, bank, :], scalar=gate_cur[:, 0, t:t + 1],
                                                   in1=acc[:, t, :], op0=ALU.mult, op1=ALU.add).then_inc(y_taken, 1)

        @block.tensor
        def _(pe):
            def turn(src, bank0, n):
                pe.wait_ge(xn_ready, n)
                for k in range(KD):
                    for t in range(TT):
                        last = pe.transpose(ps[:, bank0 + k, t * P:(t + 1) * P], src[:, t, k * P:(k + 1) * P], ident[:])
                    last.then_inc(xt_ready, 1)

            pe.wait_ge(ident_ready, 1)
            pe.wait_ge(psum_zeroed, 1)
            turn(xn0, 0, TT)
            pe.wait_ge(wq_split, 1)
            pe.wait_ge(xt_split, KD)
            for m in range(KD):
                for k in range(KD):
                    last = three_pass(pe, ps[:, 4 + m, :], wq_hi[:, k, m * P:(m + 1) * P], wq_lo[:, k, m * P:(m + 1) * P],
                                      xt0_hi[:, k, :], xt0_lo[:, k, :], k == 0, k == KD - 1)
                last.then_inc(q_ready, 1)

            def project(unit, n, bank):
                kind, a, c = unit
                for k in range(KC):
                    if kind == "keys":
                        slot, m, cols = c % 2, KEYS_EVEN[c], slice(a * P, (a + 1) * P)
                        last = three_pass(pe, ps[:, bank, 0:m], wk_hi[:, k, cols], wk_lo[:, k, cols],
                                          ctx_hi[slot][:, k, 0:m], ctx_lo[slot][:, k, 0:m], k == 0, k == KC - 1)
                    else:
                        chunk = max(i for i in range(CHUNKS) if TILE0[i] <= a)
                        slot, r, w = chunk % 2, rows_of(a), D // 2
                        keys = slice((a - TILE0[chunk]) * P, (a - TILE0[chunk]) * P + r)
                        cols = slice(c * w, (c + 1) * w)
                        last = three_pass(pe, ps[0:r, bank, 0:w], ctx_hi[slot][:, k, keys], ctx_lo[slot][:, k, keys],
                                          wv_hi[:, k, cols], wv_lo[:, k, cols], k == 0, k == KC - 1)
                last.then_inc(proj_ready, 1)

            def run_job(b, s, ks):
                for k in ks:
                    local = UNIT0[s % CHUNKS] + k
                    n = unit_no(b, s, k) if b is not None else local
                    if k == 0:
                        pe.wait_ge(ctx_split, job_no(b, s) + 1 if b is not None else s + 1)
                    if b is not None or local >= PROJ_BANKS:
                        pe.wait_ge(proj_split, n - PROJ_BANKS + 1)
                    project(units_of(s if b is not None else CHUNKS + s)[k], n, PROJ_BANK + local % PROJ_BANKS)

            pe.wait_ge(wkv_split, 2)
            pe.wait_ge(q_done, KD - 1)
            for c in range(CHUNKS):
                run_job(None, c, range(UNITS[c]))

            def context(b, s):
                n = STEPS * b + s
                pe.wait_ge(proj_split, value_units_done(b, s))
                pe.wait_ge(pt_split, CHUNKS * (n + 1))
                pe.wait_ge(pv_taken, n + 1)
                pe.wait_ge(diag_ready, n + 1)
                for t in range(KT):
                    r = rows_of(t)
                    pe.matmul(ps[:, PV_BANK, 0:2 * P], v_mix[0:r, t, s, :, :], pt_mix[0:r, t, :, :], start=(t == 0),
                              stop=(t == KT - 1))
                pe.matmul(ps[:, PV_BANK, 2 * P:3 * P], ones[:], rinv_diag[:], start=True, stop=True).then_inc(pv_ready, 1)

            def output_projection(t):
                pe.wait_ge(wo_split, 1)
                pe.wait_ge(ot_split, GROUPS if t < TILES_BEFORE else 2 * GROUPS)
                for k in range(KD):
                    rows = slice(t * P, (t + 1) * P)
                    last = three_pass(pe, ps[:, x1_bank(t), :], ot_hi[:, k, rows], ot_lo[:, k, rows], wo_hi[:, k, :],
                                      wo_lo[:, k, :], k == 0, k == KD - 1)
                last.then_inc(x1_product, 1)

            def step(b, s, before, last_batch=False):
                g, n = s // 2, STEPS * b + s
                if s % 2 == 0:
                    pe.wait_ge(qbd_ready, GROUPS * b + g + 1)
                    pe.wait_ge(proj_split, key_units_done(b, g))
                for c in range(CHUNKS):
                    if before is not None:
                        pe.wait_ge(pt_split, CHUNKS * (n - 1) + c + 1)
                    m = KEYS_EVEN[c]
                    cols = slice(KEY0[c], KEY0[c] + m)
                    pe.matmul(ps[:, SCORE_BANK + c, 0:m], qbd_hi[:, s, :], k_mix[:, s, cols], start=True, stop=False)
                    pe.matmul(ps[:, SCORE_BANK + c, 0:m], qbd_lo[:, s, :], k_mix[:, s, cols], start=False,
                              stop=True).then_inc(scores_ready, 1)
                if before is not None:
                    context(*before)
                has_job = not (last_batch and s >= CHUNKS)
                if has_job:
                    run_job(b, s, range(EARLY))
                if last_batch and s >= STEPS - 2:
                    output_projection(s - (STEPS - 2))
                for c in range(CHUNKS):
                    if c == 0 or c == FULL:
                        pe.wait_ge(exp_done, 2 * n + (1 if c == 0 else 2))
                    for i in range(CHUNK_TILES[c]):
                        r = rows_of(TILE0[c] + i)
                        key = KEY0[c] + i * P
                        last = pe.transpose(ps[0:r, SCORE_BANK + c, i * P:(i + 1) * P], probs[:, key:key + r], ident[:])
                    last.then_inc(pt_ready, 1)
                if has_job:
                    run_job(b, s, range(EARLY, UNITS[s % CHUNKS]))
                if last_batch and s == STEPS - 1:
                    output_projection(2)

            step(0, 0, None)
            with pe.Fori(0, B - 1) as b:
                for s in range(1, STEPS):
                    step(b, s, (b, s - 1))
                step(b + 1, 0, (b, STEPS - 1))
            for s in range(1, STEPS):
                step(B - 1, s, (B - 1, s - 1), last_batch=True)
            context(B - 1, STEPS - 1)

            for t in range(TILES_BEFORE, TT):
                output_projection(t)
            turn(xn, 4, 2 * TT)
            pe.wait_ge(xt_split, 2 * KD)
            pe.wait_ge(rw_split, 1)
            for k in range(KD):
                last = three_pass(pe, ps[0:E, 0, :], rw_hi[:, k, :], rw_lo[:, k, :], xt_hi[:, k, :], xt_lo[:, k, :],
                                  k == 0, k == KD - 1)
            last.then_inc(logits_product, 1)
            pe.wait_ge(logits_t_ready, 1)
            for t in range(TT):
                last = pe.transpose(ps[:, 1, t * E:(t + 1) * E], logits_t[:, t * P:(t + 1) * P], ident[0:E, 0:E])
            last.then_inc(logits_turned, 1)
            pe.wait_ge(gates_ready, 1)
            pe.wait_ge(numbers_ready, 4)
            for i, m in enumerate([before, ones]):
                pe.matmul(ps[:, 2, i * TT * E:(i + 1) * TT * E], m[:], keep[:].rearrange("p t e -> p (t e)"), start=True,
                          stop=True).then_inc(counts_product, 1)
            for t in range(TT):
                last = pe.transpose(ps[0:E, 3, t * P:(t + 1) * P], gates[:, t, :], ident[:])
            last.then_inc(gates_turned, 1)

            def gather(b, ks=range(KD)):
                pe.wait_ge(sel_ready, b + 1)
                for k in ks:
                    for i, part in enumerate([xn_hi, xn_lo]):
                        for t in range(TT):
                            last = pe.matmul(ps[:, 4 + k, i * BLOCK:(i + 1) * BLOCK], part[:, t, k * P:(k + 1) * P],
                                             sel[:, t, :], start=(t == 0), stop=(t == TT - 1))
                    last.then_inc(gather_ready, 1)

            def hidden(b, c):
                g, i = c // 4, c % 4
                if c >= 2:
                    pe.wait_ge(h_split, HT * b + c - 1)
                cols = slice(i * P, (i + 1) * P)
                for k in range(KD):
                    if i == 0:
                        pe.wait_ge(w1_split, 4 * (HG * b + g) + k + 1)
                    if c == 0:
                        pe.wait_ge(xg_low, KD * b + k + 1)
                    last = three_pass(pe, ps[:, 2 + c % 2, 0:BLOCK], w_hi[g % 2][:, 0, k, cols], w_lo[g % 2][:, 0, k, cols],
                                      xg_hi[:, k, :], xg_lo[:, k, :], k == 0, k == KD - 1)
                last.then_inc(h_ready, 1)

            def outputs(b, c, tiles):
                g, i = c // 4, c % 4
                pe.wait_ge(w2_split, 4 * (HG * b + g) + i + 1)
                pe.wait_ge(h_split, HT * b + c + 1)
                if c == 0:
                    pe.wait_ge(y_taken, TT * (b + 1))
                for t in range(tiles):
                    first = c % 2 * BLOCK + t * P if tiles == BT else i * P
                    rows = slice(first, first + P)
                    last = three_pass(pe, ps[:, t, :], h_hi[:, rows], h_lo[:, rows],
                                      w_hi[g % 2][:, 1, i, :], w_lo[g % 2][:, 1, i, :], c == 0, c == HT - 1)
                    if c == HT - 1:
                        last.then_inc(y_ready, 1 if t < tiles - 1 else BT - t)
                if i == 3 and c < HT - 1:
                    last.then_inc(w_used, 1)

            def scatter(b, tiles):
                for t in range(TT):
                    bank = t if t < 2 else 2 + t
                    if t == 0:
                        pe.wait_ge(y_split, BT * (b + 1))
                    if t == 2:
                        pe.wait_ge(xg_low, KD * (b + 1) + 2)
                    rows = slice(t * P, (t + 1) * P)
                    for u in range(tiles):
                        pe.matmul(ps[:, bank, :], sel_t[:, u, rows], y_hi[:, u, :], start=(u == 0), stop=False)
                        last = pe.matmul(ps[:, bank, :], sel_t[:, u, rows], y_lo[:, u, :], start=False,
                                         stop=(u == tiles - 1))
                    last.then_inc(scatter_ready, 1)

            pe.wait_ge(xn_split, 1)
            gather(0)
            pe.wait_ge(gates_t_ready, 1)
            for t in range(TT):
                pe.matmul(ps[:, t, :], gates_t[:, t * P:(t + 1) * P], b2_sb[:], start=True,
                          stop=True).then_inc(b2_product, 1)
            pe.wait_ge(table_ready, 1)
            blocks = pe.value_load(table[0:1, TABLE:TABLE + 1], min_val=1, max_val=MAX_BLOCKS)
            pe.wait_ge(y_taken, TT)
            pe.wait_ge(wide_ready, 1)

            def turn_sel(b):
                for u in range(BT):
                    for t in range(TT):
                        last = pe.transpose(ps[:, 6 + u, t * P:(t + 1) * P], sel[:, t, u * P:(u + 1) * P].bitcast(F32),
                                            ident[:])
                    last.then_inc(sel_turned, 1)

            def gather_next(b, ks):
                for i in range(BT):
                    pe.wait_ge(sel_t_taken[i], b + 1)
                gather(b + 1, ks)

            def wide_block(b):
                hidden(b, 0)
                turn_sel(b)
                for c in range(1, HT):
                    hidden(b, c)
                    outputs(b, c - 1, BT)
                outputs(b, HT - 1, BT)
                gather_next(b, range(KD))
                scatter(b, BT)

            def hidden_group(b, g):
                if g > 0:
                    pe.wait_ge(h_high, HT * b + 4 * g - 2)
                for k in range(KD):
                    pe.wait_ge(w1_split, 4 * (HG * b + g) + k + 1)
                    if g == 0:
                        pe.wait_ge(xg_low, KD * b + k + 1)
                    last = three_pass(pe, ps[:, 2, :], xg_hi[:, k, 0:P], xg_lo[:, k, 0:P], w_hi[g % 2][:, 0, k, :],
                                      w_lo[g % 2][:, 0, k, :], k == 0, k == KD - 1)
                last.then_inc(h_ready, 2)

            def turn_hidden(b, g):
                pe.wait_ge(h_high, HT * b + 4 * g + 2)
                for i in range(4):
                    cols = slice(i * P, (i + 1) * P)
                    last = pe.transpose(ps[:, 3, cols], h_pre[:, cols], ident[:])
                last.then_inc(h_ready, 2)

            def narrow_block(b):
                hidden_group(b, 0)
                turn_sel(b)
                turn_hidden(b, 0)
                for g in range(1, HG):
                    hidden_group(b, g)
                    for i in range(4):
                        outputs(b, 4 * (g - 1) + i, 1)
                    turn_hidden(b, g)
                gather_next(b, range(KD - 1))
                for i in range(4):
                    outputs(b, 4 * (HG - 1) + i, 1)
                gather_next(b, range(KD - 1, KD))
                scatter(b, 1)

            with pe.Fori(0, blocks) as b:
                is_wide = pe.value_load(wide[0:1, bass.ds(b, 1)], min_val=0, max_val=1)
                with pe.If(is_wide > 0):
                    wide_block(b)
                with pe.Else():
                    narrow_block(b)


_INS = ["x", "ctx_t", "wq", "bq_t", "wk", "bk_t", "wv", "bv_t", "wo", "bo", "router_w", "router_b",
        "w1", "b1_t", "w2", "b2"]


def kernel(**inputs):
    import numpy as _np
    import concourse.bacc as _bacc
    from concourse import mybir as _mybir
    from concourse.bass_utils import run_bass_kernel_spmd as _run

    a = {k: _np.asarray(v) for k, v in inputs.items()}

    def columns(v):
        return v.reshape(-1, 128).T

    laid = {
        "x": a["x"],
        "ctx_t": a["ctx_768"].transpose(0, 2, 1),
        "wq": a["L0_xattn_Wq"], "bq_t": columns(a["L0_xattn_bq"]),
        "wk": a["L0_xattn_Wk"], "bk_t": columns(a["L0_xattn_bk"]),
        "wv": a["L0_xattn_Wv"], "bv_t": columns(a["L0_xattn_bv"]),
        "wo": a["L0_xattn_Wo"], "bo": a["L0_xattn_bo"],
        "router_w": a["L0_ffn_router_w"], "router_b": a["L0_ffn_router_b"],
        "w1": a["L0_ffn_w1"],
        "b1_t": a["L0_ffn_b1"].reshape(8, 16, 128).transpose(2, 0, 1),
        "w2": a["L0_ffn_w2"], "b2": a["L0_ffn_b2"],
    }
    nc = _bacc.Bacc("TRN2", target_bir_lowering=False, num_devices=1)
    arrays, args = {}, []
    for name in _INS:
        v = _np.ascontiguousarray(laid[name])
        arrays[f"in_{name}_dram"] = v
        args.append(nc.dram_tensor(f"in_{name}_dram", v.shape, _mybir.dt.from_np(v.dtype), kind="ExternalInput").ap())
    args.append(nc.dram_tensor("out_0_dram", a["x"].shape, _mybir.dt.float32, kind="ExternalOutput").ap())
    bass_perceiver_layer_kernel(nc, *args)
    r = _run(nc, [arrays], core_ids=[0])
    return r.results[0]["out_0_dram"]
```
